# Optimizing a Trainium2 kernel written in Bass

```python
import numpy as np
import jax
import jax.numpy as jnp

def _softmax(x, axis=-1):
    return jax.nn.softmax(x, axis=axis)

def _gelu(x):
    return jax.nn.gelu(x, approximate=True)

def _silu(x):
    return jax.nn.silu(x)

def _sigmoid(x):
    return jax.nn.sigmoid(x)

def _layernorm(x, axis=-1, eps=1e-05):
    m = jnp.mean(x, axis=axis, keepdims=True)
    v = jnp.var(x, axis=axis, keepdims=True)
    return (x - m) / jnp.sqrt(v + eps)

def _scatter_add(tgt, idx, src, axis=0):
    return tgt.at[idx].add(src)

def _segment_sum(src, seg, n):
    return jax.ops.segment_sum(src, seg, n)
kernel_name = 'mk_gnn_preln_d4_gnn_r8_d6c7aa'

def setup_inputs(seed: int=0):
    np.random.seed(seed)
    _w = jnp.asarray

    def _rec_inputs():
        import jax
        import jax.numpy as jnp
        _gk = jax.random.key(seed)
        x = -8.776e-05 + 1 * jax.random.normal(jax.random.fold_in(_gk, 1), (1250, 512), jnp.float32)
        _s = jax.random.randint(jax.random.fold_in(_gk, 2), (10000,), 0, 1250, jnp.int32)
        _d = jax.random.randint(jax.random.fold_in(_gk, 3), (10000,), 0, 1250, jnp.int32)
        _loop = jnp.arange(1250, dtype=jnp.int32)
        src = jnp.concatenate([_s, _d, _loop])
        dst = jnp.concatenate([_d, _s, _loop])
        _o = jnp.argsort(dst, stable=True)
        src = src[_o]
        dst = dst[_o]
        edge_type_4 = jax.random.randint(jax.random.fold_in(_gk, 13), (21250,), 0, 4, jnp.int32)
        edge_type_8 = jax.random.randint(jax.random.fold_in(_gk, 14), (21250,), 0, 8, jnp.int32)
        edge_weight = jax.random.uniform(jax.random.fold_in(_gk, 15), (21250,), jnp.float32, 0.0, 0.999998)
        return (x, src, dst, edge_type_4, edge_type_8, edge_weight)
    x, src, dst, edge_type_4, edge_type_8, edge_weight = _rec_inputs()

    def _L0_gnn_setup():
        import jax, jax.numpy as jnp
        import numpy as np
        N_NODES = 1250
        IN_F = 512
        OUT_F = 512
        N_EDGES = 20000
        GRID_SIZE = 5
        SPLINE_ORDER = 3
        ALPHA = 0.2

        def _grid():
            step = 2.0 / GRID_SIZE
            return jnp.arange(-SPLINE_ORDER, GRID_SIZE + SPLINE_ORDER + 1, dtype=jnp.float32) * step - 1.0

        def _b_splines(x, grid):
            x = x[..., None]
            bases = ((x >= grid[:-1]) & (x < grid[1:])).astype(x.dtype)
            for p in range(1, SPLINE_ORDER + 1):
                left = (x - grid[:-(p + 1)]) / (grid[p:-1] - grid[:-(p + 1)]) * bases[..., :-1]
                right = (grid[p + 1:] - x) / (grid[p + 1:] - grid[1:-p]) * bases[..., 1:]
                bases = left + right
            return bases
        key = jax.random.key(seed)
        k1, k2, k3, k4, k5, k6 = jax.random.split(key, 6)
        h = jax.random.normal(k1, (N_NODES, IN_F), dtype=jnp.float32)
        edge_index = jax.random.randint(k2, (2, N_EDGES), 0, N_NODES, dtype=jnp.int64)
        xav = float(np.sqrt(2.0 / (IN_F + OUT_F))) * 1.414
        W = jax.random.normal(k3, (IN_F, OUT_F), dtype=jnp.float32) * xav
        a = jax.random.normal(k4, (2 * OUT_F, 1), dtype=jnp.float32) * float(np.sqrt(2.0 / (2 * OUT_F + 1)))
        base_w = jax.random.normal(k5, (OUT_F, IN_F), dtype=jnp.float32) * xav
        n_coef = GRID_SIZE + SPLINE_ORDER
        spline_w = jax.random.normal(k6, (OUT_F, IN_F, n_coef), dtype=jnp.float32) * 0.1
        return {'h': h, 'W': W, 'a': a, 'base_w': base_w, 'spline_w': spline_w, 'edge_index': edge_index}
    _L0_gnn_all = _L0_gnn_setup()
    _L0_gnn_in = {k: v for k, v in _L0_gnn_all.items() if k in ('W', 'a', 'base_w', 'spline_w')}
    del _L0_gnn_all

    def _L1_gnn_setup():
        import jax, jax.numpy as jnp
        import numpy as np
        N_NODES = 1250
        N_EDGES = 20000
        D_IN = 512
        D_OUT = 512
        key = jax.random.key(seed)
        k1, k2, k3, k4, k5 = jax.random.split(key, 5)
        feature = jax.random.normal(k1, (N_NODES, D_IN), dtype=jnp.float32)
        src = jax.random.randint(k2, (N_EDGES,), 0, N_NODES, dtype=jnp.int64)
        dst = jax.random.randint(k3, (N_EDGES,), 0, N_NODES, dtype=jnp.int64)
        W = jax.random.normal(k4, (2 * D_IN, D_OUT), dtype=jnp.float32) * (1.0 / np.sqrt(2 * D_IN))
        b = jax.random.normal(k5, (D_OUT,), dtype=jnp.float32) * 0.01
        return {'feature': feature, 'src': src, 'dst': dst, 'W': W, 'b': b}
    _L1_gnn_all = _L1_gnn_setup()
    _L1_gnn_in = {k: v for k, v in _L1_gnn_all.items() if k in ('W', 'b')}
    del _L1_gnn_all

    def _L2_gnn_setup():
        import jax, jax.numpy as jnp
        import numpy as np
        N_NODES = 2500
        N_EDGES = 40000
        D = 512
        NUM_RELS = 8
        NUM_BASES = 4

        def _rel_graph_conv(h, src, dst, etypes, norm, basis, comp, bias, loop_w, apply_relu):
            n = h.shape[0]
            hb = jnp.einsum('nd,bdo->bno', h, basis)
            coef = comp[etypes]
            m = coef[:, 0, None] * hb[0][src]
            for b in range(1, basis.shape[0]):
                m = m + coef[:, b, None] * hb[b][src]
            m = m * norm[:, None]
            agg = jax.ops.segment_sum(m, dst, num_segments=n)
            out = agg + bias + h @ loop_w
            if apply_relu:
                out = jax.nn.relu(out)
            return out
        key = jax.random.key(seed)
        ks = jax.random.split(key, 16)
        inp = {'emb': jax.random.normal(ks[0], (N_NODES, D), dtype=jnp.float32), 'src': jax.random.randint(ks[1], (N_EDGES,), 0, N_NODES), 'dst': jax.random.randint(ks[2], (N_EDGES,), 0, N_NODES), 'etypes': jax.random.randint(ks[3], (N_EDGES,), 0, NUM_RELS), 'edge_norm': jax.random.uniform(ks[4], (N_EDGES,), dtype=jnp.float32)}
        s = 1.0 / np.sqrt(D)
        inp['basis0'] = jax.random.normal(ks[5], (NUM_BASES, D, D), dtype=jnp.float32) * s
        inp['comp0'] = jax.random.normal(ks[6], (NUM_RELS, NUM_BASES), dtype=jnp.float32)
        inp['bias0'] = jnp.zeros((D,), dtype=jnp.float32)
        inp['loop0'] = jax.random.normal(ks[7], (D, D), dtype=jnp.float32) * s
        inp['basis1'] = jax.random.normal(ks[8], (NUM_BASES, D, D), dtype=jnp.float32) * s
        inp['comp1'] = jax.random.normal(ks[9], (NUM_RELS, NUM_BASES), dtype=jnp.float32)
        inp['bias1'] = jnp.zeros((D,), dtype=jnp.float32)
        inp['loop1'] = jax.random.normal(ks[10], (D, D), dtype=jnp.float32) * s
        return inp
    _L2_gnn_all = _L2_gnn_setup()
    _L2_gnn_in = {k: v for k, v in _L2_gnn_all.items() if k in ('basis0', 'comp0', 'bias0', 'loop0', 'basis1', 'comp1', 'bias1', 'loop1')}
    del _L2_gnn_all

    def _L3_gnn_setup():
        import jax, jax.numpy as jnp
        import numpy as np
        N, D, H, C, R, E, SEM = (2500, 512, 8, 64, 4, 40000, 256)
        NEG_SLOPE = 0.2
        NEG_INF = -1e+30

        def _gat_conv(x, W_r, a_src, a_dst, b_r, src, dst, valid, n):
            h, c = a_src.shape
            xt = (x @ W_r).reshape(n, h, c)
            al_s = (xt * a_src).sum(-1)
            al_d = (xt * a_dst).sum(-1)
            logits = jax.nn.leaky_relu(al_s[src] + al_d[dst], NEG_SLOPE)
            logits = jnp.where(valid[:, None], logits, NEG_INF)
            m = jax.ops.segment_max(logits, dst, num_segments=n)
            e = jnp.exp(logits - m[dst]) * valid[:, None].astype(logits.dtype)
            denom = jax.ops.segment_sum(e, dst, num_segments=n)
            alpha = e / denom[dst]
            msg = xt[src] * alpha[..., None]
            out = jax.ops.segment_sum(msg, dst, num_segments=n)
            return out.reshape(n, h * c) + b_r
        key = jax.random.key(seed)
        ks = jax.random.split(key, 10)
        s = 1.0 / np.sqrt(D)
        return {'x': jax.random.normal(ks[0], (N, D), jnp.float32), 'edge_indices': jax.random.randint(ks[1], (2, E), 0, N), 'edge_types': jax.random.randint(ks[2], (E,), 0, R), 'W': jax.random.normal(ks[3], (R, D, D), jnp.float32) * s, 'att_src': jax.random.normal(ks[4], (R, H, C), jnp.float32) * s, 'att_dst': jax.random.normal(ks[5], (R, H, C), jnp.float32) * s, 'bias': jax.random.normal(ks[6], (R, D), jnp.float32) * 0.02, 'sem_W1': jax.random.normal(ks[7], (D, SEM), jnp.float32) * s, 'sem_b1': jnp.zeros((SEM,), jnp.float32), 'sem_W2': jax.random.normal(ks[8], (SEM, 1), jnp.float32) * (1.0 / np.sqrt(SEM))}
    _L3_gnn_all = _L3_gnn_setup()
    _L3_gnn_in = {k: v for k, v in _L3_gnn_all.items() if k in ('W', 'att_src', 'att_dst', 'bias', 'sem_W1', 'sem_b1', 'sem_W2')}
    del _L3_gnn_all
    return {'x': x, 'src': src, 'dst': dst, 'edge_type_4': edge_type_4, 'edge_type_8': edge_type_8, 'edge_weight': edge_weight, 'L0_gnn_W': _L0_gnn_in['W'], 'L0_gnn_a': _L0_gnn_in['a'], 'L0_gnn_base_w': _L0_gnn_in['base_w'], 'L0_gnn_spline_w': _L0_gnn_in['spline_w'], 'L1_gnn_W': _L1_gnn_in['W'], 'L1_gnn_b': _L1_gnn_in['b'], 'L2_gnn_basis0': _L2_gnn_in['basis0'], 'L2_gnn_comp0': _L2_gnn_in['comp0'], 'L2_gnn_bias0': _L2_gnn_in['bias0'], 'L2_gnn_loop0': _L2_gnn_in['loop0'], 'L2_gnn_basis1': _L2_gnn_in['basis1'], 'L2_gnn_comp1': _L2_gnn_in['comp1'], 'L2_gnn_bias1': _L2_gnn_in['bias1'], 'L2_gnn_loop1': _L2_gnn_in['loop1'], 'L3_gnn_W': _L3_gnn_in['W'], 'L3_gnn_att_src': _L3_gnn_in['att_src'], 'L3_gnn_att_dst': _L3_gnn_in['att_dst'], 'L3_gnn_bias': _L3_gnn_in['bias'], 'L3_gnn_sem_W1': _L3_gnn_in['sem_W1'], 'L3_gnn_sem_b1': _L3_gnn_in['sem_b1'], 'L3_gnn_sem_W2': _L3_gnn_in['sem_W2']}

def reference(x, src, dst, edge_type_4, edge_type_8, edge_weight, L0_gnn_W, L0_gnn_a, L0_gnn_base_w, L0_gnn_spline_w, L1_gnn_W, L1_gnn_b, L2_gnn_basis0, L2_gnn_comp0, L2_gnn_bias0, L2_gnn_loop0, L2_gnn_basis1, L2_gnn_comp1, L2_gnn_bias1, L2_gnn_loop1, L3_gnn_W, L3_gnn_att_src, L3_gnn_att_dst, L3_gnn_bias, L3_gnn_sem_W1, L3_gnn_sem_b1, L3_gnn_sem_W2):
    import jax
    import jax.numpy as jnp

    def _L0_gnn_ref(h, W, a, base_w, spline_w, edge_index):
        import jax, jax.numpy as jnp
        import numpy as np
        N_NODES = 1250
        IN_F = 512
        OUT_F = 512
        N_EDGES = 20000
        GRID_SIZE = 5
        SPLINE_ORDER = 3
        ALPHA = 0.2

        def _grid():
            step = 2.0 / GRID_SIZE
            return jnp.arange(-SPLINE_ORDER, GRID_SIZE + SPLINE_ORDER + 1, dtype=jnp.float32) * step - 1.0

        def _b_splines(x, grid):
            x = x[..., None]
            bases = ((x >= grid[:-1]) & (x < grid[1:])).astype(x.dtype)
            for p in range(1, SPLINE_ORDER + 1):
                left = (x - grid[:-(p + 1)]) / (grid[p:-1] - grid[:-(p + 1)]) * bases[..., :-1]
                right = (grid[p + 1:] - x) / (grid[p + 1:] - grid[1:-p]) * bases[..., 1:]
                bases = left + right
            return bases
        HW = h @ W
        row, col = (edge_index[0], edge_index[1])
        s = HW @ a[:OUT_F, 0]
        t = HW @ a[OUT_F:, 0]
        e = jax.nn.leaky_relu(s[row] + t[col], negative_slope=ALPHA)
        m = jax.ops.segment_max(e, row, num_segments=N_NODES)
        ex = jnp.exp(e - m[row])
        den = jax.ops.segment_sum(ex, row, num_segments=N_NODES)
        att = ex / den[row]
        agg = jax.ops.segment_sum(att[:, None] * h[col], row, num_segments=N_NODES)
        grid = _grid()
        basis = _b_splines(agg, grid)
        out = jax.nn.silu(agg) @ base_w.T + jnp.einsum('nip,oip->no', basis, spline_w)
        return out

    def _L1_gnn_ref(feature, src, dst, W, b):
        import jax, jax.numpy as jnp
        import numpy as np
        N_NODES = 1250
        N_EDGES = 20000
        D_IN = 512
        D_OUT = 512
        n = feature.shape[0]
        neigh = jax.ops.segment_sum(feature[src], dst, num_segments=n)
        degs = jax.ops.segment_sum(jnp.ones_like(dst, dtype=feature.dtype), dst, num_segments=n)
        hk_neigh = neigh / jnp.maximum(degs, 1.0)[:, None]
        hk = jnp.concatenate([feature, hk_neigh], axis=-1) @ W + b
        return jax.nn.relu(hk)

    def _L2_gnn_ref(emb, src, dst, etypes, edge_norm, basis0, comp0, bias0, loop0, basis1, comp1, bias1, loop1):
        import jax, jax.numpy as jnp
        import numpy as np
        N_NODES = 2500
        N_EDGES = 40000
        D = 512
        NUM_RELS = 8
        NUM_BASES = 4

        def _rel_graph_conv(h, src, dst, etypes, norm, basis, comp, bias, loop_w, apply_relu):
            n = h.shape[0]
            hb = jnp.einsum('nd,bdo->bno', h, basis)
            coef = comp[etypes]
            m = coef[:, 0, None] * hb[0][src]
            for b in range(1, basis.shape[0]):
                m = m + coef[:, b, None] * hb[b][src]
            m = m * norm[:, None]
            agg = jax.ops.segment_sum(m, dst, num_segments=n)
            out = agg + bias + h @ loop_w
            if apply_relu:
                out = jax.nn.relu(out)
            return out
        h = _rel_graph_conv(emb, src, dst, etypes, edge_norm, basis0, comp0, bias0, loop0, True)
        h = _rel_graph_conv(h, src, dst, etypes, edge_norm, basis1, comp1, bias1, loop1, False)
        return h

    def _L3_gnn_ref(x, edge_indices, edge_types, W, att_src, att_dst, bias, sem_W1, sem_b1, sem_W2):
        import jax, jax.numpy as jnp
        import numpy as np
        N, D, H, C, R, E, SEM = (2500, 512, 8, 64, 4, 40000, 256)
        NEG_SLOPE = 0.2
        NEG_INF = -1e+30

        def _gat_conv(x, W_r, a_src, a_dst, b_r, src, dst, valid, n):
            h, c = a_src.shape
            xt = (x @ W_r).reshape(n, h, c)
            al_s = (xt * a_src).sum(-1)
            al_d = (xt * a_dst).sum(-1)
            logits = jax.nn.leaky_relu(al_s[src] + al_d[dst], NEG_SLOPE)
            logits = jnp.where(valid[:, None], logits, NEG_INF)
            m = jax.ops.segment_max(logits, dst, num_segments=n)
            e = jnp.exp(logits - m[dst]) * valid[:, None].astype(logits.dtype)
            denom = jax.ops.segment_sum(e, dst, num_segments=n)
            alpha = e / denom[dst]
            msg = xt[src] * alpha[..., None]
            out = jax.ops.segment_sum(msg, dst, num_segments=n)
            return out.reshape(n, h * c) + b_r
        n = x.shape[0]
        r_total = W.shape[0]
        loop = jnp.arange(n, dtype=edge_indices.dtype)
        src = jnp.concatenate([edge_indices[0], loop])
        dst = jnp.concatenate([edge_indices[1], loop])
        self_valid = jnp.ones((n,), bool)
        outs = []
        for r in range(r_total):
            valid = jnp.concatenate([edge_types == r, self_valid])
            outs.append(_gat_conv(x, W[r], att_src[r], att_dst[r], bias[r], src, dst, valid, n))
        z = jnp.stack(outs, axis=0)
        w = jnp.tanh(z @ sem_W1 + sem_b1) @ sem_W2
        beta = jax.nn.softmax(w, axis=0)
        return (beta * z).sum(0)
    edge_index = jnp.stack([src, dst])
    h = jnp.maximum(_layernorm(x, axis=-1), 0.0)
    x = x + _L0_gnn_ref(h, L0_gnn_W, L0_gnn_a, L0_gnn_base_w, L0_gnn_spline_w, edge_index)
    h = jnp.maximum(_layernorm(x, axis=-1), 0.0)
    x = x + _L1_gnn_ref(h, src, dst, L1_gnn_W, L1_gnn_b)
    h = jnp.maximum(_layernorm(x, axis=-1), 0.0)
    x = x + _L2_gnn_ref(h, src, dst, edge_type_8, edge_weight, L2_gnn_basis0, L2_gnn_comp0, L2_gnn_bias0, L2_gnn_loop0, L2_gnn_basis1, L2_gnn_comp1, L2_gnn_bias1, L2_gnn_loop1)
    h = jnp.maximum(_layernorm(x, axis=-1), 0.0)
    x = x + _L3_gnn_ref(h, edge_index, edge_type_4, L3_gnn_W, L3_gnn_att_src, L3_gnn_att_dst, L3_gnn_bias, L3_gnn_sem_W1, L3_gnn_sem_b1, L3_gnn_sem_W2)
    return x

_drawn_inputs = setup_inputs


def setup_inputs(seed=0):
    import zlib

    import numpy as np

    out = dict(_drawn_inputs(seed))
    spreads = {'L2_gnn_bias0': (0.0, 0.277), 'L2_gnn_bias1': (0.0, 0.8), 'L3_gnn_sem_b1': (0.0, 2.0)}
    factors = {'L1_gnn_b': 8.0,
     'L3_gnn_W': 3.679,
     'L3_gnn_att_src': 8.0,
     'L3_gnn_att_dst': 8.0,
     'L3_gnn_bias': 8.0,
     'L3_gnn_sem_W1': 8.0,
     'L3_gnn_sem_W2': 8.0}
    for name, (base, spread) in spreads.items():
        noise = np.random.default_rng([zlib.crc32(name.encode()), seed]).standard_normal(out[name].shape)
        drawn = base * np.exp(spread * noise) if base else spread * noise
        out[name] = jnp.asarray(drawn.astype(out[name].dtype))
    for name, factor in factors.items():
        out[name] = (out[name] * factor).astype(out[name].dtype)
    return out
```

```python
from contextlib import ExitStack

import concourse.bass as bass
from concourse import mybir

F32 = mybir.dt.float32
I32 = mybir.dt.int32
U32 = mybir.dt.uint32
ALU = mybir.AluOpType
ACT = mybir.ActivationFunctionType
AX = mybir.AxisListType

P = 128
N = 1250
D = 512
KC = D // P
T = -(-N // P)
NP = T * P
LAST = N - (T - 1) * P
E = 21250
EP, EC = 125, 170
R4, R8, BASES = 4, 8, 4
H, C = 8, 64
SEM_D = 256
NBA, NBB = T * R4, T
G = 8
PSLOTS = 4
def chunks(buckets):
    return -(-((E + buckets * (P - 1)) // P) // G) * G
NCA, NCB = chunks(NBA), chunks(NBB)
AW = D + H
REC = 8
BIG = 1.0e30
EPS = 1e-5
SC = 10
assert EP * EC == E and EC % SC == 0

A_LANE, A_SRC, A_SRC8, A_SRC4, A_WEIGHT, A_DST4 = range(6)
B_LANE, B_DST, B_SRC = range(3)


def wait_at_least(eng, sem, value):
    if not (isinstance(value, int) and value <= 0):
        eng.wait_ge(sem, value)


def peeled(eng, n, body):
    body(0)
    if n > 2:
        with eng.Fori(1, n - 1) as i:
            body(i)
    body(n - 1)


class Core:
    pass


def semaphore(m, nc, name):
    m.sems.append(nc.alloc_semaphore(name))
    return m.sems[-1]


def recycle_semaphores(m, nc):
    nc.clear_and_free_semaphores(m.sems)
    m.sems = []
    nc.all_engine_barrier()


class Chain:

    def __init__(self, eng, sem):
        self.eng, self.sem, self.base, self.k = eng, sem, 0, 0

    def link(self, ins):
        self.k += 1
        ins.then_inc(self.sem, 1)
        self.eng.wait_ge(self.sem, self.base + self.k)

    def rounds(self, n, per, body, loop=peeled):
        start = self.base + self.k

        def one(i):
            self.base, self.k = start + i * per, 0
            body(i)
            assert self.k == per, (self.k, per)

        loop(self.eng, n, one)
        self.base, self.k = start + n * per, 0


def alone(eng, m):
    eng.sem_inc(m.gate, 1)


def prepare(m, nc):
    ks = ExitStack()
    with ks:
        sb = lambda n, s, d=F32: ks.enter_context(nc.sbuf_tensor(n, s, d))
        sem = lambda n: semaphore(m, nc, n)
        ints = sb("edge_ints", [EP, 4, EC], I32)
        tmp_i = sb("edge_tmp", [EP, 2, EC], I32)
        w_in = sb("edge_weight", [EP, EC])
        key = sb("edge_key", [EP, 2, EC])
        pos = sb("edge_pos", [EP, 2, EC])
        posu = sb("edge_posu", [EP, 2, EC], U32)
        rec = m.rows[0:EP, 0:6, :].rearrange("p g d -> p (g d)")[:, 0:2 * EC * REC]\
            .rearrange("p (o c f) -> p o c f", o=2, f=REC)
        iota_b = sb("iota_b", [P, NBA])
        iota_c = sb("iota_c", [1, NCA])
        tri = sb("tri", [P, P])
        row_end = sb("row_end", [EP, NBA])
        row_tot = sb("row_tot", [EP, NBA])
        nchunk = sb("nchunk", [P, NBA])
        nchunk_i = sb("nchunk_i", [P, NBA], I32)
        end_chunk = sb("end_chunk", [P, NBA])
        off = sb("off", [EP, NBA])
        cnt = sb("cnt", [1, NCA])
        cnt_i = sb("cnt_i", [1, NCA], I32)
        blank = m.own[:, 0:NCA * REC].rearrange("p (c f) -> p c f", f=REC)
        pos_blk = sb("pos_blk", [EP, 2, SC], U32)
        rec_blk = sb("rec_blk", [EP, 2, SC, REC])
        x_in, loaded, made, counted, placed = sem("x_in"), sem("loaded"), sem("made"), sem("counted"), sem("placed")
        totals, blanked, blank_set = sem("totals"), sem("blanked"), sem("blank_set")
        copied, scattered, sorted_in = sem("copied"), sem("scattered"), sem("sorted_in")
        dve = sem("dve_prepare")
        ind = m.region[0:EP, 0:NBA * EC]
        cum = m.region[0:EP, NBA * EC:2 * NBA * EC]
        mapw = m.region[0:1, 0:NCA * NBA]

        with nc.Block() as block:

            @block.sync
            def _(sp):
                for f, a in enumerate((m.src, m.dst, m.type4, m.type8)):
                    sp.dma_start(ints[:, f, :], a.rearrange("(p c) -> p c", p=EP)).then_inc(loaded, 16)
                sp.dma_start(w_in[:, :], m.weight.rearrange("(p c) -> p c", p=EP)).then_inc(loaded, 16)
                full = m.x_in[0:(T - 1) * P, :].rearrange("(t p) d -> p t d", p=P)
                sp.wait_ge(made, 1)
                sp.dma_start(m.x[:, 0:(T - 1) * D].rearrange("p (t d) -> p t d", d=D), full).then_inc(x_in, 16)
                sp.dma_start(m.x[0:LAST, (T - 1) * D:T * D], m.x_in[(T - 1) * P:N, :]).then_inc(x_in, 16)
                sp.wait_ge(blank_set, 1)
                sp.dma_start(m.recA.rearrange("(p c) f -> p c f", p=P), blank[:, :, :]).then_inc(blanked, 16)
                sp.dma_start(m.recB.rearrange("(p c) f -> p c f", p=P), blank[:, 0:NCB, :]).then_inc(blanked, 16)
                sp.wait_ge(scattered, 16 * 2 * EC)
                sp.dma_start(m.ra[:, :, :], m.recA.rearrange("(p c) f -> p c f", p=P)).then_inc(sorted_in, 16)
                sp.dma_start(m.rb[:, :, :], m.recB.rearrange("(p c) f -> p c f", p=P)).then_inc(sorted_in, 16)
                sp.wait_ge(x_in, 32)

            @block.gpsimd
            def _(pool):
                pool.memset(m.x[:, (T - 1) * D:T * D], 0.0).then_inc(made, 1)
                pool.iota(iota_b[:, :], [[1, NBA]], base=0, channel_multiplier=0,
                          allow_small_or_imprecise_dtypes=True).then_inc(made, 1)
                pool.iota(iota_c[:, :], [[1, NCA]], base=0, channel_multiplier=0,
                          allow_small_or_imprecise_dtypes=True).then_inc(made, 1)
                pool.iota(m.lanes[:, :], [[1, P]], base=0, channel_multiplier=0,
                          allow_small_or_imprecise_dtypes=True).then_inc(made, 1)
                pool.memset(m.ones[:, :], 1.0).then_inc(made, 1)
                pool.memset(m.ident[:, :], 0.0).then_inc(made, 1)
                pool.wait_ge(made, 6)
                pool.affine_select(out=m.ident[:, :], in_=m.ident[:, :], compare_op=ALU.not_equal, fill=1.0,
                                   base=0, pattern=[[-1, P]], channel_multiplier=1).then_inc(made, 1)
                pool.affine_select(out=tri[:, :], in_=m.ones[:, :], compare_op=ALU.is_gt, fill=0.0,
                                   base=0, pattern=[[1, P]], channel_multiplier=-1).then_inc(made, 1)
                pool.wait_ge(placed, 1)
                pool.wait_ge(blanked, 32)

                def columns(i):
                    pool.tensor_copy(pos_blk[:, :, :], posu[:, :, bass.ds(i * SC, SC)]).then_inc(copied, 1)
                    pool.tensor_copy(rec_blk[:, :, :, :], rec[:, :, bass.ds(i * SC, SC), :]).then_inc(copied, 1)
                    pool.wait_ge(copied, 2 * i + 2)
                    alone(pool, m)
                    for j in range(SC):
                        for o, table in enumerate((m.recA, m.recB)):
                            pool.indirect_dma_start(
                                out=table, out_offset=bass.IndirectOffsetOnAxis(ap=pos_blk[:, o, j:j + 1], axis=0),
                                in_=rec_blk[:, o, j, :], in_offset=None).then_inc(scattered, 16)
                    pool.wait_ge(scattered, (i + 1) * (16 * 2 * SC))
                    alone(pool, m)

                with pool.Fori(0, EC // SC) as i:
                    columns(i)

            @block.tensor
            def _(pe):
                pe.wait_ge(made, 8)
                for o, nb in enumerate((NBA, NBB)):
                    pe.wait_ge(totals, o + 1)
                    pe.matmul(m.ps[0:EP, 2 * o, 0:nb], tri[0:EP, 0:EP], row_tot[:, 0:nb], start=True, stop=True)
                    pe.matmul(m.ps[:, 2 * o + 1, 0:nb], m.ones[0:EP, :], row_tot[:, 0:nb],
                              start=True, stop=True).then_inc(counted, 1)

            @block.vector
            def _(v):
                ch = Chain(v, dve)
                link = ch.link
                link(v.memset(blank[:, :, :], 0.0))
                v.memset(blank[:, :, 0:1], -1.0).then_inc(blank_set, 1)
                for j in range(R8 + 3):
                    last = v.memset(m.consts[:, j:j + 1], m.const_values[j])
                link(last)
                link(v.memset(m.zeros[:, :], 0.0))
                link(v.memset(rec[:, 0, :, :], 0.0))
                v.wait_ge(loaded, 16 * 5)
                v.wait_ge(made, 8)
                link(v.tensor_copy(rec[:, 0, :, A_WEIGHT], w_in[:, :]))
                link(v.memset(rec[:, 1, :, :], 0.0))
                src, dst, ty4, ty8 = (ints[:, f, :] for f in range(4))
                link(v.tensor_scalar(tmp_i[:, 0, :], dst, 7, None, ALU.arith_shift_right))
                link(v.scalar_tensor_tensor(out=key[:, 0, :], in0=tmp_i[:, 0, :], scalar=float(R4), in1=ty4,
                                            op0=ALU.mult, op1=ALU.add))
                link(v.tensor_scalar(tmp_i[:, 1, :], src, 7, None, ALU.arith_shift_right))
                link(v.tensor_copy(key[:, 1, :], tmp_i[:, 1, :]))
                link(v.tensor_scalar(tmp_i[:, 0, :], dst, 127, None, ALU.bitwise_and))
                link(v.tensor_scalar(tmp_i[:, 1, :], src, 127, None, ALU.bitwise_and))
                link(v.tensor_copy(rec[:, 0, :, A_LANE], tmp_i[:, 0, :]))
                link(v.tensor_copy(rec[:, 1, :, B_LANE], tmp_i[:, 1, :]))
                link(v.tensor_copy(rec[:, 0, :, A_SRC], src))
                link(v.tensor_copy(rec[:, 1, :, B_DST], dst))
                link(v.tensor_copy(rec[:, 1, :, B_SRC], src))
                link(v.scalar_tensor_tensor(out=rec[:, 0, :, A_SRC8], in0=ty8, scalar=float(NP), in1=src,
                                            op0=ALU.mult, op1=ALU.add))
                link(v.scalar_tensor_tensor(out=rec[:, 0, :, A_SRC4], in0=ty4, scalar=float(NP), in1=src,
                                            op0=ALU.mult, op1=ALU.add))
                link(v.scalar_tensor_tensor(out=rec[:, 0, :, A_DST4], in0=key[:, 0, :], scalar=float(P),
                                            in1=rec[:, 0, :, A_LANE], op0=ALU.mult, op1=ALU.add))
                for o, (nb, nch) in enumerate(((NBA, NCA), (NBB, NCB))):
                    cube = lambda a: a[:, 0:nb * EC].rearrange("p (b c) -> p b c", b=nb)
                    mine = iota_b[0:EP, 0:nb]
                    link(v.tensor_tensor(cube(ind), key[:, o, :].unsqueeze(1).broadcast_to([EP, nb, EC]),
                                         mine.unsqueeze(2).broadcast_to([EP, nb, EC]), op=ALU.is_equal))
                    link(v.tensor_tensor_scan(cum[:, 0:nb * EC], ind[:, 0:nb * EC],
                                              m.zeros[0:EP, 0:1].broadcast_to([EP, nb * EC]), 0.0,
                                              ALU.add, ALU.add))
                    link(v.tensor_copy(row_end[:, 0:nb], cube(cum)[:, :, EC - 1]))
                    link(v.tensor_copy(row_tot[:, 0:1], row_end[:, 0:1]))
                    v.tensor_tensor(row_tot[:, 1:nb], row_end[:, 1:nb], row_end[:, 0:nb - 1],
                                    op=ALU.subtract).then_inc(totals, 1)
                    v.wait_ge(counted, o + 1)
                    link(v.tensor_scalar(nchunk[:, 0:nb], m.ps[:, 2 * o + 1, 0:nb], 127.0, None, ALU.add))
                    link(v.tensor_copy(nchunk_i[:, 0:nb], nchunk[:, 0:nb]))
                    link(v.tensor_scalar(nchunk_i[:, 0:nb], nchunk_i[:, 0:nb], 7, None, ALU.arith_shift_right))
                    link(v.tensor_copy(nchunk[:, 0:nb], nchunk_i[:, 0:nb]))
                    link(v.tensor_tensor_scan(end_chunk[:, 0:nb], nchunk[:, 0:nb],
                                              m.zeros[:, 0:1].broadcast_to([P, nb]), 0.0, ALU.add, ALU.add))
                    link(v.tensor_tensor(nchunk[:, 0:nb], end_chunk[:, 0:nb], nchunk[:, 0:nb], op=ALU.subtract))
                    link(v.tensor_scalar(off[:, 0:nb], nchunk[0:EP, 0:nb], float(P), -1.0, ALU.mult, ALU.add))
                    link(v.tensor_tensor(off[:, 0:nb], off[:, 0:nb], m.ps[0:EP, 2 * o, 0:nb], op=ALU.add))
                    link(v.tensor_tensor(off[:, 1:nb], off[:, 1:nb], row_end[:, 0:nb - 1], op=ALU.subtract))
                    link(v.tensor_tensor(cube(cum), cube(cum), off[:, 0:nb].unsqueeze(2).broadcast_to([EP, nb, EC]),
                                         op=ALU.add))
                    link(v.tensor_tensor(cube(cum), cube(cum), cube(ind), op=ALU.mult))
                    link(v.tensor_reduce(pos[:, o, :], cube(cum).rearrange("p b c -> p c b"), AX.X, ALU.add))
                    link(v.tensor_copy(tmp_i[:, 0, :], pos[:, o, :]))
                    link(v.tensor_scalar(tmp_i[:, 1, :], tmp_i[:, 0, :], 127, None, ALU.bitwise_and))
                    link(v.tensor_scalar(tmp_i[:, 0, :], tmp_i[:, 0, :], 7, None, ALU.arith_shift_right))
                    link(v.scalar_tensor_tensor(out=posu[:, o, :], in0=tmp_i[:, 1, :], scalar=float(nch),
                                                in1=tmp_i[:, 0, :], op0=ALU.mult, op1=ALU.add))
                    grid = mapw[:, 0:nch * nb].rearrange("p (c b) -> p c b", b=nb)
                    link(v.tensor_tensor(grid, end_chunk[0:1, 0:nb].unsqueeze(1).broadcast_to([1, nch, nb]),
                                         iota_c[:, 0:nch].unsqueeze(2).broadcast_to([1, nch, nb]), op=ALU.is_le))
                    link(v.tensor_reduce(cnt[:, 0:nch], grid, AX.X, ALU.add))
                    link(v.tensor_scalar(cnt[:, 0:nch], cnt[:, 0:nch], float(nb - 1), None, ALU.min))
                    if o == 0:
                        link(v.tensor_scalar(m.accA[:, :], cnt[:, 0:nch], float(AW), None, ALU.mult))
                        link(v.tensor_scalar(m.maxA[:, :], cnt[:, 0:nch], float(H), None, ALU.mult))
                        link(v.tensor_copy(cnt_i[:, :], cnt[:, 0:nch]))
                        link(v.tensor_scalar(cnt_i[:, :], cnt_i[:, :], 2, None, ALU.arith_shift_right))
                        link(v.tensor_scalar(m.tileA[:, :], cnt_i[:, :], float(AW), None, ALU.mult))
                    else:
                        link(v.tensor_scalar(m.accB[:, :], cnt[:, 0:nch], float(AW), None, ALU.mult))
                        link(v.tensor_scalar(m.maxB[:, :], cnt[:, 0:nch], float(H), None, ALU.mult))
                v.sem_inc(placed, 1)
                v.wait_ge(sorted_in, 32)
                for f, a in ((A_SRC, m.ix_src), (A_SRC8, m.ix_src8), (A_SRC4, m.ix_src4), (A_DST4, m.ix_dst4)):
                    link(v.tensor_copy(a[:, :], m.ra[:, :, f]))
                for f, a in ((B_DST, m.ix_bdst), (B_SRC, m.ix_bsrc)):
                    link(v.tensor_copy(a[:, :], m.rb[:, :, f]))


def normalise_setup(m, v, ch, stats, mv, rstd, nbias, root_asked, root_done):
    def one(t):
        ch.link(v.bn_stats(stats[:, bass.ds(t * 6, 6)], m.x[:, bass.ds(t * D, D)]))
    ch.rounds(T, 1, one)
    for t in range(T):
        last = v.bn_aggr(mv[:, 2 * t:2 * t + 2], stats[:, 6 * t:6 * t + 6])
    ch.link(last)
    both = mv[:, :].rearrange("p (t k) -> p t k", k=2)
    v.tensor_scalar(rstd[:, :], both[:, :, 1], EPS, None, ALU.add).then_inc(root_asked, 1)
    v.wait_ge(root_done, 1)
    ch.link(v.reciprocal(rstd[:, :], rstd[:, :]))
    ch.link(v.scalar_tensor_tensor(out=nbias[:, :], in0=both[:, :, 0], scalar=-1.0, in1=rstd[:, :],
                                   op0=ALU.mult, op1=ALU.mult))


def project(m, nc, name, source, h_table=None, tables=(), small=None, own=None):
    n_tab = len(tables)
    outs = [("table", w, d) for w, d in tables]
    if own:
        outs.append(("own", *own))
    if small:
        outs.append(("small", *small))
    Q = 2 * len(outs)
    BANKS = 6
    engine = ["v" if outs[q % len(outs)][0] != "table" or q % 2 else "a" for q in range(Q)] if outs else []
    rank = [engine[:q].count(engine[q]) for q in range(Q)]
    per_round = {e: engine.count(e) for e in "va"}
    QT = 2 * n_tab
    SLOTS = 4

    def before(q, count, lanes):
        if q >= lanes:
            return 0, q - lanes
        return 1, max((z for z in range(count) if z % lanes == q), default=q)

    ks = ExitStack()
    with ks:
        sb = lambda n, s, d=F32: ks.enter_context(nc.sbuf_tensor(f"{name}_{n}", s, d))
        sem = lambda n: semaphore(m, nc, f"{name}_{n}")
        stats = sb("stats", [P, T * 6])
        mv = sb("mv", [P, T * 2])
        rstd = sb("rstd", [P, T])
        nbias = sb("nbias", [P, T])
        root_asked, root_done, norm_set = sem("root_asked"), sem("root_done"), sem("norm_set")
        h_ready, turned, h_turned, multiplied = sem("h_ready"), sem("turned"), sem("h_turned"), sem("multiplied")
        left = {"v": sem("left_v"), "a": sem("left_a")}
        stored = [sem(f"stored{s}") for s in range(SLOTS)]
        h_stored = [sem(f"h_stored{s}") for s in range(2)]
        dve = sem("dve")

        def tile(i, b):
            return i * 2 + b

        def leave(eng, who, i, b):
            for o, out in enumerate(outs):
                q = b * len(outs) + o
                if engine[q] != who:
                    continue
                eng.wait_ge(multiplied, i * Q + q + 1)
                bank = m.ps[:, 2 + q % BANKS, :]
                kind = out[0]
                if kind == "table":
                    qt = b * n_tab + o
                    wait_at_least(eng, stored[qt % SLOTS], (i * (QT // SLOTS) + qt // SLOTS) * 16)
                    if not isinstance(i, int):
                        alone(eng, m)
                    dst = m.stage[:, qt % SLOTS, :]
                    ins = eng.tensor_copy(dst, bank) if who == "v" else eng.activation(dst, bank, ACT.Copy)
                elif kind == "own":
                    ins = eng.tensor_tensor(out[3][:, bass.ds(tile(i, b) * D, D)], bank, out[2], op=ALU.add)
                else:
                    if not isinstance(i, int):
                        alone(eng, m)
                    w = out[1].shape[2]
                    ins = eng.tensor_copy(out[2][:, bass.ds(tile(i, b) * w, w)], bank[:, 0:w])
                ins.then_inc(left[who], 1)

        with nc.Block() as block:

            @block.vector
            def _(v):
                ch = Chain(v, dve)
                if source == "norm":
                    normalise_setup(m, v, ch, stats, mv, rstd, nbias, root_asked, root_done)
                v.sem_inc(norm_set, 1)

                def pair(i):
                    for b in range(2):
                        t = tile(i, b)
                        if source == "mid":
                            wait_at_least(v, turned, t - 1)
                            ch.link(v.tensor_tensor(m.h[:, b, :], m.region[:, bass.ds(t * AW, D)],
                                                    m.own[:, bass.ds(t * D, D)], op=ALU.add))
                            v.tensor_scalar(m.h[:, b, :], m.h[:, b, :], 0.0, None, ALU.max).then_inc(h_ready, 1)
                        if outs:
                            v.wait_ge(turned, t + 1)
                            if not (isinstance(t, int) and t < 2):
                                v.wait_ge(multiplied, (i - 1) * Q + (b + 1) * len(outs))
                            v.tensor_copy(m.hT[:, b, 0:KC, :].rearrange("p k n -> p (k n)"), m.ps[:, b, :])\
                             .then_inc(h_turned, 1)
                            leave(v, "v", i, b)
                if source == "mid" or outs:
                    ch.rounds(T // 2, 2 if source == "mid" else 0, pair)

            @block.scalar
            def _(a):
                if source == "norm":
                    a.wait_ge(root_asked, 1)
                    a.activation(rstd[:, :], rstd[:, :], ACT.Sqrt).then_inc(root_done, 1)
                a.wait_ge(norm_set, 1)
                def pair(i):
                    for b in range(2):
                        t = tile(i, b)
                        if source == "norm":
                            if outs:
                                wait_at_least(a, turned, t - 1)
                            if h_table is not None:
                                wait_at_least(a, h_stored[b], i * 16)
                            if not isinstance(i, int):
                                alone(a, m)
                            a.activation(m.h[:, b, :], m.x[:, bass.ds(t * D, D)], ACT.Relu,
                                         bias=nbias[:, bass.ds(t, 1)], scale=rstd[:, bass.ds(t, 1)])\
                             .then_inc(h_ready, 1)
                        leave(a, "a", i, b)
                peeled(a, T // 2, pair)

            @block.tensor
            def _(pe):
                def pair(i):
                    for b in range(2):
                        t = tile(i, b)
                        pe.wait_ge(h_ready, t + 1)
                        wait_at_least(pe, h_turned, t - 1)
                        for k in range(KC):
                            last = pe.transpose(m.ps[:, b, k * P:(k + 1) * P], m.h[:, b, k * P:(k + 1) * P],
                                                m.ident[:, :])
                        last.then_inc(turned, 1)
                        pe.wait_ge(h_turned, t + 1)
                        for o, out in enumerate(outs):
                            q = b * len(outs) + o
                            back, z = before(q, Q, BANKS)
                            if not (isinstance(i, int) and i < back):
                                e = engine[z]
                                pe.wait_ge(left[e], (i - back) * per_round[e] + rank[z] + 1)
                            w = out[1]
                            for k in range(KC):
                                last = pe.matmul(m.ps[:, 2 + q % BANKS, 0:w.shape[2]], m.hT[:, b, k, :],
                                                 w[:, k, :], start=k == 0, stop=k == KC - 1)
                            last.then_inc(multiplied, 1)
                if outs:
                    peeled(pe, T // 2, pair)

            @block.sync
            def _(sp):
                def pair(i):
                    for b in range(2):
                        t = tile(i, b)
                        if h_table is not None:
                            sp.wait_ge(h_ready, t + 1)
                            sp.dma_start(h_table[bass.ds(t * P, P), :], m.h[:, b, :]).then_inc(h_stored[b], 16)
                        for o in range(n_tab):
                            q, qt = b * len(outs) + o, b * n_tab + o
                            e = engine[q]
                            sp.wait_ge(left[e], i * per_round[e] + rank[q] + 1)
                            sp.dma_start(outs[o][2][bass.ds(t * P, P), :], m.stage[:, qt % SLOTS, :])\
                              .then_inc(stored[qt % SLOTS], 16)
                if h_table is not None or n_tab:
                    peeled(sp, T // 2, pair)
                if h_table is not None:
                    for s in h_stored:
                        sp.wait_ge(s, 16 * (T // 2))
                if n_tab:
                    for s in stored:
                        sp.wait_ge(s, 16 * (T // 2) * (QT // SLOTS))


def gather_rows(m, nc, name, index, n_chunks, table, width, out):
    ks = ExitStack()
    with ks:
        sem = lambda n: semaphore(m, nc, f"{name}_{n}")
        indexed, taken = sem("indexed"), sem("taken")
        fetched = [sem(f"fetched{g}") for g in range(G)]
        rounds = n_chunks // G

        with nc.Block() as block:

            @block.scalar
            def _(a):
                for g in range(G):
                    a.copy(m.ib[:, g:g + 1], index[:, g:g + 1]).then_inc(indexed, 1)
                def body(i):
                    for g in range(G):
                        a.wait_ge(taken, i * G + g + 1)
                        alone(a, m)
                        a.copy(m.ib[:, g:g + 1], index[:, bass.ds((i + 1) * G + g, 1)]).then_inc(indexed, 1)
                with a.Fori(0, rounds - 1) as i:
                    body(i)

            @block.gpsimd
            def _(pool):
                def body(i):
                    for g in range(G):
                        pool.wait_ge(indexed, i * G + g + 1)
                        alone(pool, m)
                        pool.indirect_dma_start(
                            out=m.rows[:, g, 0:width], out_offset=None, in_=table,
                            in_offset=bass.IndirectOffsetOnAxis(ap=m.ib[:, g:g + 1], axis=0))\
                            .then_inc(fetched[g], 16)
                with pool.Fori(0, rounds) as i:
                    body(i)

            @block.vector
            def _(v):
                def body(i):
                    for g in range(G):
                        v.wait_ge(fetched[g], i * 16 + 16)
                        alone(v, m)
                        v.tensor_copy(out[:, bass.ds((i * G + g) * width, width)], m.rows[:, g, 0:width])\
                         .then_inc(taken, 1)
                with v.Fori(0, rounds) as i:
                    body(i)


def segment_max(m, nc, name, n_chunks, buckets, lane, logits, heads, places, best):
    ks = ExitStack()
    with ks:
        sb = lambda n, s, d=F32: ks.enter_context(nc.sbuf_tensor(f"{name}_{n}", s, d))
        sem = lambda n: semaphore(m, nc, f"{name}_{n}")
        masks = sb("masks", [P, PSLOTS, P])
        marked = m.rows[:, :, :].rearrange("p g d -> p (g d)").rearrange("p (s w) -> p s w", s=PSLOTS)
        chunk_best = sb("chunk_best", [P, heads])
        masked, filled, turned, reduced, dve = (sem(n) for n in ("masked", "filled", "turned", "reduced", "dve"))
        rounds = n_chunks // G

        with nc.Block() as block:

            @block.vector
            def _(v):
                ch = Chain(v, dve)

                def mask(c, s):
                    v.tensor_scalar(masks[:, s, :], m.lanes[:, :], lane(c), -BIG, ALU.not_equal, ALU.mult)\
                     .then_inc(masked, 1)

                for s in range(PSLOTS):
                    mask(s, s)

                def body(i):
                    for g in range(G):
                        c, s = i * G + g, g % PSLOTS
                        at = v.value_load(places[0:1, bass.ds(c, 1)], min_val=0, max_val=(buckets - 1) * H)
                        v.wait_ge(turned, c + 1)
                        v.tensor_reduce(chunk_best[:, :],
                                        m.ps[:, 2 * s:2 * s + 2, :].rearrange("p a b -> p (a b)")[:, 0:heads * P]
                                        .rearrange("p (h e) -> p h e", e=P), AX.X, ALU.max).then_inc(reduced, 1)
                        v.wait_ge(reduced, c + 1)
                        b = best[:, bass.ds(at, heads)]
                        ch.link(v.tensor_tensor(b, b, chunk_best[:, :], op=ALU.max))
                        if not (isinstance(c, int) and c + PSLOTS >= n_chunks):
                            mask(c + PSLOTS, s)

                ch.rounds(rounds, G, body)

            @block.scalar
            def _(a):
                def body(i):
                    for g in range(G):
                        c, s = i * G + g, g % PSLOTS
                        a.wait_ge(masked, c + 1)
                        wait_at_least(a, turned, c + 1 - PSLOTS)
                        alone(a, m)
                        for h in range(heads):
                            last = a.activation(marked[:, s, h * P:(h + 1) * P], masks[:, s, :], ACT.Identity,
                                                bias=logits[:, bass.ds(c * H + h, 1)])
                        last.then_inc(filled, 1)
                peeled(a, rounds, body)

            @block.tensor
            def _(pe):
                def body(i):
                    for g in range(G):
                        c, s = i * G + g, g % PSLOTS
                        pe.wait_ge(filled, c + 1)
                        wait_at_least(pe, reduced, c + 1 - PSLOTS)
                        for h in range(heads):
                            last = pe.transpose(m.ps[:, 2 * s + h // 4, (h % 4) * P:(h % 4 + 1) * P],
                                                marked[:, s, h * P:(h + 1) * P], m.ident[:, :])
                        last.then_inc(turned, 1)
                peeled(pe, rounds, body)


def aggregate(m, nc, name, n_chunks, buckets, index, lane, table, places, weight=None, head_weight=None, sums=None):
    per_head = head_weight is not None
    width = AW if sums else D
    ks = ExitStack()
    with ks:
        sb = lambda n, s, d=F32: ks.enter_context(nc.sbuf_tensor(f"{name}_{n}", s, d))
        sem = lambda n: semaphore(m, nc, f"{name}_{n}")
        onehot = sb("onehot", [P, PSLOTS, P])
        msg = m.stage
        indexed, hot, weighed, summed, added = (sem(n) for n in ("indexed", "hot", "weighed", "summed", "added"))
        fetched = [sem(f"fetched{g}") for g in range(G)]
        rounds = n_chunks // G
        used = weighed if per_head else summed

        with nc.Block() as block:

            @block.scalar
            def _(a):
                for g in range(G):
                    a.copy(m.ib[:, g:g + 1], index[:, g:g + 1]).then_inc(indexed, 1)
                with a.Fori(0, rounds - 1) as i:
                    for g in range(G):
                        a.wait_ge(used, i * G + g + 1)
                        alone(a, m)
                        a.copy(m.ib[:, g:g + 1], index[:, bass.ds((i + 1) * G + g, 1)]).then_inc(indexed, 1)

            @block.gpsimd
            def _(pool):
                with pool.Fori(0, rounds) as i:
                    for g in range(G):
                        pool.wait_ge(indexed, i * G + g + 1)
                        alone(pool, m)
                        pool.indirect_dma_start(
                            out=m.rows[:, g, :], out_offset=None, in_=table,
                            in_offset=bass.IndirectOffsetOnAxis(ap=m.ib[:, g:g + 1], axis=0))\
                            .then_inc(fetched[g], 16)

            @block.vector
            def _(v):
                def heat(i, g):
                    c, s = i * G + g, g % PSLOTS
                    if weight is None:
                        v.tensor_scalar(onehot[:, s, :], m.lanes[:, :], lane(c), None, ALU.is_equal).then_inc(hot, 1)
                    else:
                        v.tensor_scalar(onehot[:, s, :], m.lanes[:, :], lane(c), weight(c), ALU.is_equal, ALU.mult)\
                         .then_inc(hot, 1)
                    if per_head:
                        v.wait_ge(fetched[g], i * 16 + 16)
                        v.tensor_tensor(msg[:, s, :].rearrange("p (h c) -> p h c", h=H),
                                        m.rows[:, g, :].rearrange("p (h c) -> p h c", h=H),
                                        head_weight(c).unsqueeze(2).broadcast_to([P, H, C]), op=ALU.mult)\
                         .then_inc(weighed, 1)

                for s in range(PSLOTS):
                    heat(0, s)

                def body(i):
                    for g in range(G):
                        c, s = i * G + g, g % PSLOTS
                        at = v.value_load(places[0:1, bass.ds(c, 1)], min_val=0, max_val=(buckets - 1) * AW)
                        v.wait_ge(summed, c + 1)
                        wait_at_least(v, added, c)
                        acc = m.region[:, bass.ds(at, width)]
                        sums_of = m.ps[:, 2 * s:2 * s + 2, :].rearrange("p a b -> p (a b)")[:, 0:width]
                        v.tensor_tensor(acc, acc, sums_of, op=ALU.add).then_inc(added, 1)
                        if not (isinstance(c, int) and c + PSLOTS >= n_chunks):
                            ahead = g + PSLOTS
                            heat(i + ahead // G, ahead % G)
                peeled(v, rounds, body)

            @block.tensor
            def _(pe):
                def body(i):
                    for g in range(G):
                        c, s = i * G + g, g % PSLOTS
                        pe.wait_ge(hot, c + 1)
                        if per_head:
                            pe.wait_ge(weighed, c + 1)
                        else:
                            pe.wait_ge(fetched[g], i * 16 + 16)
                        wait_at_least(pe, added, c + 1 - PSLOTS)
                        rows = msg[:, s, :] if per_head else m.rows[:, g, :]
                        if sums:
                            pe.matmul(m.ps[:, 2 * s + 1, 0:H], onehot[:, s, :], sums(c), start=True, stop=True)
                        pe.matmul(m.ps[:, 2 * s, :], onehot[:, s, :], rows, start=True, stop=True).then_inc(summed, 1)
                peeled(pe, rounds, body)


def fold_attention(m, nc, name, loads, folds):
    ks = ExitStack()
    with ks:
        sem = lambda n: semaphore(m, nc, f"{name}_{n}")
        loaded, dve = sem("loaded"), sem("dve")
        with nc.Block() as block:

            @block.sync
            def _(sp):
                for dst, src in loads:
                    sp.dma_start(dst, src).then_inc(loaded, 16)

            @block.vector
            def _(v):
                ch = Chain(v, dve)
                v.wait_ge(loaded, 16 * len(loads))
                for w, row, groups, out in folds:
                    prod = m.scratch.rearrange("p (k d) -> p k d", k=KC)
                    ch.link(v.tensor_tensor(prod, w, row.unsqueeze(1).broadcast_to([P, KC, D]), op=ALU.mult))
                    for k in range(KC):
                        ch.link(v.tensor_reduce(out[:, k, :], prod[:, k, :].rearrange("p (g c) -> p g c", g=groups),
                                                AX.X, ALU.add))


def attention_table(m, nc, name, buckets, target, best, out_sb, table, own=None):
    ks = ExitStack()
    with ks:
        sem = lambda n: semaphore(m, nc, f"{name}_{n}")
        dve, set_, stored = sem("dve"), sem("set"), sem("stored")
        asked, done = sem("asked"), sem("done")
        logit, top = out_sb[:, :, 0:H], out_sb[:, :, H:2 * H]
        with nc.Block() as block:

            @block.vector
            def _(v):
                ch = Chain(v, dve)
                link = ch.link
                link(v.tensor_copy(logit, target))
                link(v.tensor_tensor(top, best, logit, op=ALU.add))
                link(v.tensor_scalar(m.scratch[:, 0:buckets * H].rearrange("p (b h) -> p b h", h=H), top, 0.2, None, ALU.mult))
                v.tensor_tensor(top, top, m.scratch[:, 0:buckets * H].rearrange("p (b h) -> p b h", h=H),
                                op=ALU.max).then_inc(set_, 1)
                v.wait_ge(set_, 1)
                if own:
                    src, w = own
                    link(v.tensor_tensor(w, src, logit, op=ALU.add))
                    s3 = m.scratch[:, 0:buckets * H].rearrange("p (b h) -> p b h", h=H)
                    link(v.tensor_scalar(s3, w, 0.2, None, ALU.mult))
                    link(v.tensor_tensor(w, w, s3, op=ALU.max))
                    v.tensor_tensor(w, w, top, op=ALU.subtract).then_inc(asked, 1)

            @block.scalar
            def _(a):
                if own:
                    a.wait_ge(asked, 1)
                    a.activation(own[1], own[1], ACT.Exp).then_inc(done, 1)

            @block.sync
            def _(sp):
                sp.wait_ge(set_, 1)
                sp.dma_start(table.rearrange("(b p) f -> p b f", p=P), out_sb[:, 0:buckets, :]).then_inc(stored, 16)
                sp.wait_ge(stored, 16)


def edge_weights(m, nc, name, n_chunks, logits, targets, out):
    ks = ExitStack()
    with ks:
        sem = lambda n: semaphore(m, nc, f"{name}_{n}")
        dve, asked, done = sem("dve"), sem("asked"), sem("done")
        w = n_chunks * H
        cube = lambda a: a.rearrange("p (c h) -> p c h", h=H)
        tg = targets[:, 0:n_chunks * 2 * H].rearrange("p (c f) -> p c f", f=2 * H)
        scr = m.scratch[:, 0:w]
        with nc.Block() as block:

            @block.vector
            def _(v):
                ch = Chain(v, dve)
                link = ch.link
                link(v.tensor_tensor(cube(out[:, 0:w]), cube(logits[:, 0:w]), tg[:, :, 0:H], op=ALU.add))
                link(v.tensor_scalar(scr, out[:, 0:w], 0.2, None, ALU.mult))
                link(v.tensor_tensor(out[:, 0:w], out[:, 0:w], scr, op=ALU.max))
                link(v.tensor_tensor(cube(out[:, 0:w]), cube(out[:, 0:w]), tg[:, :, H:2 * H], op=ALU.subtract))
                v.tensor_scalar(out[:, 0:w], out[:, 0:w], 0.0, None, ALU.min).then_inc(asked, 1)

            @block.scalar
            def _(a):
                a.wait_ge(asked, 1)
                a.activation(out[:, 0:w], out[:, 0:w], ACT.Exp).then_inc(done, 1)


def fill(m, nc, name, jobs):
    ks = ExitStack()
    with ks:
        sem = lambda n: semaphore(m, nc, f"{name}_{n}")
        dve, stored, set_ = sem("dve"), sem("stored"), sem("set")
        with nc.Block() as block:

            @block.vector
            def _(v):
                ch = Chain(v, dve)
                for kind, dst, what in jobs:
                    if kind == "set":
                        ch.link(v.memset(dst, what))
                    elif kind == "copy":
                        ch.link(v.tensor_copy(dst, what))
                    elif kind == "add":
                        ch.link(v.tensor_tensor(dst, dst, what, op=ALU.add))
                v.sem_inc(set_, 1)

            @block.sync
            def _(sp):
                stores = [(d, w) for k, d, w in jobs if k == "store"]
                if stores:
                    sp.wait_ge(set_, 1)
                    for d, w in stores:
                        sp.dma_start(d, w).then_inc(stored, 16)
                    sp.wait_ge(stored, 16 * len(stores))


def acc_rows(m, n=T):
    return m.region[:, 0:n * AW].rearrange("p (b w) -> p b w", w=AW)


def spline_network(m, nc):
    J2 = 2
    PIECES = R8 // J2
    W = J2 * D
    CA, CB = (1 / 6) ** (1 / 3), (4 / 6) ** (1 / 3)
    ks = ExitStack()
    with ks:
        sb = lambda n, s, d=F32: ks.enter_context(nc.sbuf_tensor(f"kan_{n}", s, d))
        sem = lambda n: semaphore(m, nc, f"kan_{n}")
        weights = m.region[:, T * AW:T * AW + (R8 + 1) * KC * D].rearrange("p (j k d) -> p j k d", k=KC, d=D)
        dist, wide, near, wide2, near2 = (m.own[:, n * W:(n + 1) * W] for n in range(5))
        basis = m.rows[:, 0:4, :].rearrange("p (b a) d -> p b (a d)", b=2)
        aT, silu, grown = (m.rows[:, 4 + n, :] for n in range(3))
        rden = sb("rden", [P, T])
        loaded, den_set, agg_ready, turned = (sem(n) for n in ("loaded", "den_set", "agg_ready", "turned"))
        aT_set, grown_set, silu_set, powers = (sem(n) for n in ("aT_set", "grown_set", "silu_set", "powers"))
        cubed, basis_set, eaten, whole, added = (sem(n) for n in ("cubed", "basis_set", "eaten", "whole", "added"))
        dve, act = sem("dve"), sem("act")
        acc = acc_rows(m)

        with nc.Block() as block:

            @block.sync
            def _(sp):
                sp.dma_start(weights[:, 0, :, :], m.base_wT.rearrange("(k p) d -> p k d", p=P)).then_inc(loaded, 16)
                for j in range(R8):
                    sp.dma_start(weights[:, 1 + j, :, :], m.spline_wT[j].rearrange("(k p) d -> p k d", p=P))\
                      .then_inc(loaded, 16)

            @block.scalar
            def _(a):
                ch = Chain(a, act)
                a.wait_ge(den_set, 1)

                def one(t):
                    wait_at_least(a, turned, t)
                    if not isinstance(t, int):
                        alone(a, m)
                    a.activation(m.h[:, 0, :], m.region[:, bass.ds(t * AW, D)], ACT.Copy,
                                 scale=rden[:, bass.ds(t, 1)]).then_inc(agg_ready, 1)
                    a.wait_ge(aT_set, t + 1)
                    wait_at_least(a, silu_set, t)
                    a.activation(grown, aT, ACT.Exp, scale=-1.0).then_inc(grown_set, 1)
                    for q in range(PIECES):
                        for j in range(J2):
                            last = a.activation(dist[:, j * D:(j + 1) * D], aT, ACT.Abs, scale=2.5,
                                                bias=m.consts[:, J2 * q + j:J2 * q + j + 1])
                        ch.link(last)
                        wait_at_least(a, cubed, t * PIECES + q)
                        a.activation(wide, dist, ACT.Relu, scale=-CA, bias=m.consts[:, R8:R8 + 1])
                        ch.link(a.activation(near, dist, ACT.Relu, scale=-CB,
                                             bias=m.consts[:, R8 + 1:R8 + 2]))
                        a.activation(wide2, wide, ACT.Square)
                        a.activation(near2, near, ACT.Square).then_inc(powers, 1)
                ch.rounds(T, 2 * PIECES, one)

            @block.vector
            def _(v):
                ch = Chain(v, dve)
                link = ch.link
                link(v.tensor_scalar(rden[:, :], acc[:, :, D], 1e-30, None, ALU.max))
                v.reciprocal(rden[:, :], rden[:, :]).then_inc(den_set, 1)

                def one(t):
                    v.wait_ge(turned, t + 1)
                    wait_at_least(v, powers, t * PIECES)
                    v.tensor_copy(aT, m.ps[:, 0, :]).then_inc(aT_set, 1)
                    v.wait_ge(grown_set, t + 1)
                    v.wait_ge(aT_set, t + 1)
                    link(v.tensor_scalar(grown, grown, 1.0, None, ALU.add))
                    link(v.reciprocal(grown, grown))
                    wait_at_least(v, whole, t)
                    v.tensor_tensor(silu, aT, grown, op=ALU.mult).then_inc(silu_set, 1)
                    for q in range(PIECES):
                        b = q % 2
                        v.wait_ge(powers, t * PIECES + q + 1)
                        v.tensor_tensor(wide2, wide2, wide, op=ALU.mult)
                        link(v.tensor_tensor(near2, near2, near, op=ALU.mult))
                        wait_at_least(v, eaten, t * PIECES + q - 1)
                        v.tensor_tensor(basis[:, b, :], wide2, near2, op=ALU.subtract)\
                         .then_inc(basis_set, 1)
                        v.wait_ge(basis_set, t * PIECES + q + 1)
                        v.sem_inc(cubed, 1)
                    v.wait_ge(whole, t + 1)
                    xt = m.x[:, bass.ds(t * D, D)]
                    v.tensor_tensor(xt, xt, m.ps[:, 2, :], op=ALU.add).then_inc(added, 1)
                ch.rounds(T, 2 + PIECES, one)

            @block.tensor
            def _(pe):
                pe.wait_ge(loaded, 16 * (R8 + 1))

                def one(t):
                    pe.wait_ge(agg_ready, t + 1)
                    wait_at_least(pe, aT_set, t)
                    for k in range(KC):
                        last = pe.transpose(m.ps[:, 0, k * P:(k + 1) * P], m.h[:, 0, k * P:(k + 1) * P], m.ident[:, :])
                    last.then_inc(turned, 1)
                    pe.wait_ge(silu_set, t + 1)
                    wait_at_least(pe, added, t)
                    for k in range(KC):
                        pe.matmul(m.ps[:, 2, :], silu[:, k * P:(k + 1) * P], weights[:, 0, k, :],
                                  start=k == 0, stop=False)
                    for q in range(PIECES):
                        pe.wait_ge(basis_set, t * PIECES + q + 1)
                        for j in range(J2):
                            for k in range(KC):
                                end = q == PIECES - 1 and j == J2 - 1 and k == KC - 1
                                last = pe.matmul(m.ps[:, 2, :], basis[:, q % 2, j * D + k * P:j * D + (k + 1) * P],
                                                 weights[:, 1 + J2 * q + j, k, :], start=False, stop=end)
                        last.then_inc(eaten, 1)
                    pe.wait_ge(eaten, (t + 1) * PIECES)
                    pe.sem_inc(whole, 1)
                peeled(pe, T, one)


def mean_layer(m, nc):
    ks = ExitStack()
    with ks:
        sb = lambda n, s, d=F32: ks.enter_context(nc.sbuf_tensor(f"mean_{n}", s, d))
        sem = lambda n: semaphore(m, nc, f"mean_{n}")
        weights = m.region[:, T * AW:T * AW + 2 * KC * D].rearrange("p (k d) -> p k d", d=D)
        bias = sb("bias", [P, D])
        rdeg = sb("rdeg", [P, T])
        loaded, deg_set, neigh_ready, turned, copied, whole, added = (
            sem(n) for n in ("loaded", "deg_set", "neigh_ready", "turned", "copied", "whole", "added"))
        h_in = [sem(f"h_in{b}") for b in range(2)]
        dve = sem("dve")
        acc = acc_rows(m)

        with nc.Block() as block:

            @block.sync
            def _(sp):
                sp.dma_start(weights, m.w1.rearrange("(k p) d -> p k d", p=P)).then_inc(loaded, 16)
                sp.dma_start(bias[:, :], m.b1.rearrange("(a d) -> a d", a=1).broadcast_to([P, D])).then_inc(loaded, 16)

                def pair(i):
                    for b in range(2):
                        t = 2 * i + b
                        wait_at_least(sp, turned, t - 1)
                        sp.dma_start(m.rows[:, b, :], m.h_table[bass.ds(t * P, P), :]).then_inc(h_in[b], 16)
                peeled(sp, T // 2, pair)

            @block.scalar
            def _(a):
                a.wait_ge(deg_set, 1)

                def pair(i):
                    for b in range(2):
                        t = 2 * i + b
                        wait_at_least(a, turned, t - 1)
                        if not isinstance(i, int):
                            alone(a, m)
                        a.activation(m.h[:, b, :], m.region[:, bass.ds(t * AW, D)], ACT.Copy,
                                     scale=rdeg[:, bass.ds(t, 1)]).then_inc(neigh_ready, 1)
                peeled(a, T // 2, pair)

            @block.tensor
            def _(pe):
                pe.wait_ge(loaded, 32)

                def pair(i):
                    for b in range(2):
                        t = 2 * i + b
                        pe.wait_ge(h_in[b], i * 16 + 16)
                        pe.wait_ge(neigh_ready, t + 1)
                        wait_at_least(pe, copied, t - 1)
                        for o, rows in enumerate((m.rows[:, b, :], m.h[:, b, :])):
                            for k in range(KC):
                                last = pe.transpose(m.ps[:, 2 * b + o, k * P:(k + 1) * P], rows[:, k * P:(k + 1) * P],
                                                    m.ident[:, :])
                        last.then_inc(turned, 1)
                        pe.wait_ge(copied, t + 1)
                        wait_at_least(pe, added, t - 1)
                        for k in range(2 * KC):
                            last = pe.matmul(m.ps[:, 4 + b, :], m.hT[:, b, k, :], weights[:, k, :],
                                             start=k == 0, stop=k == 2 * KC - 1)
                        last.then_inc(whole, 1)
                peeled(pe, T // 2, pair)

            @block.vector
            def _(v):
                ch = Chain(v, dve)
                ch.link(v.tensor_scalar(rdeg[:, :], acc[:, :, D], 1.0, None, ALU.max))
                v.reciprocal(rdeg[:, :], rdeg[:, :]).then_inc(deg_set, 1)
                v.wait_ge(loaded, 32)

                def pair(i):
                    for b in range(2):
                        t = 2 * i + b
                        v.wait_ge(turned, t + 1)
                        wait_at_least(v, whole, t - 1)
                        v.tensor_copy(m.hT[:, b, :, :].rearrange("p k n -> p (k n)"),
                                      m.ps[:, 2 * b:2 * b + 2, :].rearrange("p a n -> p (a n)")).then_inc(copied, 1)
                        v.wait_ge(whole, t + 1)
                        ch.link(v.tensor_tensor(m.stage[:, b, :], m.ps[:, 4 + b, :], bias[:, :], op=ALU.add))
                        xt = m.x[:, bass.ds(t * D, D)]
                        v.scalar_tensor_tensor(out=xt, in0=m.stage[:, b, :], scalar=0.0, in1=xt,
                                               op0=ALU.max, op1=ALU.add).then_inc(added, 1)
                ch.rounds(T // 2, 2, pair)


def mix_bases(m, nc, name, basis, comp, loop_w, bias):
    ks = ExitStack()
    with ks:
        sem = lambda n: semaphore(m, nc, f"{name}_{n}")
        loaded, dve = sem("loaded"), sem("dve")
        base_in = [sem(f"base_in{b}") for b in range(2)]
        weights = m.region[:, T * AW:T * AW + R8 * KC * D].rearrange("p (r n) -> p r n", r=R8)
        mixed = sem("mixed")
        with nc.Block() as block:

            @block.sync
            def _(sp):
                sp.dma_start(m.comp[:, :], comp.rearrange("(a r) b -> a (r b)", a=1).broadcast_to([P, R8 * BASES]))\
                  .then_inc(loaded, 16)
                sp.dma_start(m.own_bias[:, :], bias.rearrange("(a d) -> a d", a=1).broadcast_to([P, D])).then_inc(loaded, 16)
                sp.dma_start(m.loop_w[:, :, :], loop_w.rearrange("(k p) d -> p k d", p=P)).then_inc(loaded, 16)
                for b in range(BASES):
                    if b >= 2:
                        sp.wait_ge(mixed, b - 1)
                    sp.dma_start(m.rows[:, 4 * (b % 2):4 * (b % 2) + 4, :], basis[b].rearrange("(k p) d -> p k d", p=P))\
                      .then_inc(base_in[b % 2], 16)

            @block.vector
            def _(v):
                ch = Chain(v, dve)
                v.wait_ge(loaded, 48)
                for b in range(BASES):
                    v.wait_ge(base_in[b % 2], 16 * (b // 2 + 1))
                    src = m.rows[:, 4 * (b % 2):4 * (b % 2) + 4, :].rearrange("p k d -> p (k d)")
                    for r in range(R8):
                        c = m.comp[:, r * BASES + b:r * BASES + b + 1]
                        if b == 0:
                            last = v.tensor_scalar(weights[:, r, :], src, c, None, ALU.mult)
                        else:
                            last = v.scalar_tensor_tensor(out=weights[:, r, :], in0=src, scalar=c,
                                                          in1=weights[:, r, :], op0=ALU.mult, op1=ALU.add)
                        if r < R8 - 1:
                            continue
                        last.then_inc(mixed, 1)
                        v.wait_ge(mixed, b + 1)


def fuse_relations(m, nc):
    ks = ExitStack()
    with ks:
        sb = lambda n, s, d=F32: ks.enter_context(nc.sbuf_tensor(f"fuse_{n}", s, d))
        sem = lambda n: semaphore(m, nc, f"fuse_{n}")
        w1 = m.rows[:, 0:2, :].rearrange("p a d -> p (a d)").rearrange("p (k d) -> p k d", k=KC)
        b1 = sb("b1", [P, SEM_D])
        w2 = sb("w2", [P, SEM_D])
        bias = m.rows[:, 2:2 + R4, :]
        five = lambda o, n: m.own[:, o * D:(o + n) * D].rearrange("p (r d) -> p r d", d=D)
        xt, z, zT = five(0, R4), five(R4, R4), five(2 * R4, 2)
        den = sb("den", [P, R4, H])
        own = sb("own", [P, R4, H])
        pre, th = (m.rows[:, 6 + n, :].rearrange("p (b d) -> p b d", b=2) for n in range(2))
        junk = sb("junk", [P, SEM_D])
        w = sb("w", [P, R4])
        top = sb("top", [P, 4])
        beta = sb("beta", [P, R4])
        loaded, xt_in, z_ready, turned, zT_set, pre_ready = (
            sem(n) for n in ("loaded", "xt_in", "z_ready", "turned", "zT_set", "pre_ready"))
        pre_set, th_set, scored, asked, answered, out_set, stored = (
            sem(n) for n in ("pre_set", "th_set", "scored", "asked", "answered", "out_set", "stored"))
        dve = sem("dve")
        acc = m.region[:, 0:NBA * AW]

        with nc.Block() as block:

            @block.sync
            def _(sp):
                sp.dma_start(w1[:, :, :], m.sem_w1.rearrange("(k p) d -> p k d", p=P)).then_inc(loaded, 16)
                sp.dma_start(b1[:, :], m.sem_b1.rearrange("(a d) -> a d", a=1).broadcast_to([P, SEM_D])).then_inc(loaded, 16)
                sp.dma_start(w2[:, :], m.sem_w2.rearrange("d a -> a d").broadcast_to([P, SEM_D])).then_inc(loaded, 16)
                sp.dma_start(bias[:, :, :].rearrange("p r d -> p (r d)"),
                             m.bias3.rearrange("(a r) d -> a (r d)", a=1).broadcast_to([P, R4 * D])).then_inc(loaded, 16)
                view = m.xt_table.rearrange("(r n) d -> n r d", r=R4)

                def one(t):
                    wait_at_least(sp, z_ready, R4 * t)
                    sp.dma_start(xt[:, :, :], view[bass.ds(t * P, P), :, :]).then_inc(xt_in, 16)
                peeled(sp, T, one)

            @block.vector
            def _(v):
                ch = Chain(v, dve)
                link = ch.link
                v.wait_ge(loaded, 64)
                by_head = lambda a: a.rearrange("p (h c) -> p h c", h=H)
                wide = lambda a: a.unsqueeze(2).broadcast_to([P, H, C])

                def one(t):
                    v.wait_ge(xt_in, t * 16 + 16)
                    mine = m.region[:, bass.ds(t * R4 * AW, R4 * AW)].rearrange("p (r w) -> p r w", w=AW)
                    selfs = m.self_w[:, bass.ds(t * R4 * H, R4 * H)].rearrange("p (r h) -> p r h", h=H)
                    link(v.tensor_tensor(den[:, :, :], mine[:, :, D:AW], selfs, op=ALU.add))
                    link(v.reciprocal(den[:, :, :], den[:, :, :]))
                    link(v.tensor_tensor(own[:, :, :], selfs, den[:, :, :], op=ALU.mult))
                    for r in range(R4):
                        link(v.tensor_tensor(by_head(z[:, r, :]), by_head(mine[:, r, 0:D]), wide(den[:, r, :]), op=ALU.mult))
                        link(v.tensor_tensor(by_head(xt[:, r, :]), by_head(xt[:, r, :]), wide(own[:, r, :]), op=ALU.mult))
                        link(v.tensor_tensor(z[:, r, :], z[:, r, :], xt[:, r, :], op=ALU.add))
                        v.tensor_tensor(z[:, r, :], z[:, r, :], bias[:, r, :], op=ALU.add).then_inc(z_ready, 1)
                    for r in range(R4):
                        v.wait_ge(pre_ready, t * R4 + r + 1)
                        link(v.tensor_tensor(pre[:, r % 2, :], m.ps[:, 2 + r % 2, 0:SEM_D], b1[:, :], op=ALU.add))
                        v.sem_inc(pre_set, 1)
                        v.wait_ge(th_set, t * R4 + r + 1)
                        link(v.tensor_tensor(junk[:, :], th[:, r % 2, :], w2[:, :], op=ALU.mult))
                        link(v.tensor_reduce(w[:, r:r + 1], junk[:, :], AX.X, ALU.add))
                    link(v.tensor_reduce(top[:, 0:1], w[:, :], AX.X, ALU.max))
                    v.tensor_scalar(beta[:, :], w[:, :], top[:, 0:1], None, ALU.subtract).then_inc(asked, 1)
                    v.wait_ge(answered, t + 1)
                    link(v.tensor_reduce(top[:, 1:2], beta[:, :], AX.X, ALU.add))
                    link(v.reciprocal(top[:, 2:3], top[:, 1:2]))
                    link(v.tensor_scalar(beta[:, :], beta[:, :], top[:, 2:3], None, ALU.mult))
                    xs = m.x[:, bass.ds(t * D, D)]
                    for r in range(R4):
                        link(v.scalar_tensor_tensor(out=xs, in0=z[:, r, :], scalar=beta[:, r:r + 1], in1=xs,
                                                    op0=ALU.mult, op1=ALU.add))
                    v.sem_inc(out_set, 1)
                ch.rounds(T, 3 + 3 * R4 + 3 * R4 + 1 + 3 + R4, one)

            @block.scalar
            def _(a):
                def one(t):
                    for r in range(R4):
                        a.wait_ge(turned, t * R4 + r + 1)
                        wait_at_least(a, pre_ready, t * R4 + r - 1)
                        a.activation(zT[:, r % 2, :], m.ps[:, r % 2, :], ACT.Copy).then_inc(zT_set, 1)
                        a.wait_ge(pre_set, t * R4 + r + 1)
                        a.activation(th[:, r % 2, :], pre[:, r % 2, :], ACT.Tanh).then_inc(th_set, 1)
                    a.wait_ge(asked, t + 1)
                    a.activation(beta[:, :], beta[:, :], ACT.Exp).then_inc(answered, 1)
                peeled(a, T, one)

            @block.tensor
            def _(pe):
                pe.wait_ge(loaded, 64)

                def one(t):
                    for r in range(R4):
                        pe.wait_ge(z_ready, t * R4 + r + 1)
                        wait_at_least(pe, zT_set, t * R4 + r - 1)
                        for k in range(KC):
                            last = pe.transpose(m.ps[:, r % 2, k * P:(k + 1) * P], z[:, r, k * P:(k + 1) * P],
                                                m.ident[:, :])
                        last.then_inc(turned, 1)
                        pe.wait_ge(zT_set, t * R4 + r + 1)
                        wait_at_least(pe, pre_set, t * R4 + r - 1)
                        for k in range(KC):
                            last = pe.matmul(m.ps[:, 2 + r % 2, 0:SEM_D], zT[:, r % 2, k * P:(k + 1) * P], w1[:, k, :],
                                             start=k == 0, stop=k == KC - 1)
                        last.then_inc(pre_ready, 1)
                peeled(pe, T, one)

            @block.gpsimd
            def _(pool):
                for t in range(T):
                    pool.wait_ge(out_set, t + 1)
                    rows = P if t < T - 1 else LAST
                    pool.dma_start(m.out[t * P:t * P + rows, :], m.x[0:rows, t * D:(t + 1) * D]).then_inc(stored, 16)
                pool.wait_ge(stored, 16 * T)


def gnn_kernel(nc, a, probe=None):
    m = Core()
    m.x_in, m.src, m.dst, m.type4 = a["x_in"], a["src"], a["dst"], a["type4"]
    m.type8, m.weight, m.w0, m.a0 = a["type8"], a["weight"], a["w0"], a["a0"]
    m.w1, m.b1, m.w3, m.att_src = a["w1"], a["b1"], a["w3"], a["att_src"]
    m.att_dst, m.bias3, m.sem_w1, m.sem_b1 = a["att_dst"], a["bias3"], a["sem_w1"], a["sem_b1"]
    m.sem_w2, m.base_wT, m.spline_wT, m.basis = a["sem_w2"], a["base_wT"], a["spline_wT"], a["basis"]
    m.comps, m.biases, m.loops, m.out = a["comps"], a["biases"], a["loops"], a["out"]
    ks = ExitStack()
    with ks:
        sb = lambda n, s, d=F32: ks.enter_context(nc.sbuf_tensor(n, s, d))
        dram = lambda n, s: nc.dram_tensor(n, s, F32, kind="Internal").ap()
        m.gate = nc.alloc_semaphore("gate")
        m.sems = []
        m.recA, m.recB = dram("recA", (P * NCA, REC)), dram("recB", (P * NCB, REC))
        m.h_table = dram("h_table", (NP, D))
        m.rel_table = dram("rel_table", (R8 * NP, D))
        m.xt_table = dram("xt_table", (R4 * NP, D))
        m.source_table = dram("source_table", (R4 * NP, H))
        m.target_table = dram("target_table", (R4 * NP, 2 * H))
        m.source_table0 = dram("source_table0", (NP, H))
        m.target_table0 = dram("target_table0", (NP, 2 * H))

        m.ps = ks.enter_context(nc.psum_tensor("ps", [P, 8, 512], F32))
        m.x = sb("x", [P, T * D])
        m.region = sb("region", [P, T * AW + (R8 + 1) * KC * D])
        m.own = sb("own", [P, T * D])
        m.rows = sb("rows", [P, G, D])
        m.ib = sb("ib", [P, G], U32)
        m.h = sb("h", [P, 2, D])
        m.stage = sb("stage", [P, 4, D])
        m.scratch = m.stage[:, :, :].rearrange("p s d -> p (s d)")
        m.hT = sb("hT", [P, 2, 2 * KC, P])
        m.ident = sb("ident", [P, P])
        m.ones = sb("ones", [P, P])
        m.lanes = sb("lanes", [P, P])
        m.zeros = sb("zeros", [P, 8])
        m.consts = sb("consts", [P, R8 + 3])
        m.const_values = [3.5 - j for j in range(R8)] + [2 * (1 / 6) ** (1 / 3), (4 / 6) ** (1 / 3), 0.0]
        m.ra = sb("ra", [P, NCA, REC])
        m.rb = sb("rb", [P, NCB, REC])
        m.ix_src, m.ix_src8, m.ix_src4, m.ix_dst4 = (sb(f"ix_{n}", [P, NCA], U32) for n in ("src", "src8", "src4", "dst4"))
        m.ix_bdst, m.ix_bsrc = (sb(f"ix_{n}", [P, NCB], U32) for n in ("bdst", "bsrc"))
        m.accA, m.tileA, m.maxA = (sb(n, [1, NCA], I32) for n in ("accA", "tileA", "maxA"))
        m.accB, m.maxB = (sb(n, [1, NCB], I32) for n in ("accB", "maxB"))
        edge = m.own
        prepare(m, nc)

        laneA = lambda c: m.ra[:, bass.ds(c, 1), A_LANE]
        laneB = lambda c: m.rb[:, bass.ds(c, 1), B_LANE]
        sums_of_ones = lambda c: m.ones[:, 0:H]
        weights_at = lambda o, n=KC * D: m.region[:, T * AW + o * KC * D:T * AW + o * KC * D + n]
        cube = lambda ap: ap.rearrange("p (k d) -> p k d", d=D)
        zero = ("set", m.region[:, 0:T * AW], 0.0)

        with ExitStack() as layer:
            sl = lambda n, s, d=F32: layer.enter_context(nc.sbuf_tensor(n, s, d))
            fold = sl("fold0", [P, KC, 2])
            st = sl("st", [P, T * 2])
            att = weights_at(1, 2 * D)
            fold_attention(m, nc, "fold0",
                           [(cube(weights_at(0)), m.w0.rearrange("(k p) d -> p k d", p=P)),
                            (att, m.a0.rearrange("d a -> a d").broadcast_to([P, 2 * D]))],
                           [(cube(weights_at(0)), att[:, j * D:(j + 1) * D], 1, fold[:, :, j:j + 1]) for j in range(2)])
            project(m, nc, "p0", "norm", h_table=m.h_table, small=(fold[:, :, :], st[:, :]))
            st3 = st[:, :].rearrange("p (t k) -> p t k", k=2)
            src8 = sl("src8", [P, T, H])
            tgt = sl("tgt0", [P, T, H])
            best = sl("best0", [P, T * H])
            tt = sl("tt0", [P, T, 2 * H])
            fill(m, nc, "f0", [("set", src8[:, :, :], 0.0), ("copy", src8[:, :, 0], st3[:, :, 1]),
                               ("set", tgt[:, :, :], 0.0), ("copy", tgt[:, :, 0], st3[:, :, 0]),
                               ("set", best[:, :], -BIG), zero,
                               ("store", m.source_table0.rearrange("(t p) h -> p t h", p=P), src8[:, :, :])])
            logits, targets = edge[:, 0:NCB * H], edge[:, NCB * H:NCB * 3 * H]
            weights = sl("ew0", [P, NCB * H])
            gather_rows(m, nc, "g0s", m.ix_bdst, NCB, m.source_table0, H, logits)
            segment_max(m, nc, "m0", NCB, NBB, laneB, logits, 1, m.maxB, best)
            attention_table(m, nc, "t0", T, tgt[:, :, :], best[:, :].rearrange("p (b h) -> p b h", h=H), tt, m.target_table0)
            gather_rows(m, nc, "g0t", m.ix_bsrc, NCB, m.target_table0, 2 * H, targets)
            edge_weights(m, nc, "e0", NCB, logits, targets, weights)
            aggregate(m, nc, "a0", NCB, NBB, m.ix_bdst, laneB, m.h_table, m.accB,
                      weight=lambda c: weights[:, bass.ds(c * H, 1)], sums=sums_of_ones)
        if probe == "agg0":
            return m
        spline_network(m, nc)
        if probe == "l0":
            return m

        recycle_semaphores(m, nc)

        project(m, nc, "p1", "norm", h_table=m.h_table)
        fill(m, nc, "f1", [zero])
        aggregate(m, nc, "a1", NCA, T, m.ix_src, laneA, m.h_table, m.tileA, sums=sums_of_ones)
        mean_layer(m, nc)
        if probe == "l1":
            return m

        recycle_semaphores(m, nc)

        with ExitStack() as layer:
            sl = lambda n, s, d=F32: layer.enter_context(nc.sbuf_tensor(n, s, d))
            m.comp = sl("comp", [P, R8 * BASES])
            m.own_bias = sl("own_bias", [P, D])
            m.loop_w = cube(weights_at(R8))
            rel = lambda r: m.rel_table[r * NP:(r + 1) * NP, :]
            for n in range(2):
                mix_bases(m, nc, f"x2{n}", m.basis[n], m.comps[n], m.loops[n], m.biases[n])
                project(m, nc, f"p2{n}", ("norm", "mid")[n],
                        tables=[(cube(weights_at(r)), rel(r)) for r in range(R8)],
                        own=(m.loop_w[:, :, :], m.own_bias[:, :], m.own))
                fill(m, nc, f"f2{n}", [zero])
                aggregate(m, nc, f"a2{n}", NCA, T, m.ix_src8, laneA, m.rel_table, m.tileA,
                          weight=lambda c: m.ra[:, bass.ds(c, 1), A_WEIGHT])
            fill(m, nc, "f22", [("add", m.x[:, :].rearrange("p (t d) -> p t d", d=D), acc_rows(m)[:, :, 0:D]),
                                ("add", m.x[:, :], m.own[:, :])])
        if probe == "l2":
            return m

        recycle_semaphores(m, nc)

        fold = sb("fold3", [P, KC, R4 * 2 * H])
        al = sb("al", [P, T * R4 * 2 * H])
        best = sb("best3", [P, NBA * H])
        m.self_w = sb("self_w", [P, NBA * H])
        tt = m.region[:, NBA * AW:NBA * (AW + 2 * H)].rearrange("p (b f) -> p b f", f=2 * H)
        al3 = al[:, :].rearrange("p (b f) -> p b f", f=2 * H)
        with ExitStack() as layer:
            sl = lambda n, s, d=F32: layer.enter_context(nc.sbuf_tensor(n, s, d))
            att = weights_at(R4, 2 * R4 * D)
            folds = []
            for r in range(R4):
                for o in range(2):
                    row = att[:, (o * R4 + r) * D:(o * R4 + r + 1) * D]
                    folds.append((cube(weights_at(r)), row, H, fold[:, :, r * 2 * H + o * H:r * 2 * H + (o + 1) * H]))
            flat = lambda ap: ap.rearrange("(a r) h c -> a (r h c)", a=1).broadcast_to([P, R4 * D])
            fold_attention(m, nc, "fold3",
                           [(cube(weights_at(r)), m.w3[r].rearrange("(k p) d -> p k d", p=P)) for r in range(R4)] +
                           [(att[:, 0:R4 * D], flat(m.att_src)), (att[:, R4 * D:2 * R4 * D], flat(m.att_dst))], folds)
            project(m, nc, "p3", "norm", tables=[(cube(weights_at(r)), m.xt_table[r * NP:(r + 1) * NP, :]) for r in range(R4)],
                    small=(fold[:, :, :], al[:, :]))
            al4 = al[:, :].rearrange("p (t r f) -> p t r f", r=R4, f=2 * H)
            fill(m, nc, "f3", [("copy", best[:, :].rearrange("p (b h) -> p b h", h=H), al3[:, :, 0:H]),
                               ("set", m.region[:, 0:NBA * AW], 0.0)] +
                 [("store", m.source_table[r * NP:(r + 1) * NP, :].rearrange("(t p) h -> p t h", p=P), al4[:, :, r, 0:H])
                  for r in range(R4)])
            logits, targets = edge[:, 0:NCA * H], edge[:, NCA * H:NCA * 3 * H]
            gather_rows(m, nc, "g3s", m.ix_src4, NCA, m.source_table, H, logits)
            segment_max(m, nc, "m3", NCA, NBA, laneA, logits, H, m.maxA, best)
            attention_table(m, nc, "t3", NBA, al3[:, :, H:2 * H], best[:, :].rearrange("p (b h) -> p b h", h=H), tt,
                            m.target_table, own=(al3[:, :, 0:H], m.self_w[:, :].rearrange("p (b h) -> p b h", h=H)))
            gather_rows(m, nc, "g3t", m.ix_dst4, NCA, m.target_table, 2 * H, targets)
            weights = m.region[:, NBA * (AW + 2 * H):NBA * (AW + 2 * H) + NCA * H]
            edge_weights(m, nc, "e3", NCA, logits, targets, weights)
            col = lambda c: weights[:, bass.ds(c * H, H)]
            aggregate(m, nc, "a3", NCA, NBA, m.ix_src4, laneA, m.xt_table, m.accA, head_weight=col, sums=col)
        fuse_relations(m, nc)
    return m


_NAMES = dict(x="x_in", src="src", dst="dst", edge_type_4="type4", edge_type_8="type8", edge_weight="weight",
              L0_gnn_W="w0", L0_gnn_a="a0", L1_gnn_W="w1", L1_gnn_b="b1", L3_gnn_W="w3",
              L3_gnn_att_src="att_src", L3_gnn_att_dst="att_dst", L3_gnn_bias="bias3", L3_gnn_sem_W1="sem_w1",
              L3_gnn_sem_b1="sem_b1", L3_gnn_sem_W2="sem_w2",
              L2_gnn_basis0="basis0", L2_gnn_comp0="comp0", L2_gnn_bias0="bias0", L2_gnn_loop0="loop0",
              L2_gnn_basis1="basis1", L2_gnn_comp1="comp1", L2_gnn_bias1="bias1", L2_gnn_loop1="loop1")


def lay_out(inputs):
    import numpy as np
    arrays = {mine: np.ascontiguousarray(inputs[name]) for name, mine in _NAMES.items()}
    arrays["base_wT"] = np.ascontiguousarray(np.transpose(np.asarray(inputs["L0_gnn_base_w"])))
    arrays["spline_wT"] = np.ascontiguousarray(np.transpose(np.asarray(inputs["L0_gnn_spline_w"]), (2, 1, 0)))
    return arrays


def program(nc, arrays, **how):
    a = {n: nc.dram_tensor(f"in_{n}", v.shape, mybir.dt.from_np(v.dtype), kind="ExternalInput").ap()
         for n, v in arrays.items()}
    a["out"] = nc.dram_tensor("out_dram", (N, D), F32, kind="ExternalOutput").ap()
    for one, both in (("basis", "basis"), ("comp", "comps"), ("bias", "biases"), ("loop", "loops")):
        a[both] = (a[one + "0"], a[one + "1"])
    return gnn_kernel(nc, a, **how)


def kernel(**inputs):
    import concourse.bacc as _bacc
    from concourse.bass_utils import run_bass_kernel_spmd as _run

    arrays = lay_out(inputs)
    nc = _bacc.Bacc("TRN2", target_bir_lowering=False, num_devices=1)
    program(nc, arrays)
    r = _run(nc, [{f"in_{n}": v for n, v in arrays.items()}], core_ids=[0])
    return r.results[0]["out_dram"]
```

```python
from contextlib import ExitStack

import concourse.bass as bass
from concourse import mybir

F32 = mybir.dt.float32
I32 = mybir.dt.int32
U32 = mybir.dt.uint32
ALU = mybir.AluOpType
ACT = mybir.ActivationFunctionType
AX = mybir.AxisListType

P = 128
N = 1250
D = 512
KC = D // P
T = -(-N // P)
NP = T * P
LAST = N - (T - 1) * P
E = 21250
EP, EC = 125, 170
R4, R8, BASES = 4, 8, 4
H, C = 8, 64
SEM_D = 256
NBA, NBB = T * R4, T
G = 8
PSLOTS = 4
def chunks(buckets):
    return -(-((E + buckets * (P - 1)) // P) // G) * G
NCA, NCB = chunks(NBA), chunks(NBB)
AW = D + H
REC = 8
BIG = 1.0e30
EPS = 1e-5
F = 4
SC = 10
assert EP * EC == E and EC % SC == 0

A_LANE, A_SRC, A_SRC8, A_SRC4, A_WEIGHT = range(5)
B_LANE, B_DST = range(2)


def wait_at_least(eng, sem, value):
    if not (isinstance(value, int) and value <= 0):
        eng.wait_ge(sem, value)


def peeled(eng, n, body):
    body(0)
    if n > 2:
        with eng.Fori(1, n - 1) as i:
            body(i)
    body(n - 1)


class Core:
    pass


def semaphore(m, nc, name):
    m.sems.append(nc.alloc_semaphore(name))
    return m.sems[-1]


def recycle_semaphores(m, nc):
    nc.clear_and_free_semaphores(m.sems)
    m.sems = []
    nc.all_engine_barrier()


class Chain:

    def __init__(self, eng, sem):
        self.eng, self.sem, self.base, self.k = eng, sem, 0, 0

    def link(self, ins):
        self.k += 1
        ins.then_inc(self.sem, 1)
        self.eng.wait_ge(self.sem, self.base + self.k)

    def rounds(self, n, per, body, loop=peeled):
        start = self.base + self.k

        def one(i):
            self.base, self.k = start + i * per, 0
            body(i)
            assert self.k == per, (self.k, per)

        loop(self.eng, n, one)
        self.base, self.k = start + n * per, 0


def alone(eng, m):
    eng.sem_inc(m.gate, 1)


def offsets(nc, engine, places, c, n, last):
    _, values = nc.values_load_multi_w_load_instructions(
        places[0:1, bass.ds(c, n)], engines=(engine,), min_val=0, max_val=last,
        skip_runtime_bounds_check_because="the places are worked out from bucket numbers, which are bounded")
    return values


class Scatter:

    def __init__(self, m, nc, name, table):
        sem = lambda n: semaphore(m, nc, f"{name}_{n}")
        self.m, self.table = m, table
        self.copied, self.scattered, self.sorted_in = sem("copied"), sem("scattered"), sem("sorted_in")

    def run(self, pool, pos, rec):
        m = self.m
        with pool.Fori(0, EC // SC) as i:
            pool.tensor_copy(m.pos_blk[:, :], pos[:, bass.ds(i * SC, SC)]).then_inc(self.copied, 1)
            pool.tensor_copy(m.rec_blk[:, :, :], rec[:, bass.ds(i * SC, SC), :]).then_inc(self.copied, 1)
            pool.wait_ge(self.copied, 2 * i + 2)
            alone(pool, m)
            for j in range(SC):
                pool.indirect_dma_start(
                    out=self.table, out_offset=bass.IndirectOffsetOnAxis(ap=m.pos_blk[:, j:j + 1], axis=0),
                    in_=m.rec_blk[:, j, :], in_offset=None).then_inc(self.scattered, 16)
            pool.wait_ge(self.scattered, (i + 1) * (16 * SC))
            alone(pool, m)

    def load(self, sp, dst):
        sp.wait_ge(self.scattered, 16 * EC)
        sp.dma_start(dst[:, :, :], self.table.rearrange("(p c) f -> p c f", p=P)).then_inc(self.sorted_in, 16)
        sp.wait_ge(self.sorted_in, 16)


def prepare(m, nc):
    ks = ExitStack()
    with ks:
        sb = lambda n, s, d=F32: ks.enter_context(nc.sbuf_tensor(n, s, d))
        sem = lambda n: semaphore(m, nc, n)
        spare = m.hT[0:EP, 0, :, :].rearrange("p k n -> p (k n)").bitcast(I32)
        ints = spare[:, 0:4 * EC].rearrange("p (f c) -> p f c", f=4)
        tmp_i = spare[:, 4 * EC:6 * EC].rearrange("p (f c) -> p f c", f=2)
        w_in = sb("edge_weight", [EP, EC])
        key = sb("edge_key", [EP, 2, EC])
        pos = sb("edge_pos", [EP, 2, EC])
        recs, posus = (m.rec_inA, m.rec_inB), (m.posA, m.posB)
        iota_b = sb("iota_b", [P, NBA])
        iota_c = sb("iota_c", [1, NCA])
        tri = sb("tri", [P, P])
        row_end = sb("row_end", [EP, NBA])
        row_tot = sb("row_tot", [EP, NBA])
        nchunk = sb("nchunk", [P, NBA])
        nchunk_i = sb("nchunk_i", [P, NBA], I32)
        end_chunk = sb("end_chunk", [P, NBA])
        off = sb("off", [EP, NBA])
        cnt = sb("cnt", [1, NCA])
        cnt_i = sb("cnt_i", [1, NCA], I32)
        blank = m.own[:, 0:NCA * REC].rearrange("p (c f) -> p c f", f=REC)
        x_in, loaded, made, counted, placed = sem("x_in"), sem("loaded"), sem("made"), sem("counted"), sem("placed")
        totals, blanked, blank_set = sem("totals"), sem("blanked"), sem("blank_set")
        dve = sem("dve_prepare")
        ind = m.region[0:EP, 0:NBA * EC]
        cum = m.region[0:EP, NBA * EC:2 * NBA * EC]
        mapw = m.region[0:1, 0:NCA * NBA]

        with nc.Block() as block:

            @block.sync
            def _(sp):
                for f, a in enumerate((m.src, m.dst, m.type4, m.type8)):
                    sp.dma_start(ints[:, f, :], a.rearrange("(p c) -> p c", p=EP)).then_inc(loaded, 16)
                sp.dma_start(w_in[:, :], m.weight.rearrange("(p c) -> p c", p=EP)).then_inc(loaded, 16)
                full = m.x_in[0:(T - 1) * P, :].rearrange("(t p) d -> p t d", p=P)
                sp.wait_ge(made, 1)
                sp.dma_start(m.x[:, 0:(T - 1) * D].rearrange("p (t d) -> p t d", d=D), full).then_inc(x_in, 16)
                sp.dma_start(m.x[0:LAST, (T - 1) * D:T * D], m.x_in[(T - 1) * P:N, :]).then_inc(x_in, 16)
                sp.wait_ge(blank_set, 1)
                sp.dma_start(m.recA.rearrange("(p c) f -> p c f", p=P), blank[:, :, :]).then_inc(blanked, 16)
                sp.dma_start(m.recB.rearrange("(p c) f -> p c f", p=P), blank[:, 0:NCB, :]).then_inc(blanked, 16)
                sp.wait_ge(x_in, 32)

            @block.gpsimd
            def _(pool):
                pool.memset(m.x[:, (T - 1) * D:T * D], 0.0).then_inc(made, 1)
                pool.iota(iota_b[:, :], [[1, NBA]], base=0, channel_multiplier=0,
                          allow_small_or_imprecise_dtypes=True).then_inc(made, 1)
                pool.iota(iota_c[:, :], [[1, NCA]], base=0, channel_multiplier=0,
                          allow_small_or_imprecise_dtypes=True).then_inc(made, 1)
                pool.iota(m.lanes[:, :], [[1, P]], base=0, channel_multiplier=0,
                          allow_small_or_imprecise_dtypes=True).then_inc(made, 1)
                pool.memset(m.ones[:, :], 1.0).then_inc(made, 1)
                pool.memset(m.ident[:, :], 0.0).then_inc(made, 1)
                pool.wait_ge(made, 6)
                pool.affine_select(out=m.ident[:, :], in_=m.ident[:, :], compare_op=ALU.not_equal, fill=1.0,
                                   base=0, pattern=[[-1, P]], channel_multiplier=1).then_inc(made, 1)
                pool.affine_select(out=tri[:, :], in_=m.ones[:, :], compare_op=ALU.is_gt, fill=0.0,
                                   base=0, pattern=[[1, P]], channel_multiplier=-1).then_inc(made, 1)
                pool.wait_ge(blanked, 32)

            @block.tensor
            def _(pe):
                pe.wait_ge(made, 8)
                for turn, (o, nb) in enumerate(((1, NBB), (0, NBA))):
                    pe.wait_ge(totals, turn + 1)
                    pe.matmul(m.ps[0:EP, 2 * o, 0:nb], tri[0:EP, 0:EP], row_tot[:, 0:nb], start=True, stop=True)
                    pe.matmul(m.ps[:, 2 * o + 1, 0:nb], m.ones[0:EP, :], row_tot[:, 0:nb],
                              start=True, stop=True).then_inc(counted, 1)

            @block.vector
            def _(v):
                ch = Chain(v, dve)
                link = ch.link
                link(v.memset(blank[:, :, :], 0.0))
                v.memset(blank[:, :, 0:1], -1.0).then_inc(blank_set, 1)
                for j in range(R8 + 3):
                    last = v.memset(m.consts[:, j:j + 1], m.const_values[j])
                link(last)
                link(v.memset(m.zeros[:, :], 0.0))
                link(v.memset(recs[0][:, :, :], 0.0))
                v.wait_ge(loaded, 16 * 5)
                v.wait_ge(made, 8)
                link(v.tensor_copy(recs[0][:, :, A_WEIGHT], w_in[:, :]))
                link(v.memset(recs[1][:, :, :], 0.0))
                src, dst, ty4, ty8 = (ints[:, f, :] for f in range(4))
                link(v.tensor_scalar(tmp_i[:, 0, :], dst, 7, None, ALU.arith_shift_right))
                link(v.scalar_tensor_tensor(out=key[:, 0, :], in0=tmp_i[:, 0, :], scalar=float(R4), in1=ty4,
                                            op0=ALU.mult, op1=ALU.add))
                link(v.tensor_scalar(tmp_i[:, 1, :], src, 7, None, ALU.arith_shift_right))
                link(v.tensor_copy(key[:, 1, :], tmp_i[:, 1, :]))
                link(v.tensor_scalar(tmp_i[:, 0, :], dst, 127, None, ALU.bitwise_and))
                link(v.tensor_scalar(tmp_i[:, 1, :], src, 127, None, ALU.bitwise_and))
                link(v.tensor_copy(recs[0][:, :, A_LANE], tmp_i[:, 0, :]))
                link(v.tensor_copy(recs[1][:, :, B_LANE], tmp_i[:, 1, :]))
                link(v.tensor_copy(recs[0][:, :, A_SRC], src))
                link(v.tensor_copy(recs[1][:, :, B_DST], dst))
                link(v.scalar_tensor_tensor(out=recs[0][:, :, A_SRC8], in0=ty8, scalar=float(NP), in1=src,
                                            op0=ALU.mult, op1=ALU.add))
                link(v.scalar_tensor_tensor(out=recs[0][:, :, A_SRC4], in0=ty4, scalar=float(NP), in1=src,
                                            op0=ALU.mult, op1=ALU.add))
                for turn, (o, nb, nch) in enumerate(((1, NBB, NCB), (0, NBA, NCA))):
                    cube = lambda a: a[:, 0:nb * EC].rearrange("p (b c) -> p b c", b=nb)
                    mine = iota_b[0:EP, 0:nb]
                    link(v.tensor_tensor(cube(ind), key[:, o, :].unsqueeze(1).broadcast_to([EP, nb, EC]),
                                         mine.unsqueeze(2).broadcast_to([EP, nb, EC]), op=ALU.is_equal))
                    link(v.tensor_tensor_scan(cum[:, 0:nb * EC], ind[:, 0:nb * EC],
                                              m.zeros[0:EP, 0:1].broadcast_to([EP, nb * EC]), 0.0,
                                              ALU.add, ALU.add))
                    link(v.tensor_copy(row_end[:, 0:nb], cube(cum)[:, :, EC - 1]))
                    link(v.tensor_copy(row_tot[:, 0:1], row_end[:, 0:1]))
                    v.tensor_tensor(row_tot[:, 1:nb], row_end[:, 1:nb], row_end[:, 0:nb - 1],
                                    op=ALU.subtract).then_inc(totals, 1)
                    v.wait_ge(counted, turn + 1)
                    link(v.tensor_scalar(nchunk[:, 0:nb], m.ps[:, 2 * o + 1, 0:nb], 127.0, None, ALU.add))
                    link(v.tensor_copy(nchunk_i[:, 0:nb], nchunk[:, 0:nb]))
                    link(v.tensor_scalar(nchunk_i[:, 0:nb], nchunk_i[:, 0:nb], 7, None, ALU.arith_shift_right))
                    link(v.tensor_copy(nchunk[:, 0:nb], nchunk_i[:, 0:nb]))
                    link(v.tensor_tensor_scan(end_chunk[:, 0:nb], nchunk[:, 0:nb],
                                              m.zeros[:, 0:1].broadcast_to([P, nb]), 0.0, ALU.add, ALU.add))
                    link(v.tensor_tensor(nchunk[:, 0:nb], end_chunk[:, 0:nb], nchunk[:, 0:nb], op=ALU.subtract))
                    link(v.tensor_scalar(off[:, 0:nb], nchunk[0:EP, 0:nb], float(P), -1.0, ALU.mult, ALU.add))
                    link(v.tensor_tensor(off[:, 0:nb], off[:, 0:nb], m.ps[0:EP, 2 * o, 0:nb], op=ALU.add))
                    link(v.tensor_tensor(off[:, 1:nb], off[:, 1:nb], row_end[:, 0:nb - 1], op=ALU.subtract))
                    link(v.tensor_tensor(cube(cum), cube(cum), off[:, 0:nb].unsqueeze(2).broadcast_to([EP, nb, EC]),
                                         op=ALU.add))
                    link(v.tensor_tensor(cube(cum), cube(cum), cube(ind), op=ALU.mult))
                    link(v.tensor_reduce(pos[:, o, :], cube(cum).rearrange("p b c -> p c b"), AX.X, ALU.add))
                    link(v.tensor_copy(tmp_i[:, 0, :], pos[:, o, :]))
                    link(v.tensor_scalar(tmp_i[:, 1, :], tmp_i[:, 0, :], 127, None, ALU.bitwise_and))
                    link(v.tensor_scalar(tmp_i[:, 0, :], tmp_i[:, 0, :], 7, None, ALU.arith_shift_right))
                    link(v.scalar_tensor_tensor(out=posus[o][:, :], in0=tmp_i[:, 1, :], scalar=float(nch),
                                                in1=tmp_i[:, 0, :], op0=ALU.mult, op1=ALU.add))
                    grid = mapw[:, 0:nch * nb].rearrange("p (c b) -> p c b", b=nb)
                    link(v.tensor_tensor(grid, end_chunk[0:1, 0:nb].unsqueeze(1).broadcast_to([1, nch, nb]),
                                         iota_c[:, 0:nch].unsqueeze(2).broadcast_to([1, nch, nb]), op=ALU.is_le))
                    link(v.tensor_reduce(cnt[:, 0:nch], grid, AX.X, ALU.add))
                    link(v.tensor_scalar(cnt[:, 0:nch], cnt[:, 0:nch], float(nb - 1), None, ALU.min))
                    if o == 0:
                        link(v.tensor_scalar(m.accA[:, :], cnt[:, 0:nch], float(AW), None, ALU.mult))
                        link(v.tensor_scalar(m.maxA[:, :], cnt[:, 0:nch], float(H), None, ALU.mult))
                        link(v.tensor_copy(cnt_i[:, :], cnt[:, 0:nch]))
                        link(v.tensor_scalar(cnt_i[:, :], cnt_i[:, :], 2, None, ALU.arith_shift_right))
                        link(v.tensor_scalar(m.tileA[:, :], cnt_i[:, :], float(AW), None, ALU.mult))
                    else:
                        link(v.tensor_scalar(m.accB[:, :], cnt[:, 0:nch], float(AW), None, ALU.mult))
                        link(v.tensor_scalar(m.maxB[:, :], cnt[:, 0:nch], float(H), None, ALU.mult))


def normalise_setup(m, v, ch, stats, mv, rstd, nbias, root_asked, root_done):
    def one(t):
        ch.link(v.bn_stats(stats[:, bass.ds(t * 6, 6)], m.x[:, bass.ds(t * D, D)]))
    ch.rounds(T, 1, one)
    for t in range(T):
        last = v.bn_aggr(mv[:, 2 * t:2 * t + 2], stats[:, 6 * t:6 * t + 6])
    ch.link(last)
    both = mv[:, :].rearrange("p (t k) -> p t k", k=2)
    v.tensor_scalar(rstd[:, :], both[:, :, 1], EPS, None, ALU.add).then_inc(root_asked, 1)
    v.wait_ge(root_done, 1)
    ch.link(v.reciprocal(rstd[:, :], rstd[:, :]))
    ch.link(v.scalar_tensor_tensor(out=nbias[:, :], in0=both[:, :, 0], scalar=-1.0, in1=rstd[:, :],
                                   op0=ALU.mult, op1=ALU.mult))


def project(m, nc, name, h_table=None, tables=(), small=None, beside=None):
    n_tab = len(tables)
    outs = [("table", w, d) for w, d in tables]
    if small:
        outs.append(("small", *small))
    Q = 2 * len(outs)
    BANKS = 6
    engine = ["v" if outs[q % len(outs)][0] != "table" or q % 2 else "a" for q in range(Q)] if outs else []
    rank = [engine[:q].count(engine[q]) for q in range(Q)]
    per_round = {e: engine.count(e) for e in "va"}
    QT = 2 * n_tab
    SLOTS = 4

    def before(q, count, lanes):
        if q >= lanes:
            return 0, q - lanes
        return 1, max((z for z in range(count) if z % lanes == q), default=q)

    ks = ExitStack()
    with ks:
        sb = lambda n, s, d=F32: ks.enter_context(nc.sbuf_tensor(f"{name}_{n}", s, d))
        sem = lambda n: semaphore(m, nc, f"{name}_{n}")
        stats = sb("stats", [P, T * 6])
        mv = sb("mv", [P, T * 2])
        rstd = sb("rstd", [P, T])
        nbias = sb("nbias", [P, T])
        root_asked, root_done, norm_set = sem("root_asked"), sem("root_done"), sem("norm_set")
        h_ready, turned, h_turned, multiplied = sem("h_ready"), sem("turned"), sem("h_turned"), sem("multiplied")
        left = {"v": sem("left_v"), "a": sem("left_a")}
        stored = [sem(f"stored{s}") for s in range(SLOTS)]
        h_stored = [sem(f"h_stored{s}") for s in range(2)]
        dve = sem("dve")

        def tile(i, b):
            return i * 2 + b

        def leave(eng, who, i, b):
            for o, out in enumerate(outs):
                q = b * len(outs) + o
                if engine[q] != who:
                    continue
                eng.wait_ge(multiplied, i * Q + q + 1)
                bank = m.ps[:, 2 + q % BANKS, :]
                kind = out[0]
                if kind == "table":
                    qt = b * n_tab + o
                    wait_at_least(eng, stored[qt % SLOTS], (i * (QT // SLOTS) + qt // SLOTS) * 16)
                    if not isinstance(i, int):
                        alone(eng, m)
                    dst = m.stage[:, qt % SLOTS, :]
                    ins = eng.tensor_copy(dst, bank) if who == "v" else eng.activation(dst, bank, ACT.Copy)
                else:
                    if not isinstance(i, int):
                        alone(eng, m)
                    w = out[1].shape[2]
                    ins = eng.tensor_copy(out[2][:, bass.ds(tile(i, b) * w, w)], bank[:, 0:w])
                ins.then_inc(left[who], 1)

        with nc.Block() as block:

            @block.vector
            def _(v):
                ch = Chain(v, dve)
                normalise_setup(m, v, ch, stats, mv, rstd, nbias, root_asked, root_done)
                v.sem_inc(norm_set, 1)

                def copy_hT(t, b):
                    v.wait_ge(turned, t + 1)
                    wait_at_least(v, multiplied, (t - 1) * len(outs))
                    v.tensor_copy(m.hT[:, b, 0:KC, :].rearrange("p k n -> p (k n)"), m.ps[:, b, :])\
                     .then_inc(h_turned, 1)

                def pair(i):
                    for b in range(2):
                        t = tile(i, b)
                        if not (isinstance(t, int) and t == T - 1):
                            copy_hT(t + 1, 1 - b)
                        leave(v, "v", i, b)
                if outs:
                    copy_hT(0, 0)
                    peeled(v, T // 2, pair)

            @block.scalar
            def _(a):
                a.wait_ge(root_asked, 1)
                a.activation(rstd[:, :], rstd[:, :], ACT.Sqrt).then_inc(root_done, 1)
                a.wait_ge(norm_set, 1)

                def rows(t, i, b):
                    if outs:
                        wait_at_least(a, turned, t - 1)
                    if h_table is not None:
                        wait_at_least(a, h_stored[b], i * 16)
                    if not isinstance(i, int):
                        alone(a, m)
                    a.activation(m.h[:, b, :], m.x[:, bass.ds(t * D, D)], ACT.Relu,
                                 bias=nbias[:, bass.ds(t, 1)], scale=rstd[:, bass.ds(t, 1)]).then_inc(h_ready, 1)

                def pair(i):
                    for b in range(2):
                        t = tile(i, b)
                        if not (isinstance(t, int) and t == T - 1):
                            rows(t + 1, i + b, 1 - b)
                        leave(a, "a", i, b)
                rows(0, 0, 0)
                peeled(a, T // 2, pair)

            @block.tensor
            def _(pe):
                def turn(t, b):
                    pe.wait_ge(h_ready, t + 1)
                    wait_at_least(pe, h_turned, t - 1)
                    for k in range(KC):
                        last = pe.transpose(m.ps[:, b, k * P:(k + 1) * P], m.h[:, b, k * P:(k + 1) * P], m.ident[:, :])
                    last.then_inc(turned, 1)

                def pair(i):
                    for b in range(2):
                        t = tile(i, b)
                        if not (isinstance(t, int) and t == T - 1):
                            turn(t + 1, 1 - b)
                        pe.wait_ge(h_turned, t + 1)
                        for o, out in enumerate(outs):
                            q = b * len(outs) + o
                            back, z = before(q, Q, BANKS)
                            if not (isinstance(i, int) and i < back):
                                e = engine[z]
                                pe.wait_ge(left[e], (i - back) * per_round[e] + rank[z] + 1)
                            w = out[1]
                            for k in range(KC):
                                last = pe.matmul(m.ps[:, 2 + q % BANKS, 0:w.shape[2]], m.hT[:, b, k, :],
                                                 w[:, k, :], start=k == 0, stop=k == KC - 1)
                            last.then_inc(multiplied, 1)
                if outs:
                    turn(0, 0)
                    peeled(pe, T // 2, pair)

            @block.sync
            def _(sp):
                def pair(i):
                    for b in range(2):
                        t = tile(i, b)
                        if h_table is not None:
                            sp.wait_ge(h_ready, t + 1)
                            sp.dma_start(h_table[bass.ds(t * P, P), :], m.h[:, b, :]).then_inc(h_stored[b], 16)
                        for o in range(n_tab):
                            q, qt = b * len(outs) + o, b * n_tab + o
                            e = engine[q]
                            sp.wait_ge(left[e], i * per_round[e] + rank[q] + 1)
                            sp.dma_start(outs[o][2][bass.ds(t * P, P), :], m.stage[:, qt % SLOTS, :])\
                              .then_inc(stored[qt % SLOTS], 16)
                if h_table is not None or n_tab:
                    peeled(sp, T // 2, pair)
                if h_table is not None:
                    for s in h_stored:
                        sp.wait_ge(s, 16 * (T // 2))
                if n_tab:
                    for s in stored:
                        sp.wait_ge(s, 16 * (T // 2) * (QT // SLOTS))
                if beside:
                    beside[0].load(sp, beside[3])

            if beside:
                @block.gpsimd
                def _(pool):
                    scatter, pos, rec, _ = beside
                    scatter.run(pool, pos, rec)


def target_values(m, nc, name, n_chunks, buckets, records, places, table, out):
    W2 = 2 * H
    ks = ExitStack()
    with ks:
        sb = lambda n, s, d=F32: ks.enter_context(nc.sbuf_tensor(f"{name}_{n}", s, d))
        sem = lambda n: semaphore(m, nc, f"{name}_{n}")
        onehot = m.stage[:, 0:2, :]
        flipped = m.stage[:, 2:4, :]
        hot, turned, copied, valued, taken = (sem(n) for n in ("hot", "turned", "copied", "valued", "taken"))
        rounds = n_chunks // (2 * F)
        flat = table.rearrange("p b f -> p (b f)")

        with nc.Block() as block:

            @block.vector
            def _(v):
                def heat(q, u):
                    v.tensor_tensor(onehot[:, u, :].rearrange("p (f n) -> p f n", f=F),
                                    m.lanes[:, :].unsqueeze(1).broadcast_to([P, F, P]),
                                    records[:, bass.ds(q * F, F), A_LANE:A_LANE + 1].broadcast_to([P, F, P]),
                                    op=ALU.is_equal).then_inc(hot, 1)
                heat(0, 0)
                heat(1, 1)

                def body(i):
                    for u in range(2):
                        q = 2 * i + u
                        if not (isinstance(q, int) and q + 2 >= 2 * rounds):
                            v.wait_ge(turned, q + 1)
                            heat(q + 2, u)
                        v.wait_ge(valued, q + 1)
                        alone(v, m)
                        v.tensor_copy(out[:, bass.ds(q * (F * W2), F * W2)], m.ps[:, 2 + u, 0:F * W2]).then_inc(taken, 1)
                peeled(v, rounds, body)

            @block.scalar
            def _(a):
                def body(i):
                    for u in range(2):
                        q = 2 * i + u
                        a.wait_ge(turned, q + 1)
                        wait_at_least(a, valued, q - 1)
                        a.activation(flipped[:, u, :], m.ps[:, u, :], ACT.Copy).then_inc(copied, 1)
                peeled(a, rounds, body)

            @block.tensor
            def _(pe):
                def turn(q, u):
                    pe.wait_ge(hot, q + 1)
                    wait_at_least(pe, copied, q - 1)
                    for f in range(F):
                        last = pe.transpose(m.ps[:, u, f * P:(f + 1) * P], onehot[:, u, f * P:(f + 1) * P],
                                            m.ident[:, :])
                    last.then_inc(turned, 1)

                turn(0, 0)

                def body(i):
                    for u in range(2):
                        q = 2 * i + u
                        if not (isinstance(q, int) and q + 1 >= 2 * rounds):
                            turn(q + 1, 1 - u)
                        at = offsets(nc, mybir.EngineType.PE, places, q * F, F, (buckets - 1) * H)
                        pe.wait_ge(copied, q + 1)
                        wait_at_least(pe, taken, q - 1)
                        for f in range(F):
                            last = pe.matmul(m.ps[:, 2 + u, f * W2:(f + 1) * W2], flipped[:, u, f * P:(f + 1) * P],
                                             flat[:, bass.ds(at[f] * 2, W2)], start=True, stop=True)
                        last.then_inc(valued, 1)
                peeled(pe, rounds, body)


class Gather:

    def __init__(self, m, nc, name, index, table, ring, width):
        self.m, self.index, self.table, self.ring, self.width = m, index, table, ring, width
        self.indexed = semaphore(m, nc, f"{name}_indexed")
        self.fetched = [semaphore(m, nc, f"{name}_fetched{g}") for g in range(G)]

    def feed(self, a, c, g):
        a.copy(self.m.ib[:, g:g + 1], self.index[:, bass.ds(c, 1)]).then_inc(self.indexed, 1)

    def fetch(self, pool, c, g):
        pool.wait_ge(self.indexed, c + 1)
        alone(pool, self.m)
        pool.indirect_dma_start(out=self.ring[:, g, 0:self.width], out_offset=None, in_=self.table,
                                in_offset=bass.IndirectOffsetOnAxis(ap=self.m.ib[:, g:g + 1], axis=0))\
            .then_inc(self.fetched[g], 16)


def segment_max_one(m, nc, name, n_chunks, buckets, records, index, table, logits, places, best):
    ks = ExitStack()
    with ks:
        sb = lambda n, s, d=F32: ks.enter_context(nc.sbuf_tensor(f"{name}_{n}", s, d))
        sem = lambda n: semaphore(m, nc, f"{name}_{n}")
        other = m.stage[:, 0:2, :]
        marked = m.stage[:, 2:4, :]
        ring = sb("ring", [P, G, H])
        chunk_best = sb("chunk_best", [P, F])
        compared, filled, turned, reduced, kept, dve = (
            sem(n) for n in ("compared", "filled", "turned", "reduced", "kept", "dve"))
        rows = Gather(m, nc, name, index, table, ring, H)
        rounds = n_chunks // G

        with nc.Block() as block:

            @block.gpsimd
            def _(pool):
                with pool.Fori(0, rounds) as i:
                    for g in range(G):
                        rows.fetch(pool, i * G + g, g)

            @block.scalar
            def _(a):
                for g in range(G):
                    rows.feed(a, g, g)

                def body(i):
                    for u in range(2):
                        q = 2 * i + u
                        for f in range(F):
                            a.wait_ge(rows.fetched[F * u + f], 16 * i + 16)
                        alone(a, m)
                        a.activation(logits[:, bass.ds(q * (F * H), F * H)],
                                     ring[:, F * u:F * (u + 1), :].rearrange("p f h -> p (f h)"), ACT.Copy).then_inc(kept, 1)
                        a.wait_ge(filled, q + 1)
                        a.wait_ge(kept, q + 1)
                        alone(a, m)
                        if not (isinstance(q, int) and q + 2 >= 2 * rounds):
                            for f in range(F):
                                rows.feed(a, (q + 2) * F + f, F * u + f)
                peeled(a, rounds, body)

            @block.vector
            def _(v):
                ch = Chain(v, dve)

                def mark(q, i, u):
                    for f in range(F):
                        v.wait_ge(rows.fetched[F * u + f], 16 * i + 16)
                    wide = lambda t: t[:, u, :].rearrange("p (f n) -> p f n", f=F)
                    v.tensor_tensor(wide(other), m.lanes[:, :].unsqueeze(1).broadcast_to([P, F, P]),
                                    records[:, bass.ds(q * F, F), A_LANE:A_LANE + 1].broadcast_to([P, F, P]),
                                    op=ALU.not_equal).then_inc(compared, 1)
                    v.wait_ge(compared, q + 1)
                    v.scalar_tensor_tensor(out=wide(marked), in0=wide(other), scalar=-BIG,
                                           in1=ring[:, F * u:F * (u + 1), 0:1].broadcast_to([P, F, P]),
                                           op0=ALU.mult, op1=ALU.add).then_inc(filled, 1)

                mark(0, 0, 0)
                mark(1, 0, 1)

                def body(i):
                    for u in range(2):
                        q = 2 * i + u
                        v.wait_ge(turned, q + 1)
                        v.tensor_reduce(chunk_best[:, :], m.ps[:, u, :].rearrange("p (f e) -> p f e", f=F),
                                        AX.X, ALU.max).then_inc(reduced, 1)
                        at = offsets(nc, mybir.EngineType.DVE, places, q * F, F, (buckets - 1) * H)
                        v.wait_ge(reduced, q + 1)
                        for f in range(F):
                            b = best[:, bass.ds(at[f], 1)]
                            ch.link(v.tensor_tensor(b, b, chunk_best[:, f:f + 1], op=ALU.max))
                        if not (isinstance(q, int) and q + 2 >= 2 * rounds):
                            mark(q + 2, i + 1, u)
                ch.rounds(rounds, 2 * F, body)

            @block.tensor
            def _(pe):
                def body(i):
                    for u in range(2):
                        q = 2 * i + u
                        pe.wait_ge(filled, q + 1)
                        wait_at_least(pe, reduced, q - 1)
                        for f in range(F):
                            last = pe.transpose(m.ps[:, u, f * P:(f + 1) * P], marked[:, u, f * P:(f + 1) * P],
                                                m.ident[:, :])
                        last.then_inc(turned, 1)
                peeled(pe, rounds, body)


def segment_max(m, nc, name, n_chunks, buckets, lane, index, table, logits, places, best):
    ON_ACT, ON_POOL = 5, 2
    AHEAD, LAG = 4, 3
    ks = ExitStack()
    with ks:
        sb = lambda n, s, d=F32: ks.enter_context(nc.sbuf_tensor(f"{name}_{n}", s, d))
        sem = lambda n: semaphore(m, nc, f"{name}_{n}")
        masks = sb("masks", [P, PSLOTS, P])
        marked = m.rows[:, :, :].rearrange("p g d -> p (g d)").rearrange("p (s w) -> p s w", s=PSLOTS)
        ring = sb("ring", [P, G, H])
        chunk_best = sb("chunk_best", [P, H])
        masked, kept, turned, reduced, dve = (sem(n) for n in ("masked", "kept", "turned", "reduced", "dve"))
        filled_a, filled_p, filled_v = (sem(f"filled_{n}") for n in "apv")
        rows = Gather(m, nc, name, index, table, ring, H)
        rounds = n_chunks // G
        heads_of = lambda s, lo, hi: marked[:, s, lo * P:hi * P]

        with nc.Block() as block:

            @block.gpsimd
            def _(pool):
                for c in range(AHEAD):
                    rows.fetch(pool, c, c % G)

                def body(i):
                    for g in range(G):
                        c, s = i * G + g, g % PSLOTS
                        if not (isinstance(c, int) and c + AHEAD >= n_chunks):
                            rows.fetch(pool, c + AHEAD, (g + AHEAD) % G)
                        pool.wait_ge(rows.fetched[g], 16 * i + 16)
                        wait_at_least(pool, turned, c + 1 - PSLOTS)
                        pool.wait_ge(masked, c + 1)
                        pool.tensor_tensor(
                            heads_of(s, ON_ACT, ON_ACT + ON_POOL).rearrange("p (h n) -> p h n", h=ON_POOL),
                            masks[:, s, :].unsqueeze(1).broadcast_to([P, ON_POOL, P]),
                            ring[:, g, ON_ACT:ON_ACT + ON_POOL].unsqueeze(2).broadcast_to([P, ON_POOL, P]),
                            op=ALU.add).then_inc(filled_p, 1)
                peeled(pool, rounds, body)

            @block.scalar
            def _(a):
                for g in range(G):
                    rows.feed(a, g, g)

                def body(i):
                    for g in range(G):
                        c, s = i * G + g, g % PSLOTS
                        a.wait_ge(rows.fetched[g], 16 * i + 16)
                        wait_at_least(a, turned, c + 1 - PSLOTS)
                        a.wait_ge(masked, c + 1)
                        for h in range(ON_ACT):
                            last = a.activation(heads_of(s, h, h + 1), masks[:, s, :], ACT.Identity,
                                                bias=ring[:, g, h:h + 1])
                        last.then_inc(filled_a, 1)
                        a.copy(logits[:, bass.ds(c * H, H)], ring[:, g, :]).then_inc(kept, 1)
                        if isinstance(c, int) and (c < LAG or c - LAG + G >= n_chunks):
                            continue
                        a.wait_ge(turned, c - LAG + 1)
                        a.wait_ge(kept, c - LAG + 1)
                        alone(a, m)
                        rows.feed(a, c - LAG + G, (g - LAG) % G)
                peeled(a, rounds, body)

            @block.vector
            def _(v):
                ch = Chain(v, dve)

                def mask(c, s):
                    v.tensor_scalar(masks[:, s, :], m.lanes[:, :], lane(c), -BIG, ALU.not_equal, ALU.mult)\
                     .then_inc(masked, 1)

                def fill_rest(i, c, g):
                    v.wait_ge(rows.fetched[g], 16 * i + 16)
                    v.wait_ge(masked, c + 1)
                    n = H - ON_ACT - ON_POOL
                    v.tensor_tensor(
                        heads_of(g % PSLOTS, H - n, H).rearrange("p (h n) -> p h n", h=n),
                        masks[:, g % PSLOTS, :].unsqueeze(1).broadcast_to([P, n, P]),
                        ring[:, g, H - n:H].unsqueeze(2).broadcast_to([P, n, P]), op=ALU.add).then_inc(filled_v, 1)

                for s in range(PSLOTS):
                    mask(s, s)
                for g in range(2):
                    fill_rest(0, g, g)

                def body(i):
                    for g in range(G):
                        c, s = i * G + g, g % PSLOTS
                        v.wait_ge(turned, c + 1)
                        v.tensor_reduce(chunk_best[:, :],
                                        m.ps[:, 2 * s:2 * s + 2, :].rearrange("p a b -> p (a b)")
                                        .rearrange("p (h e) -> p h e", e=P), AX.X, ALU.max).then_inc(reduced, 1)
                        if g % F == 0:
                            at = offsets(nc, mybir.EngineType.DVE, places, c, F, (buckets - 1) * H)
                        if not (isinstance(c, int) and c + PSLOTS >= n_chunks):
                            mask(c + PSLOTS, s)
                        v.wait_ge(reduced, c + 1)
                        b = best[:, bass.ds(at[g % F], H)]
                        ch.link(v.tensor_tensor(b, b, chunk_best[:, :], op=ALU.max))
                        if not (isinstance(c, int) and c + 2 >= n_chunks):
                            wait_at_least(v, turned, c + 3 - PSLOTS)
                            fill_rest(i + (g + 2) // G, c + 2, (g + 2) % G)
                ch.rounds(rounds, G, body)

            @block.tensor
            def _(pe):
                def body(i):
                    for g in range(G):
                        c, s = i * G + g, g % PSLOTS
                        pe.wait_ge(filled_a, c + 1)
                        pe.wait_ge(filled_p, c + 1)
                        pe.wait_ge(filled_v, c + 1)
                        wait_at_least(pe, reduced, c + 1 - PSLOTS)
                        for h in range(H):
                            last = pe.transpose(m.ps[:, 2 * s + h // 4, (h % 4) * P:(h % 4 + 1) * P],
                                                heads_of(s, h, h + 1), m.ident[:, :])
                        last.then_inc(turned, 1)
                peeled(pe, rounds, body)


def aggregate(m, nc, name, n_chunks, buckets, index, lane, table, places, weight=None, head_weight=None, sums=None,
              prefetch=()):
    per_head = head_weight is not None
    width = AW if sums else D
    ks = ExitStack()
    with ks:
        sb = lambda n, s, d=F32: ks.enter_context(nc.sbuf_tensor(f"{name}_{n}", s, d))
        sem = lambda n: semaphore(m, nc, f"{name}_{n}")
        onehot = sb("onehot", [P, PSLOTS, P])
        msg = m.stage
        indexed, hot, weighed, summed, added = (sem(n) for n in ("indexed", "hot", "weighed", "summed", "added"))
        fetched = [sem(f"fetched{g}") for g in range(G)]
        rounds = n_chunks // G
        weighed_a = sem("weighed_a")
        ON_ACT = 4
        prefetched = sem("prefetched")

        with nc.Block() as block:

            @block.sync
            def _(sp):
                for dst, src in prefetch:
                    sp.dma_start(dst, src).then_inc(prefetched, 16)
                if prefetch:
                    sp.wait_ge(prefetched, 16 * len(prefetch))

            @block.scalar
            def _(a):
                for g in range(G):
                    a.copy(m.ib[:, g:g + 1], index[:, g:g + 1]).then_inc(indexed, 1)
                if per_head:
                    def body(i):
                        for g in range(G):
                            c, s = i * G + g, g % PSLOTS
                            a.wait_ge(fetched[g], i * 16 + 16)
                            wait_at_least(a, summed, c + 1 - PSLOTS)
                            alone(a, m)
                            for h in range(ON_ACT):
                                last = a.activation(msg[:, s, h * C:(h + 1) * C], m.rows[:, g, h * C:(h + 1) * C], ACT.Copy,
                                                    scale=head_weight(c, h))
                            last.then_inc(weighed_a, 1)
                            if isinstance(i, int) and c + G - 1 >= n_chunks or isinstance(c, int) and c < 1:
                                continue
                            a.wait_ge(weighed, c)
                            a.wait_ge(weighed_a, c)
                            alone(a, m)
                            a.copy(m.ib[:, (g - 1) % G:(g - 1) % G + 1], index[:, bass.ds(c - 1 + G, 1)]).then_inc(indexed, 1)
                    peeled(a, rounds, body)
                else:
                    with a.Fori(0, rounds - 1) as i:
                        for g in range(G):
                            a.wait_ge(summed, i * G + g + 1)
                            alone(a, m)
                            a.copy(m.ib[:, g:g + 1], index[:, bass.ds((i + 1) * G + g, 1)]).then_inc(indexed, 1)

            @block.gpsimd
            def _(pool):
                with pool.Fori(0, rounds) as i:
                    for g in range(G):
                        pool.wait_ge(indexed, i * G + g + 1)
                        alone(pool, m)
                        pool.indirect_dma_start(
                            out=m.rows[:, g, :], out_offset=None, in_=table,
                            in_offset=bass.IndirectOffsetOnAxis(ap=m.ib[:, g:g + 1], axis=0))\
                            .then_inc(fetched[g], 16)

            @block.vector
            def _(v):
                def heat(i, g):
                    c, s = i * G + g, g % PSLOTS
                    if weight is None:
                        v.tensor_scalar(onehot[:, s, :], m.lanes[:, :], lane(c), None, ALU.is_equal).then_inc(hot, 1)
                    else:
                        v.tensor_scalar(onehot[:, s, :], m.lanes[:, :], lane(c), weight(c), ALU.is_equal, ALU.mult)\
                         .then_inc(hot, 1)
                    if per_head:
                        v.wait_ge(fetched[g], i * 16 + 16)
                        on_dve = lambda rows: rows[:, ON_ACT * C:D].rearrange("p (h c) -> p h c", c=C)
                        v.tensor_tensor(on_dve(msg[:, s, :]), on_dve(m.rows[:, g, :]),
                                        head_weight(c, ON_ACT, H - ON_ACT).unsqueeze(2).broadcast_to([P, H - ON_ACT, C]),
                                        op=ALU.mult)\
                         .then_inc(weighed, 1)

                for s in range(PSLOTS):
                    heat(0, s)

                def body(i):
                    for g in range(G):
                        c, s = i * G + g, g % PSLOTS
                        if g % F == 0:
                            at = offsets(nc, mybir.EngineType.DVE, places, c, F, (buckets - 1) * AW)
                        v.wait_ge(summed, c + 1)
                        wait_at_least(v, added, c)
                        acc = m.region[:, bass.ds(at[g % F], width)]
                        sums_of = m.ps[:, 2 * s:2 * s + 2, :].rearrange("p a b -> p (a b)")[:, 0:width]
                        v.tensor_tensor(acc, acc, sums_of, op=ALU.add).then_inc(added, 1)
                        if not (isinstance(c, int) and c + PSLOTS >= n_chunks):
                            ahead = g + PSLOTS
                            heat(i + ahead // G, ahead % G)
                peeled(v, rounds, body)

            @block.tensor
            def _(pe):
                def body(i):
                    for g in range(G):
                        c, s = i * G + g, g % PSLOTS
                        pe.wait_ge(hot, c + 1)
                        if per_head:
                            pe.wait_ge(weighed, c + 1)
                            pe.wait_ge(weighed_a, c + 1)
                        else:
                            pe.wait_ge(fetched[g], i * 16 + 16)
                        wait_at_least(pe, added, c + 1 - PSLOTS)
                        rows = msg[:, s, :] if per_head else m.rows[:, g, :]
                        if sums:
                            pe.matmul(m.ps[:, 2 * s + 1, 0:H], onehot[:, s, :], sums(c), start=True, stop=True)
                        pe.matmul(m.ps[:, 2 * s, :], onehot[:, s, :], rows, start=True, stop=True).then_inc(summed, 1)
                peeled(pe, rounds, body)


def fold_attention(m, nc, name, loads, folds):
    ks = ExitStack()
    with ks:
        sem = lambda n: semaphore(m, nc, f"{name}_{n}")
        loaded, dve = sem("loaded"), sem("dve")
        with nc.Block() as block:

            @block.sync
            def _(sp):
                for dst, src in loads:
                    sp.dma_start(dst, src).then_inc(loaded, 16)

            @block.vector
            def _(v):
                ch = Chain(v, dve)
                if loads:
                    v.wait_ge(loaded, 16 * len(loads))
                for w, row, groups, out in folds:
                    prod = m.scratch.rearrange("p (k d) -> p k d", k=KC)
                    ch.link(v.tensor_tensor(prod, w, row.unsqueeze(1).broadcast_to([P, KC, D]), op=ALU.mult))
                    for k in range(KC):
                        ch.link(v.tensor_reduce(out[:, k, :], prod[:, k, :].rearrange("p (g c) -> p g c", g=groups),
                                                AX.X, ALU.add))


def attention_table(m, nc, name, buckets, target, best, out_sb, own=None):
    ks = ExitStack()
    with ks:
        sem = lambda n: semaphore(m, nc, f"{name}_{n}")
        dve, set_ = sem("dve"), sem("set")
        asked, done = sem("asked"), sem("done")
        logit, top = out_sb[:, :, 0:H], out_sb[:, :, H:2 * H]
        with nc.Block() as block:

            @block.vector
            def _(v):
                ch = Chain(v, dve)
                link = ch.link
                link(v.tensor_copy(logit, target))
                link(v.tensor_tensor(top, best, logit, op=ALU.add))
                link(v.tensor_scalar(m.scratch[:, 0:buckets * H].rearrange("p (b h) -> p b h", h=H), top, 0.2, None, ALU.mult))
                v.tensor_tensor(top, top, m.scratch[:, 0:buckets * H].rearrange("p (b h) -> p b h", h=H),
                                op=ALU.max).then_inc(set_, 1)
                v.wait_ge(set_, 1)
                if own:
                    src, w = own
                    link(v.tensor_tensor(w, src, logit, op=ALU.add))
                    s3 = m.scratch[:, 0:buckets * H].rearrange("p (b h) -> p b h", h=H)
                    link(v.tensor_scalar(s3, w, 0.2, None, ALU.mult))
                    link(v.tensor_tensor(w, w, s3, op=ALU.max))
                    v.tensor_tensor(w, w, top, op=ALU.subtract).then_inc(asked, 1)

            @block.scalar
            def _(a):
                if own:
                    a.wait_ge(asked, 1)
                    a.activation(own[1], own[1], ACT.Exp).then_inc(done, 1)


def edge_weights(m, nc, name, n_chunks, logits, targets, out):
    ks = ExitStack()
    with ks:
        sem = lambda n: semaphore(m, nc, f"{name}_{n}")
        dve, asked, done = sem("dve"), sem("asked"), sem("done")
        w = n_chunks * H
        cube = lambda a: a.rearrange("p (c h) -> p c h", h=H)
        tg = targets[:, 0:n_chunks * 2 * H].rearrange("p (c f) -> p c f", f=2 * H)
        scr = m.scratch[:, 0:w]
        with nc.Block() as block:

            @block.vector
            def _(v):
                ch = Chain(v, dve)
                link = ch.link
                link(v.tensor_tensor(cube(out[:, 0:w]), cube(logits[:, 0:w]), tg[:, :, 0:H], op=ALU.add))
                link(v.tensor_scalar(scr, out[:, 0:w], 0.2, None, ALU.mult))
                link(v.tensor_tensor(out[:, 0:w], out[:, 0:w], scr, op=ALU.max))
                link(v.tensor_tensor(cube(out[:, 0:w]), cube(out[:, 0:w]), tg[:, :, H:2 * H], op=ALU.subtract))
                v.tensor_scalar(out[:, 0:w], out[:, 0:w], 0.0, None, ALU.min).then_inc(asked, 1)

            @block.scalar
            def _(a):
                a.wait_ge(asked, 1)
                a.activation(out[:, 0:w], out[:, 0:w], ACT.Exp).then_inc(done, 1)


def fill(m, nc, name, jobs):
    ks = ExitStack()
    with ks:
        sem = lambda n: semaphore(m, nc, f"{name}_{n}")
        dve, stored, set_ = sem("dve"), sem("stored"), sem("set")
        with nc.Block() as block:

            @block.vector
            def _(v):
                ch = Chain(v, dve)
                for kind, dst, what in jobs:
                    if kind == "set":
                        ch.link(v.memset(dst, what))
                    elif kind == "copy":
                        ch.link(v.tensor_copy(dst, what))
                    elif kind == "add":
                        ch.link(v.tensor_tensor(dst, dst, what, op=ALU.add))
                v.sem_inc(set_, 1)

            @block.sync
            def _(sp):
                stores = [(d, w) for k, d, w in jobs if k == "store"]
                if stores:
                    sp.wait_ge(set_, 1)
                    for d, w in stores:
                        sp.dma_start(d, w).then_inc(stored, 16)
                    sp.wait_ge(stored, 16 * len(stores))


def acc_rows(m, n=T):
    return m.region[:, 0:n * AW].rearrange("p (b w) -> p b w", w=AW)


def spline_network(m, nc):
    CA, CB = (1 / 6) ** (1 / 3), (4 / 6) ** (1 / 3)
    ks = ExitStack()
    with ks:
        sb = lambda n, s, d=F32: ks.enter_context(nc.sbuf_tensor(f"kan_{n}", s, d))
        sem = lambda n: semaphore(m, nc, f"kan_{n}")
        weights = m.region[:, T * AW:T * AW + (R8 + 1) * KC * D].rearrange("p (j k d) -> p j k d", k=KC, d=D)
        dist, wide, near, wide2, near2 = (
            m.own[:, 2 * n * D:2 * (n + 1) * D].rearrange("p (b d) -> p b d", b=2) for n in range(5))
        basis = m.rows[:, 0:4, :]
        aT, silu = m.rows[:, 4:6, :], m.rows[:, 6:8, :]
        grown = m.stage[:, 0, :]
        rden = sb("rden", [P, T])
        den_set, agg_ready, turned = (sem(n) for n in ("den_set", "agg_ready", "turned"))
        aT_set, grown_set, silu_set, powers = (sem(n) for n in ("aT_set", "grown_set", "silu_set", "powers"))
        basis_set, eaten, added = (sem(n) for n in ("basis_set", "eaten", "added"))
        dve, act = sem("dve"), sem("act")
        acc = acc_rows(m)
        scatter = Scatter(m, nc, "scatterA", m.recA)

        with nc.Block() as block:

            @block.sync
            def _(sp):
                scatter.load(sp, m.ra)

            @block.gpsimd
            def _(pool):
                scatter.run(pool, m.posA, m.rec_inA)

            @block.scalar
            def _(a):
                ch = Chain(a, act)
                a.wait_ge(den_set, 1)

                def agg(t, b):
                    wait_at_least(a, turned, t - 1)
                    if not isinstance(t, int):
                        alone(a, m)
                    a.activation(m.h[:, b, :], m.region[:, bass.ds(t * AW, D)], ACT.Copy,
                                 scale=rden[:, bass.ds(t, 1)]).then_inc(agg_ready, 1)

                def pair(i):
                    for b in range(2):
                        t = 2 * i + b
                        if not (isinstance(t, int) and t == T - 1):
                            agg(t + 1, 1 - b)
                        a.wait_ge(aT_set, t + 1)
                        wait_at_least(a, silu_set, t)
                        a.activation(grown, aT[:, b, :], ACT.Exp, scale=-1.0).then_inc(grown_set, 1)
                        for q in range(R8):
                            z = q % 2
                            wait_at_least(a, basis_set, t * R8 + q - 1)
                            ch.link(a.activation(dist[:, z, :], aT[:, b, :], ACT.Abs, scale=2.5,
                                                 bias=m.consts[:, q:q + 1]))
                            a.activation(wide[:, z, :], dist[:, z, :], ACT.Relu, scale=-CA, bias=m.consts[:, R8:R8 + 1])
                            ch.link(a.activation(near[:, z, :], dist[:, z, :], ACT.Relu, scale=-CB,
                                                 bias=m.consts[:, R8 + 1:R8 + 2]))
                            a.activation(wide2[:, z, :], wide[:, z, :], ACT.Square)
                            a.activation(near2[:, z, :], near[:, z, :], ACT.Square).then_inc(powers, 1)
                agg(0, 0)
                ch.rounds(T // 2, 4 * R8, pair)

            @block.vector
            def _(v):
                ch = Chain(v, dve)
                link = ch.link
                link(v.tensor_scalar(rden[:, :], acc[:, :, D], 1e-30, None, ALU.max))
                v.reciprocal(rden[:, :], rden[:, :]).then_inc(den_set, 1)

                def copy_aT(t, b):
                    v.wait_ge(turned, t + 1)
                    wait_at_least(v, powers, (t - 1) * R8)
                    v.tensor_copy(aT[:, b, :], m.ps[:, b, :]).then_inc(aT_set, 1)

                def one_basis(t, q):
                    z = q % 2
                    v.wait_ge(powers, t * R8 + q + 1)
                    v.tensor_tensor(wide2[:, z, :], wide2[:, z, :], wide[:, z, :], op=ALU.mult)
                    link(v.tensor_tensor(near2[:, z, :], near2[:, z, :], near[:, z, :], op=ALU.mult))
                    wait_at_least(v, eaten, t * R8 + q - 3)
                    v.tensor_tensor(basis[:, q % 4, :], wide2[:, z, :], near2[:, z, :], op=ALU.subtract)\
                     .then_inc(basis_set, 1)

                def add_x(t, b):
                    v.wait_ge(eaten, (t + 1) * R8)
                    xt = m.x[:, bass.ds(t * D, D)]
                    v.tensor_tensor(xt, xt, m.ps[:, 2 + b, :], op=ALU.add).then_inc(added, 1)

                def pair(i):
                    for b in range(2):
                        t = 2 * i + b
                        v.wait_ge(grown_set, t + 1)
                        v.wait_ge(aT_set, t + 1)
                        link(v.tensor_scalar(grown, grown, 1.0, None, ALU.add))
                        link(v.reciprocal(grown, grown))
                        wait_at_least(v, eaten, (t - 1) * R8)
                        v.tensor_tensor(silu[:, b, :], aT[:, b, :], grown, op=ALU.mult).then_inc(silu_set, 1)
                        for q in range(R8):
                            if q == 2 and not (isinstance(t, int) and t == 0):
                                add_x(t - 1, 1 - b)
                            if q == 4 and not (isinstance(t, int) and t == T - 1):
                                copy_aT(t + 1, 1 - b)
                            one_basis(t, q)
                copy_aT(0, 0)
                ch.rounds(T // 2, 2 * (2 + R8), pair)
                add_x(T - 1, 1)

            @block.tensor
            def _(pe):
                def turn(t, b):
                    pe.wait_ge(agg_ready, t + 1)
                    wait_at_least(pe, aT_set, t - 1)
                    for k in range(KC):
                        last = pe.transpose(m.ps[:, b, k * P:(k + 1) * P], m.h[:, b, k * P:(k + 1) * P], m.ident[:, :])
                    last.then_inc(turned, 1)

                def pair(i):
                    for b in range(2):
                        t = 2 * i + b
                        if not (isinstance(t, int) and t == T - 1):
                            turn(t + 1, 1 - b)
                        pe.wait_ge(silu_set, t + 1)
                        wait_at_least(pe, added, t - 1)
                        for k in range(KC):
                            pe.matmul(m.ps[:, 2 + b, :], silu[:, b, k * P:(k + 1) * P], weights[:, 0, k, :],
                                      start=k == 0, stop=False)
                        for q in range(R8):
                            pe.wait_ge(basis_set, t * R8 + q + 1)
                            for k in range(KC):
                                last = pe.matmul(m.ps[:, 2 + b, :], basis[:, q % 4, k * P:(k + 1) * P],
                                                 weights[:, 1 + q, k, :], start=False, stop=q == R8 - 1 and k == KC - 1)
                            last.then_inc(eaten, 1)
                turn(0, 0)
                peeled(pe, T // 2, pair)


def mean_layer(m, nc, weights):
    ks = ExitStack()
    with ks:
        sb = lambda n, s, d=F32: ks.enter_context(nc.sbuf_tensor(f"mean_{n}", s, d))
        sem = lambda n: semaphore(m, nc, f"mean_{n}")
        bias = sb("bias", [P, D])
        rdeg = sb("rdeg", [P, T])
        loaded, deg_set, neigh_ready, turned, copied, whole, added = (
            sem(n) for n in ("loaded", "deg_set", "neigh_ready", "turned", "copied", "whole", "added"))
        h_in = [sem(f"h_in{b}") for b in range(2)]
        dve = sem("dve")
        acc = acc_rows(m)

        with nc.Block() as block:

            @block.sync
            def _(sp):
                sp.dma_start(bias[:, :], m.b1.rearrange("(a d) -> a d", a=1).broadcast_to([P, D])).then_inc(loaded, 16)

                def pair(i):
                    for b in range(2):
                        t = 2 * i + b
                        wait_at_least(sp, turned, t - 1)
                        sp.dma_start(m.rows[:, b, :], m.h_table[bass.ds(t * P, P), :]).then_inc(h_in[b], 16)
                peeled(sp, T // 2, pair)

            @block.scalar
            def _(a):
                a.wait_ge(deg_set, 1)

                def pair(i):
                    for b in range(2):
                        t = 2 * i + b
                        wait_at_least(a, turned, t - 1)
                        if not isinstance(i, int):
                            alone(a, m)
                        a.activation(m.h[:, b, :], m.region[:, bass.ds(t * AW, D)], ACT.Copy,
                                     scale=rdeg[:, bass.ds(t, 1)]).then_inc(neigh_ready, 1)
                peeled(a, T // 2, pair)

            @block.tensor
            def _(pe):
                def turn(t, i, b):
                    pe.wait_ge(h_in[b], i * 16 + 16)
                    pe.wait_ge(neigh_ready, t + 1)
                    wait_at_least(pe, copied, t - 1)
                    for o, rows in enumerate((m.rows[:, b, :], m.h[:, b, :])):
                        for k in range(KC):
                            last = pe.transpose(m.ps[:, 2 * b + o, k * P:(k + 1) * P], rows[:, k * P:(k + 1) * P],
                                                m.ident[:, :])
                    last.then_inc(turned, 1)

                turn(0, 0, 0)

                def pair(i):
                    for b in range(2):
                        t = 2 * i + b
                        if not (isinstance(t, int) and t == T - 1):
                            turn(t + 1, i + b, 1 - b)
                        pe.wait_ge(copied, t + 1)
                        wait_at_least(pe, added, t - 1)
                        for k in range(2 * KC):
                            last = pe.matmul(m.ps[:, 4 + b, :], m.hT[:, b, k, :], weights[:, k, :],
                                             start=k == 0, stop=k == 2 * KC - 1)
                        last.then_inc(whole, 1)
                peeled(pe, T // 2, pair)

            @block.vector
            def _(v):
                ch = Chain(v, dve)
                ch.link(v.tensor_scalar(rdeg[:, :], acc[:, :, D], 1.0, None, ALU.max))
                v.reciprocal(rdeg[:, :], rdeg[:, :]).then_inc(deg_set, 1)
                v.wait_ge(loaded, 16)

                def copy_hT(t, b):
                    v.wait_ge(turned, t + 1)
                    wait_at_least(v, whole, t - 1)
                    v.tensor_copy(m.hT[:, b, :, :].rearrange("p k n -> p (k n)"),
                                  m.ps[:, 2 * b:2 * b + 2, :].rearrange("p a n -> p (a n)")).then_inc(copied, 1)

                copy_hT(0, 0)

                def pair(i):
                    for b in range(2):
                        t = 2 * i + b
                        if not (isinstance(t, int) and t == T - 1):
                            copy_hT(t + 1, 1 - b)
                        v.wait_ge(whole, t + 1)
                        ch.link(v.tensor_tensor(m.stage[:, b, :], m.ps[:, 4 + b, :], bias[:, :], op=ALU.add))
                        xt = m.x[:, bass.ds(t * D, D)]
                        v.scalar_tensor_tensor(out=xt, in0=m.stage[:, b, :], scalar=0.0, in1=xt,
                                               op0=ALU.max, op1=ALU.add).then_inc(added, 1)
                ch.rounds(T // 2, 2, pair)


def relational(m, nc, name, source, comp, bias):
    ks = ExitStack()
    with ks:
        sb = lambda n, s, d=F32: ks.enter_context(nc.sbuf_tensor(f"{name}_{n}", s, d))
        sem = lambda n: semaphore(m, nc, f"{name}_{n}")
        stats = sb("stats", [P, T * 6])
        mv = sb("mv", [P, T * 2])
        rstd = sb("rstd", [P, T])
        nbias = sb("nbias", [P, T])
        slab = lambda o, n: m.region[:, T * AW + o * KC * D:T * AW + (o + n) * KC * D]
        weights = slab(0, BASES).rearrange("p (b k d) -> p b k d", b=BASES, k=KC)
        loop = slab(BASES, 1).rearrange("p (k d) -> p k d", k=KC)
        hb = slab(BASES + 1, 2).rearrange("p (s b d) -> p s b d", s=2, b=BASES)
        mix = slab(BASES + 3, 2).rearrange("p (r d) -> p r d", r=R8)
        root_asked, root_done, norm_set = sem("root_asked"), sem("root_done"), sem("norm_set")
        few_in, h_ready, turned, h_turned = sem("few_in"), sem("h_ready"), sem("turned"), sem("h_turned")
        multiplied, own_ready, h_summed = sem("multiplied"), sem("own_ready"), sem("h_summed")
        hb_set, own_set, begun, mixed = sem("hb_set"), sem("own_set"), sem("begun"), sem("mixed")
        stored = [sem(f"stored{r}") for r in range(R8)]
        dve = sem("dve")
        MIX = (BASES - 1) * R8

        with nc.Block() as block:

            @block.sync
            def _(sp):
                sp.dma_start(m.comp[:, :], comp.rearrange("(a r) b -> a (r b)", a=1).broadcast_to([P, R8 * BASES]))\
                  .then_inc(few_in, 16)
                sp.dma_start(m.own_bias[:, :], bias.rearrange("(a d) -> a d", a=1).broadcast_to([P, D])).then_inc(few_in, 16)

                def pair(i):
                    for b in range(2):
                        t = 2 * i + b
                        for r in range(R8):
                            sp.wait_ge(mixed, t * MIX + MIX - R8 + r + 1)
                            sp.dma_start(m.rel_table[bass.ds(t * P + r * NP, P), :], mix[:, r, :])\
                              .then_inc(stored[r], 16)
                peeled(sp, T // 2, pair)
                for s in stored:
                    sp.wait_ge(s, 16 * T)

            @block.vector
            def _(v):
                ch = Chain(v, dve)
                if source == "norm":
                    normalise_setup(m, v, ch, stats, mv, rstd, nbias, root_asked, root_done)
                v.sem_inc(norm_set, 1)
                v.wait_ge(few_in, 32)

                def mid_rows(t, b):
                    wait_at_least(v, turned, t - 1)
                    v.tensor_tensor(m.h[:, b, :], m.region[:, bass.ds(t * AW, D)],
                                    m.own[:, bass.ds(t * D, D)], op=ALU.add).then_inc(h_summed, 1)
                    v.wait_ge(h_summed, t + 1)
                    v.tensor_scalar(m.h[:, b, :], m.h[:, b, :], 0.0, None, ALU.max).then_inc(h_ready, 1)

                def copy_hT(t, b):
                    v.wait_ge(turned, t + 1)
                    wait_at_least(v, own_ready, t - 1)
                    v.tensor_copy(m.hT[:, b, 0:KC, :].rearrange("p k n -> p (k n)"), m.ps[:, b, :])\
                     .then_inc(h_turned, 1)

                def pair(i):
                    for b in range(2):
                        t = 2 * i + b
                        more = not (isinstance(t, int) and t == T - 1)
                        if more and source == "mid":
                            mid_rows(t + 1, 1 - b)
                        for j in range(1, BASES):
                            if j == 2 and more:
                                copy_hT(t + 1, 1 - b)
                            for r in range(R8):
                                if j == 1:
                                    v.wait_ge(begun, t * R8 + r + 1)
                                else:
                                    v.wait_ge(mixed, t * MIX + (j - 2) * R8 + r + 1)
                                if r == 0:
                                    v.wait_ge(hb_set, t * BASES + j + 1)
                                v.scalar_tensor_tensor(
                                    out=mix[:, r, :], in0=hb[:, b, j, :], scalar=m.comp[:, r * BASES + j:r * BASES + j + 1],
                                    in1=mix[:, r, :], op0=ALU.mult, op1=ALU.add).then_inc(mixed, 1)
                            if j == BASES - 1:
                                v.wait_ge(own_ready, t + 1)
                                v.tensor_tensor(m.own[:, bass.ds(t * D, D)], m.ps[:, 6 + b, :], m.own_bias[:, :],
                                                op=ALU.add).then_inc(own_set, 1)
                if source == "mid":
                    mid_rows(0, 0)
                copy_hT(0, 0)
                peeled(v, T // 2, pair)

            @block.scalar
            def _(a):
                if source == "norm":
                    a.wait_ge(root_asked, 1)
                    a.activation(rstd[:, :], rstd[:, :], ACT.Sqrt).then_inc(root_done, 1)
                a.wait_ge(norm_set, 1)
                a.wait_ge(few_in, 32)

                def rows(t, b):
                    wait_at_least(a, turned, t - 1)
                    if not isinstance(t, int):
                        alone(a, m)
                    a.activation(m.h[:, b, :], m.x[:, bass.ds(t * D, D)], ACT.Relu,
                                 bias=nbias[:, bass.ds(t, 1)], scale=rstd[:, bass.ds(t, 1)]).then_inc(h_ready, 1)

                def pair(i):
                    for b in range(2):
                        t = 2 * i + b
                        if source == "norm" and not (isinstance(t, int) and t == T - 1):
                            rows(t + 1, 1 - b)
                        wait_at_least(a, mixed, (t - 1) * MIX)
                        for j in range(BASES):
                            a.wait_ge(multiplied, t * BASES + j + 1)
                            a.activation(hb[:, b, j, :], m.ps[:, 2 + j, :], ACT.Copy).then_inc(hb_set, 1)
                            if j == 0:
                                a.wait_ge(hb_set, t * BASES + 1)
                                for r in range(R8):
                                    wait_at_least(a, stored[r], t * 16)
                                    a.activation(mix[:, r, :], hb[:, b, 0, :], ACT.Copy,
                                                 scale=m.comp[:, r * BASES:r * BASES + 1]).then_inc(begun, 1)
                if source == "norm":
                    rows(0, 0)
                peeled(a, T // 2, pair)

            @block.tensor
            def _(pe):
                def turn(t, b):
                    pe.wait_ge(h_ready, t + 1)
                    wait_at_least(pe, h_turned, t - 1)
                    for k in range(KC):
                        last = pe.transpose(m.ps[:, b, k * P:(k + 1) * P], m.h[:, b, k * P:(k + 1) * P], m.ident[:, :])
                    last.then_inc(turned, 1)

                def pair(i):
                    for b in range(2):
                        t = 2 * i + b
                        if not (isinstance(t, int) and t == T - 1):
                            turn(t + 1, 1 - b)
                        pe.wait_ge(h_turned, t + 1)
                        for j in range(BASES):
                            wait_at_least(pe, hb_set, (t - 1) * BASES + j + 1)
                            for k in range(KC):
                                last = pe.matmul(m.ps[:, 2 + j, :], m.hT[:, b, k, :], weights[:, j, k, :],
                                                 start=k == 0, stop=k == KC - 1)
                            last.then_inc(multiplied, 1)
                        wait_at_least(pe, own_set, t - 1)
                        for k in range(KC):
                            last = pe.matmul(m.ps[:, 6 + b, :], m.hT[:, b, k, :], loop[:, k, :],
                                             start=k == 0, stop=k == KC - 1)
                        last.then_inc(own_ready, 1)
                turn(0, 0)
                peeled(pe, T // 2, pair)


def fuse_relations(m, nc):
    ks = ExitStack()
    with ks:
        sb = lambda n, s, d=F32: ks.enter_context(nc.sbuf_tensor(f"fuse_{n}", s, d))
        sem = lambda n: semaphore(m, nc, f"fuse_{n}")
        behind = m.region[:, NBA * AW:]
        w1 = behind[:, 0:KC * SEM_D].rearrange("p (k d) -> p k d", k=KC)
        b1, w2, junk = (behind[:, (KC + n) * SEM_D:(KC + n + 1) * SEM_D] for n in range(3))
        bias = m.stage
        xt = m.rows[:, :, :].rearrange("p (b r) d -> p b r d", b=2)
        z = m.own[:, 0:2 * R4 * D].rearrange("p (b r d) -> p b r d", b=2, r=R4)
        zT = m.own[:, 2 * R4 * D:2 * R4 * D + 2 * D].rearrange("p (b d) -> p b d", b=2)
        th = m.hT[:, :, :, :].rearrange("p b k n -> p (b k n)").rearrange("p (b r d) -> p b r d", b=2, r=R4)
        den = sb("den", [P, R4, H])
        own = sb("own", [P, R4, H])
        w = sb("w", [P, R4])
        top = sb("top", [P, 4])
        beta = sb("beta", [P, R4])
        loaded, z_ready, turned, zT_set, pre_ready = (
            sem(n) for n in ("loaded", "z_ready", "turned", "zT_set", "pre_ready"))
        th_set, asked, answered, out_set, stored = (sem(n) for n in ("th_set", "asked", "answered", "out_set", "stored"))
        xt_in = [sem(f"xt_in{b}") for b in range(2)]
        dve, dve_z = sem("dve"), sem("dve_z")

        with nc.Block() as block:

            @block.sync
            def _(sp):
                sp.dma_start(w1, m.sem_w1.rearrange("(k p) d -> p k d", p=P)).then_inc(loaded, 16)
                sp.dma_start(b1, m.sem_b1.rearrange("(a d) -> a d", a=1).broadcast_to([P, SEM_D])).then_inc(loaded, 16)
                sp.dma_start(w2, m.sem_w2.rearrange("d a -> a d").broadcast_to([P, SEM_D])).then_inc(loaded, 16)
                sp.dma_start(bias[:, :, :].rearrange("p r d -> p (r d)"),
                             m.bias3.rearrange("(a r) d -> a (r d)", a=1).broadcast_to([P, R4 * D])).then_inc(loaded, 16)
                view = m.xt_table.rearrange("(r n) d -> n r d", r=R4)

                def pair(i):
                    for b in range(2):
                        t = 2 * i + b
                        wait_at_least(sp, z_ready, R4 * (t - 1))
                        sp.dma_start(xt[:, b, :, :], view[bass.ds(t * P, P), :, :]).then_inc(xt_in[b], 16)
                peeled(sp, T // 2, pair)

            @block.vector
            def _(v):
                cz, cs = Chain(v, dve_z), Chain(v, dve)
                by_head = lambda a: a.rearrange("p (h c) -> p h c", h=H)
                wide = lambda a: a.unsqueeze(2).broadcast_to([P, H, C])
                LZ, LS = 3 + 3 * R4, R4 + 1 + 3 + R4

                def outputs(t, i, b):
                    cz.base, cz.k = t * LZ, 0
                    link = cz.link
                    v.wait_ge(xt_in[b], i * 16 + 16)
                    mine = m.region[:, bass.ds(t * R4 * AW, R4 * AW)].rearrange("p (r w) -> p r w", w=AW)
                    selfs = m.self_w[:, bass.ds(t * R4 * H, R4 * H)].rearrange("p (r h) -> p r h", h=H)
                    link(v.tensor_tensor(den[:, :, :], mine[:, :, D:AW], selfs, op=ALU.add))
                    link(v.reciprocal(den[:, :, :], den[:, :, :]))
                    link(v.tensor_tensor(own[:, :, :], selfs, den[:, :, :], op=ALU.mult))
                    for r in range(R4):
                        zr, xr = z[:, b, r, :], xt[:, b, r, :]
                        link(v.tensor_tensor(by_head(zr), by_head(mine[:, r, 0:D]), wide(den[:, r, :]), op=ALU.mult))
                        link(v.tensor_tensor(by_head(xr), by_head(xr), wide(own[:, r, :]), op=ALU.mult))
                        link(v.tensor_tensor(zr, zr, xr, op=ALU.add))
                        v.tensor_tensor(zr, zr, bias[:, r, :], op=ALU.add).then_inc(z_ready, 1)
                    assert cz.k == LZ

                def scores(t, b):
                    cs.base, cs.k = t * LS, 0
                    link = cs.link
                    for r in range(R4):
                        v.wait_ge(th_set, t * R4 + r + 1)
                        link(v.tensor_tensor_reduce(out=junk, in0=th[:, b, r, :], in1=w2, scale=1.0, scalar=0.0,
                                                    op0=ALU.mult, op1=ALU.add, accum_out=w[:, r:r + 1]))
                    link(v.tensor_reduce(top[:, 0:1], w[:, :], AX.X, ALU.max))
                    v.tensor_scalar(beta[:, :], w[:, :], top[:, 0:1], None, ALU.subtract).then_inc(asked, 1)
                    v.wait_ge(answered, t + 1)
                    link(v.tensor_reduce(top[:, 1:2], beta[:, :], AX.X, ALU.add))
                    link(v.reciprocal(top[:, 2:3], top[:, 1:2]))
                    link(v.tensor_scalar(beta[:, :], beta[:, :], top[:, 2:3], None, ALU.mult))
                    xs = m.x[:, bass.ds(t * D, D)]
                    for r in range(R4):
                        link(v.scalar_tensor_tensor(out=xs, in0=z[:, b, r, :], scalar=beta[:, r:r + 1], in1=xs,
                                                    op0=ALU.mult, op1=ALU.add))
                    v.sem_inc(out_set, 1)
                    assert cs.k == LS

                v.wait_ge(loaded, 64)
                outputs(0, 0, 0)

                def pair(i):
                    for b in range(2):
                        t = 2 * i + b
                        if not (isinstance(t, int) and t == T - 1):
                            wait_at_least(v, turned, R4 * t)
                            outputs(t + 1, i + b, 1 - b)
                        scores(t, b)
                peeled(v, T // 2, pair)

            @block.scalar
            def _(a):
                def pair(i):
                    for b in range(2):
                        t = 2 * i + b
                        for r in range(R4):
                            a.wait_ge(turned, t * R4 + r + 1)
                            wait_at_least(a, pre_ready, t * R4 + r - 1)
                            a.activation(zT[:, r % 2, :], m.ps[:, r % 2, :], ACT.Copy).then_inc(zT_set, 1)
                            if r:
                                squash(t, r - 1, b)
                        squash(t, R4 - 1, b)
                        a.wait_ge(asked, t + 1)
                        a.activation(beta[:, :], beta[:, :], ACT.Exp).then_inc(answered, 1)

                def squash(t, r, b):
                    a.wait_ge(pre_ready, t * R4 + r + 1)
                    a.activation(th[:, b, r, :], m.ps[:, 2 + r % 2, 0:SEM_D], ACT.Tanh).then_inc(th_set, 1)
                peeled(a, T // 2, pair)

            @block.tensor
            def _(pe):
                pe.wait_ge(loaded, 64)

                def pair(i):
                    for b in range(2):
                        t = 2 * i + b
                        for r in range(R4):
                            pe.wait_ge(z_ready, t * R4 + r + 1)
                            wait_at_least(pe, zT_set, t * R4 + r - 1)
                            for k in range(KC):
                                last = pe.transpose(m.ps[:, r % 2, k * P:(k + 1) * P], z[:, b, r, k * P:(k + 1) * P],
                                                    m.ident[:, :])
                            last.then_inc(turned, 1)
                            wait_at_least(pe, th_set, t * R4 + r - 1)
                            pre = m.ps[:, 2 + r % 2, 0:SEM_D]
                            pe.matmul(pre, m.ones[0:1, :], b1[0:1, :], start=True, stop=False)
                            pe.wait_ge(zT_set, t * R4 + r + 1)
                            for k in range(KC):
                                last = pe.matmul(pre, zT[:, r % 2, k * P:(k + 1) * P], w1[:, k, :],
                                                 start=False, stop=k == KC - 1)
                            last.then_inc(pre_ready, 1)
                peeled(pe, T // 2, pair)

            @block.gpsimd
            def _(pool):
                for t in range(T):
                    pool.wait_ge(out_set, t + 1)
                    rows = P if t < T - 1 else LAST
                    pool.dma_start(m.out[t * P:t * P + rows, :], m.x[0:rows, t * D:(t + 1) * D]).then_inc(stored, 16)
                pool.wait_ge(stored, 16 * T)


def gnn_kernel(nc, a, probe=None):
    m = Core()
    m.x_in, m.src, m.dst, m.type4 = a["x_in"], a["src"], a["dst"], a["type4"]
    m.type8, m.weight, m.w0, m.a0 = a["type8"], a["weight"], a["w0"], a["a0"]
    m.w1, m.b1, m.w3, m.att_src = a["w1"], a["b1"], a["w3"], a["att_src"]
    m.att_dst, m.bias3, m.sem_w1, m.sem_b1 = a["att_dst"], a["bias3"], a["sem_w1"], a["sem_b1"]
    m.sem_w2, m.base_wT, m.spline_wT, m.basis = a["sem_w2"], a["base_wT"], a["spline_wT"], a["basis"]
    m.comps, m.biases, m.loops, m.out = a["comps"], a["biases"], a["loops"], a["out"]
    ks = ExitStack()
    with ks:
        sb = lambda n, s, d=F32: ks.enter_context(nc.sbuf_tensor(n, s, d))
        dram = lambda n, s: nc.dram_tensor(n, s, F32, kind="Internal").ap()
        m.gate = nc.alloc_semaphore("gate")
        m.sems = []
        m.recA, m.recB = dram("recA", (P * NCA, REC)), dram("recB", (P * NCB, REC))
        m.h_table = dram("h_table", (NP, D))
        m.rel_table = dram("rel_table", (R8 * NP, D))
        m.xt_table = dram("xt_table", (R4 * NP, D))
        m.source_table = dram("source_table", (R4 * NP, H))
        m.source_table0 = dram("source_table0", (NP, H))

        m.ps = ks.enter_context(nc.psum_tensor("ps", [P, 8, 512], F32))
        m.x = sb("x", [P, T * D])
        m.region = sb("region", [P, T * AW + (R8 + 1) * KC * D])
        m.own = sb("own", [P, T * D])
        m.rows = sb("rows", [P, G, D])
        m.ib = sb("ib", [P, G], U32)
        m.h = sb("h", [P, 2, D])
        m.stage = sb("stage", [P, 4, D])
        m.scratch = m.stage[:, :, :].rearrange("p s d -> p (s d)")
        m.hT = sb("hT", [P, 2, 2 * KC, P])
        m.ident = sb("ident", [P, P])
        m.ones = sb("ones", [P, P])
        m.lanes = sb("lanes", [P, P])
        m.zeros = sb("zeros", [P, 8])
        m.consts = sb("consts", [P, R8 + 3])
        m.const_values = [3.5 - j for j in range(R8)] + [2 * (1 / 6) ** (1 / 3), (4 / 6) ** (1 / 3), 0.0]
        m.ra = sb("ra", [P, NCA, REC])
        m.rb = sb("rb", [P, NCB, REC])
        m.ix_src, m.ix_src8, m.ix_src4 = (sb(f"ix_{n}", [P, NCA], U32) for n in ("src", "src8", "src4"))
        m.ix_bdst = sb("ix_bdst", [P, NCB], U32)
        m.accA, m.tileA, m.maxA = (sb(n, [1, NCA], I32) for n in ("accA", "tileA", "maxA"))
        m.accB, m.maxB = (sb(n, [1, NCB], I32) for n in ("accB", "maxB"))
        edge = m.own
        records = ks.enter_context(ExitStack())
        sr = lambda n, s, d=F32: records.enter_context(nc.sbuf_tensor(n, s, d))
        m.posA, m.rec_inA = sr("posA", [EP, EC], U32), sr("rec_inA", [EP, EC, REC])
        m.pos_blk, m.rec_blk = sr("pos_blk", [EP, SC], U32), sr("rec_blk", [EP, SC, REC])
        m.posB = sr("posB", [EP, EC], U32)
        m.rec_inB = m.rows[0:EP, 0:3, :].rearrange("p g d -> p (g d)")[:, 0:EC * REC].rearrange("p (c f) -> p c f", f=REC)
        prepare(m, nc)

        laneA = lambda c: m.ra[:, bass.ds(c, 1), A_LANE]
        laneB = lambda c: m.rb[:, bass.ds(c, 1), B_LANE]
        sums_of_ones = lambda c: m.ones[:, 0:H]
        weights_at = lambda o, n=KC * D: m.region[:, T * AW + o * KC * D:T * AW + o * KC * D + n]
        cube = lambda ap: ap.rearrange("p (k d) -> p k d", d=D)
        by_k = lambda w: w.rearrange("(k p) d -> p k d", p=P)
        zero = ("set", m.region[:, 0:T * AW], 0.0)

        with ExitStack() as layer:
            sl = lambda n, s, d=F32: layer.enter_context(nc.sbuf_tensor(n, s, d))
            fold = sl("fold0", [P, KC, 2])
            st = sl("st", [P, T * 2])
            att = weights_at(1, 2 * D)
            fold_attention(m, nc, "fold0",
                           [(cube(weights_at(0)), m.w0.rearrange("(k p) d -> p k d", p=P)),
                            (att, m.a0.rearrange("d a -> a d").broadcast_to([P, 2 * D]))],
                           [(cube(weights_at(0)), att[:, j * D:(j + 1) * D], 1, fold[:, :, j:j + 1]) for j in range(2)])
            project(m, nc, "p0", h_table=m.h_table, small=(fold[:, :, :], st[:, :]),
                    beside=(Scatter(m, nc, "scatterB", m.recB), m.posB, m.rec_inB, m.rb))
            st3 = st[:, :].rearrange("p (t k) -> p t k", k=2)
            src8 = sl("src8", [P, T, H])
            tgt = sl("tgt0", [P, T, H])
            best = sl("best0", [P, T * H])
            tt = sl("tt0", [P, T, 2 * H])
            fill(m, nc, "f0", [("set", src8[:, :, :], 0.0), ("copy", src8[:, :, 0], st3[:, :, 1]),
                               ("set", tgt[:, :, :], 0.0), ("copy", tgt[:, :, 0], st3[:, :, 0]),
                               ("set", best[:, :], -BIG), zero,
                               ("copy", m.ix_bdst[:, :], m.rb[:, :, B_DST]),
                               ("store", m.source_table0.rearrange("(t p) h -> p t h", p=P), src8[:, :, :])])
            logits, targets = edge[:, 0:NCB * H], edge[:, NCB * H:NCB * 3 * H]
            weights = sl("ew0", [P, NCB * H])
            segment_max_one(m, nc, "m0", NCB, NBB, m.rb, m.ix_bdst, m.source_table0, logits, m.maxB, best)
            attention_table(m, nc, "t0", T, tgt[:, :, :], best[:, :].rearrange("p (b h) -> p b h", h=H), tt)
            target_values(m, nc, "v0", NCB, NBB, m.rb, m.maxB, tt[:, :, :], targets)
            edge_weights(m, nc, "e0", NCB, logits, targets, weights)
            aggregate(m, nc, "a0", NCB, NBB, m.ix_bdst, laneB, m.h_table, m.accB,
                      weight=lambda c: weights[:, bass.ds(c * H, 1)], sums=sums_of_ones,
                      prefetch=[(cube(weights_at(0)), by_k(m.base_wT))] +
                      [(cube(weights_at(1 + j)), by_k(m.spline_wT[j])) for j in range(R8)])
        if probe == "agg0":
            return m
        spline_network(m, nc)
        if probe == "l0":
            return m
        records.close()

        recycle_semaphores(m, nc)

        mean_w = m.region[:, T * AW + (R8 - 1) * KC * D:T * AW + (R8 + 1) * KC * D].rearrange("p (k d) -> p k d", d=D)

        def relation_weights(n):
            return [(cube(weights_at(b)), by_k(m.basis[n][b])) for b in range(BASES)] + \
                [(cube(weights_at(BASES)), by_k(m.loops[n]))]

        project(m, nc, "p1", h_table=m.h_table)
        fill(m, nc, "f1", [zero] + [("copy", a[:, :], m.ra[:, :, f]) for f, a in (
            (A_SRC, m.ix_src), (A_SRC8, m.ix_src8), (A_SRC4, m.ix_src4))])
        aggregate(m, nc, "a1", NCA, T, m.ix_src, laneA, m.h_table, m.tileA, sums=sums_of_ones,
                  prefetch=[(mean_w, by_k(m.w1))] + relation_weights(0))
        mean_layer(m, nc, mean_w)
        if probe == "l1":
            return m

        recycle_semaphores(m, nc)

        flat = lambda ap: ap.rearrange("(a r) h c -> a (r h c)", a=1).broadcast_to([P, R4 * D])
        att3 = weights_at(R4, 2 * R4 * D)

        with ExitStack() as layer:
            sl = lambda n, s, d=F32: layer.enter_context(nc.sbuf_tensor(n, s, d))
            m.comp = sl("comp", [P, R8 * BASES])
            m.own_bias = sl("own_bias", [P, D])
            for n in range(2):
                relational(m, nc, f"r2{n}", ("norm", "mid")[n], m.comps[n], m.biases[n])
                fill(m, nc, f"f2{n}", [zero])
                aggregate(m, nc, f"a2{n}", NCA, T, m.ix_src8, laneA, m.rel_table, m.tileA,
                          weight=lambda c: m.ra[:, bass.ds(c, 1), A_WEIGHT],
                          prefetch=relation_weights(1) if n == 0 else
                          [(cube(weights_at(r)), by_k(m.w3[r])) for r in range(R4)] +
                          [(att3[:, 0:R4 * D], flat(m.att_src)), (att3[:, R4 * D:2 * R4 * D], flat(m.att_dst))])
            fill(m, nc, "f22", [("add", m.x[:, :].rearrange("p (t d) -> p t d", d=D), acc_rows(m)[:, :, 0:D]),
                                ("add", m.x[:, :], m.own[:, :])])
        if probe == "l2":
            return m

        recycle_semaphores(m, nc)

        fold = sb("fold3", [P, KC, R4 * 2 * H])
        al = sb("al", [P, T * R4 * 2 * H])
        best = sb("best3", [P, NBA * H])
        m.self_w = sb("self_w", [P, NBA * H])
        tt = m.region[:, NBA * AW:NBA * (AW + 2 * H)].rearrange("p (b f) -> p b f", f=2 * H)
        al3 = al[:, :].rearrange("p (b f) -> p b f", f=2 * H)
        with ExitStack() as layer:
            sl = lambda n, s, d=F32: layer.enter_context(nc.sbuf_tensor(n, s, d))
            folds = []
            for r in range(R4):
                for o in range(2):
                    row = att3[:, (o * R4 + r) * D:(o * R4 + r + 1) * D]
                    folds.append((cube(weights_at(r)), row, H, fold[:, :, r * 2 * H + o * H:r * 2 * H + (o + 1) * H]))
            fold_attention(m, nc, "fold3", [], folds)
            project(m, nc, "p3", tables=[(cube(weights_at(r)), m.xt_table[r * NP:(r + 1) * NP, :]) for r in range(R4)],
                    small=(fold[:, :, :], al[:, :]))
            al4 = al[:, :].rearrange("p (t r f) -> p t r f", r=R4, f=2 * H)
            fill(m, nc, "f3", [("copy", best[:, :].rearrange("p (b h) -> p b h", h=H), al3[:, :, 0:H]),
                               ("set", m.region[:, 0:NBA * AW], 0.0)] +
                 [("store", m.source_table[r * NP:(r + 1) * NP, :].rearrange("(t p) h -> p t h", p=P), al4[:, :, r, 0:H])
                  for r in range(R4)])
            logits, targets = edge[:, 0:NCA * H], edge[:, NCA * H:NCA * 3 * H]
            segment_max(m, nc, "m3", NCA, NBA, laneA, m.ix_src4, m.source_table, logits, m.maxA, best)
            attention_table(m, nc, "t3", NBA, al3[:, :, H:2 * H], best[:, :].rearrange("p (b h) -> p b h", h=H), tt,
                            own=(al3[:, :, 0:H], m.self_w[:, :].rearrange("p (b h) -> p b h", h=H)))
            target_values(m, nc, "v3", NCA, NBA, m.ra, m.maxA, tt, targets)
            weights = m.region[:, NBA * (AW + 2 * H):NBA * (AW + 2 * H) + NCA * H]
            edge_weights(m, nc, "e3", NCA, logits, targets, weights)
            col = lambda c, h=0, n=H: weights[:, bass.ds(c * H + h, n)]
            head = lambda c, h, n=1: col(c, h, n)
            aggregate(m, nc, "a3", NCA, NBA, m.ix_src4, laneA, m.xt_table, m.accA, head_weight=head, sums=col)
        fuse_relations(m, nc)
    return m


_NAMES = dict(x="x_in", src="src", dst="dst", edge_type_4="type4", edge_type_8="type8", edge_weight="weight",
              L0_gnn_W="w0", L0_gnn_a="a0", L1_gnn_W="w1", L1_gnn_b="b1", L3_gnn_W="w3",
              L3_gnn_att_src="att_src", L3_gnn_att_dst="att_dst", L3_gnn_bias="bias3", L3_gnn_sem_W1="sem_w1",
              L3_gnn_sem_b1="sem_b1", L3_gnn_sem_W2="sem_w2",
              L2_gnn_basis0="basis0", L2_gnn_comp0="comp0", L2_gnn_bias0="bias0", L2_gnn_loop0="loop0",
              L2_gnn_basis1="basis1", L2_gnn_comp1="comp1", L2_gnn_bias1="bias1", L2_gnn_loop1="loop1")


def lay_out(inputs):
    import numpy as np
    arrays = {mine: np.ascontiguousarray(inputs[name]) for name, mine in _NAMES.items()}
    arrays["base_wT"] = np.ascontiguousarray(np.transpose(np.asarray(inputs["L0_gnn_base_w"])))
    arrays["spline_wT"] = np.ascontiguousarray(np.transpose(np.asarray(inputs["L0_gnn_spline_w"]), (2, 1, 0)))
    return arrays


def program(nc, arrays, **how):
    a = {n: nc.dram_tensor(f"in_{n}", v.shape, mybir.dt.from_np(v.dtype), kind="ExternalInput").ap()
         for n, v in arrays.items()}
    a["out"] = nc.dram_tensor("out_dram", (N, D), F32, kind="ExternalOutput").ap()
    for one, both in (("basis", "basis"), ("comp", "comps"), ("bias", "biases"), ("loop", "loops")):
        a[both] = (a[one + "0"], a[one + "1"])
    return gnn_kernel(nc, a, **how)


def kernel(**inputs):
    import concourse.bacc as _bacc
    from concourse.bass_utils import run_bass_kernel_spmd as _run

    arrays = lay_out(inputs)
    nc = _bacc.Bacc("TRN2", target_bir_lowering=False, num_devices=1)
    program(nc, arrays)
    r = _run(nc, [{f"in_{n}": v for n, v in arrays.items()}], core_ids=[0])
    return r.results[0]["out_dram"]
```

```python
import math
from contextlib import ExitStack

import concourse.bass as bass
from concourse import mybir

F32 = mybir.dt.float32
I32 = mybir.dt.int32
U32 = mybir.dt.uint32
BF16 = mybir.dt.bfloat16
ALU = mybir.AluOpType
ACT = mybir.ActivationFunctionType
AX = mybir.AxisListType

P = 128
N = 1250
D = 512
KC = D // P
T = -(-N // P)
NP = T * P
LAST = N - (T - 1) * P
E = 21250
EP, EC = 125, 170
R4, R8, BASES = 4, 8, 4
H, C = 8, 64
SEM_D = 256
NBA, NBB = T * R4, T
G = 8
PSLOTS = 4
def chunks(buckets):
    return -(-((E + buckets * (P - 1)) // P) // G) * G
NCA, NCB = chunks(NBA), chunks(NBB)
AW = D + H
REC = 8
BIG = 1.0e30
EPS = 1e-5
F = 4
SC = 5
assert EP * EC == E and EC % (2 * SC) == 0 and NCA % (4 * F) == 0 and NCB % (4 * F) == 0

A_LANE, A_SRC, A_SRC8, A_SRC4, A_WEIGHT = range(5)
B_LANE, B_DST, B_DST_LANE, B_DST_TILE = range(4)


def wait_at_least(eng, sem, value):
    if not (isinstance(value, int) and value <= 0):
        eng.wait_ge(sem, value)


def peeled(eng, n, body):
    body(0)
    if n > 2:
        with eng.Fori(1, n - 1) as i:
            body(i)
    body(n - 1)


class Core:
    pass


def semaphore(m, nc, name):
    m.sems.append(nc.alloc_semaphore(name))
    return m.sems[-1]


def recycle_semaphores(m, nc):
    nc.clear_and_free_semaphores(m.sems)
    m.sems = []
    nc.all_engine_barrier()


class Chain:

    def __init__(self, eng, sem):
        self.eng, self.sem, self.base, self.k = eng, sem, 0, 0

    def link(self, ins):
        self.k += 1
        ins.then_inc(self.sem, 1)
        self.eng.wait_ge(self.sem, self.base + self.k)

    def rounds(self, n, per, body, loop=peeled):
        start = self.base + self.k

        def one(i):
            self.base, self.k = start + i * per, 0
            body(i)
            assert self.k == per, (self.k, per)

        loop(self.eng, n, one)
        self.base, self.k = start + n * per, 0


def alone(eng, m):
    eng.sem_inc(m.gate, 1)


def offsets(nc, engine, places, c, n, last):
    _, values = nc.values_load_multi_w_load_instructions(
        places[0:1, bass.ds(c, n)], engines=(engine,), min_val=0, max_val=last,
        skip_runtime_bounds_check_because="the places are worked out from bucket numbers, which are bounded")
    return values


class Scatter:

    def __init__(self, m, nc, name, table):
        sem = lambda n: semaphore(m, nc, f"{name}_{n}")
        self.m, self.table = m, table
        self.copied, self.sorted_in = sem("copied"), sem("sorted_in")
        self.scattered = [sem(f"scattered{u}") for u in range(2)]

    def run(self, pool, pos, rec):
        m = self.m

        def body(i):
            for u in range(2):
                q = 2 * i + u
                wait_at_least(pool, self.scattered[u], i * (16 * SC))
                if not isinstance(i, int):
                    alone(pool, m)
                pool.tensor_copy(m.pos_blk[:, u, :], pos[:, bass.ds(q * SC, SC)]).then_inc(self.copied, 1)
                pool.tensor_copy(m.rec_blk[:, u, :, :], rec[:, bass.ds(q * SC, SC), :]).then_inc(self.copied, 1)
                pool.wait_ge(self.copied, 2 * q + 2)
                alone(pool, m)
                for j in range(SC):
                    pool.indirect_dma_start(
                        out=self.table, out_offset=bass.IndirectOffsetOnAxis(ap=m.pos_blk[:, u, j:j + 1], axis=0),
                        in_=m.rec_blk[:, u, j, :], in_offset=None).then_inc(self.scattered[u], 16)
        peeled(pool, EC // (2 * SC), body)

    def load(self, sp, dst):
        for s in self.scattered:
            sp.wait_ge(s, 8 * EC)
        sp.dma_start(dst[:, :, :], self.table.rearrange("(p c) f -> p c f", p=P)).then_inc(self.sorted_in, 16)
        sp.wait_ge(self.sorted_in, 16)


def prepare(m, nc):
    ks = ExitStack()
    with ks:
        sem = lambda n: semaphore(m, nc, n)
        used = [0]

        def sb(rows, shape, d=F32):
            n = math.prod(shape)
            piece = m.own[0:rows, used[0]:used[0] + n]
            used[0] += n
            if d is not F32:
                piece = piece.bitcast(d)
            if len(shape) == 1:
                return piece
            names = " ".join("abc"[:len(shape)])
            return piece.rearrange(f"p ({names}) -> p {names}", **dict(zip("abc", shape)))

        blank = sb(P, [NCA, REC])
        ints, tmp_i = sb(EP, [4, EC], I32), sb(EP, [2, EC], I32)
        w_in = sb(EP, [EC])
        key, pos = sb(EP, [3, EC]), sb(EP, [3, EC])
        recs, posus = (m.rec_inA, m.rec_inB), (m.posA, m.posB, m.posC)
        iota_b, iota_c = sb(P, [NBA]), sb(1, [NCA])
        tri = sb(P, [P])
        row_end, row_tot = sb(EP, [NBA]), sb(EP, [NBA])
        nchunk, nchunk_i = sb(P, [NBA]), sb(P, [NBA], I32)
        end_chunk, off = sb(P, [NBA]), sb(EP, [NBA])
        cnt = sb(1, [NCA])
        x_in, loaded, made, counted = sem("x_in"), sem("loaded"), sem("made"), sem("counted")
        totals, blanked, blank_set = sem("totals"), sem("blanked"), sem("blank_set")
        dve = sem("dve_prepare")
        ind = m.region[0:EP, 0:NBA * EC]
        cum = m.region[0:EP, NBA * EC:2 * NBA * EC]
        mapw = m.region[0:1, 0:NCA * NBA]

        def bucket_ends(pe, turn, o):
            nb = (NBA, NBB, NBB)[o]
            pe.wait_ge(totals, turn + 1)
            pe.matmul(m.ps[0:EP, 2 * o, 0:nb], tri[0:EP, 0:EP], row_tot[:, 0:nb], start=True, stop=True)
            pe.matmul(m.ps[:, 2 * o + 1, 0:nb], m.ones[0:EP, :], row_tot[:, 0:nb],
                      start=True, stop=True).then_inc(counted, 1)

        def positions(v, turn, o):
            nb, nch = ((NBA, NCA), (NBB, NCB), (NBB, NCB))[o]
            ch = Chain(v, sem(f"placing{o}"))
            link = ch.link
            cube = lambda a: a[:, 0:nb * EC].rearrange("p (b c) -> p b c", b=nb)
            mine = iota_b[0:EP, 0:nb]
            link(v.tensor_tensor(cube(ind), key[:, o, :].unsqueeze(1).broadcast_to([EP, nb, EC]),
                                 mine.unsqueeze(2).broadcast_to([EP, nb, EC]), op=ALU.is_equal))
            link(v.tensor_tensor_scan(cum[:, 0:nb * EC], ind[:, 0:nb * EC],
                                      m.zeros[0:EP, 0:1].broadcast_to([EP, nb * EC]), 0.0,
                                      ALU.add, ALU.add))
            link(v.tensor_copy(row_end[:, 0:nb], cube(cum)[:, :, EC - 1]))
            link(v.tensor_copy(row_tot[:, 0:1], row_end[:, 0:1]))
            v.tensor_tensor(row_tot[:, 1:nb], row_end[:, 1:nb], row_end[:, 0:nb - 1],
                            op=ALU.subtract).then_inc(totals, 1)
            v.wait_ge(counted, turn + 1)
            link(v.tensor_scalar(nchunk[:, 0:nb], m.ps[:, 2 * o + 1, 0:nb], 127.0, None, ALU.add))
            link(v.tensor_copy(nchunk_i[:, 0:nb], nchunk[:, 0:nb]))
            link(v.tensor_scalar(nchunk_i[:, 0:nb], nchunk_i[:, 0:nb], 7, None, ALU.arith_shift_right))
            link(v.tensor_copy(nchunk[:, 0:nb], nchunk_i[:, 0:nb]))
            link(v.tensor_tensor_scan(end_chunk[:, 0:nb], nchunk[:, 0:nb],
                                      m.zeros[:, 0:1].broadcast_to([P, nb]), 0.0, ALU.add, ALU.add))
            link(v.tensor_tensor(nchunk[:, 0:nb], end_chunk[:, 0:nb], nchunk[:, 0:nb], op=ALU.subtract))
            link(v.tensor_scalar(off[:, 0:nb], nchunk[0:EP, 0:nb], float(P), -1.0, ALU.mult, ALU.add))
            link(v.tensor_tensor(off[:, 0:nb], off[:, 0:nb], m.ps[0:EP, 2 * o, 0:nb], op=ALU.add))
            link(v.tensor_tensor(off[:, 1:nb], off[:, 1:nb], row_end[:, 0:nb - 1], op=ALU.subtract))
            link(v.tensor_tensor(cube(cum), cube(cum), off[:, 0:nb].unsqueeze(2).broadcast_to([EP, nb, EC]),
                                 op=ALU.add))
            link(v.tensor_tensor(cube(cum), cube(cum), cube(ind), op=ALU.mult))
            link(v.tensor_reduce(pos[:, o, :], cube(cum).rearrange("p b c -> p c b"), AX.X, ALU.add))
            link(v.tensor_copy(tmp_i[:, 0, :], pos[:, o, :]))
            link(v.tensor_scalar(tmp_i[:, 1, :], tmp_i[:, 0, :], 127, None, ALU.bitwise_and))
            link(v.tensor_scalar(tmp_i[:, 0, :], tmp_i[:, 0, :], 7, None, ALU.arith_shift_right))
            link(v.scalar_tensor_tensor(out=posus[o][:, :], in0=tmp_i[:, 1, :], scalar=float(nch),
                                        in1=tmp_i[:, 0, :], op0=ALU.mult, op1=ALU.add))
            grid = mapw[:, 0:nch * nb].rearrange("p (c b) -> p c b", b=nb)
            link(v.tensor_tensor(grid, end_chunk[0:1, 0:nb].unsqueeze(1).broadcast_to([1, nch, nb]),
                                 iota_c[:, 0:nch].unsqueeze(2).broadcast_to([1, nch, nb]), op=ALU.is_le))
            link(v.tensor_reduce(cnt[:, 0:nch], grid, AX.X, ALU.add))
            link(v.tensor_scalar(cnt[:, 0:nch], cnt[:, 0:nch], float(nb - 1), None, ALU.min))
            if o == 0:
                link(v.tensor_scalar(m.accA[:, :], cnt[:, 0:nch], float(AW), None, ALU.mult))
                link(v.tensor_scalar(m.maxA[:, :], cnt[:, 0:nch], float(H), None, ALU.mult))
            elif o == 2:
                link(v.tensor_scalar(m.accC[:, :], cnt[:, 0:nch], float(AW), None, ALU.mult))
            else:
                link(v.tensor_scalar(m.accB[:, :], cnt[:, 0:nch], float(AW), None, ALU.mult))
                link(v.tensor_scalar(m.maxB[:, :], cnt[:, 0:nch], float(H), None, ALU.mult))

        with nc.Block() as block:

            @block.sync
            def _(sp):
                for f, a in enumerate((m.src, m.dst, m.type4, m.type8)):
                    sp.dma_start(ints[:, f, :], a.rearrange("(p c) -> p c", p=EP)).then_inc(loaded, 16)
                sp.dma_start(w_in[:, :], m.weight.rearrange("(p c) -> p c", p=EP)).then_inc(loaded, 16)
                full = m.x_in[0:(T - 1) * P, :].rearrange("(t p) d -> p t d", p=P)
                sp.wait_ge(made, 1)
                sp.dma_start(m.x[:, 0:(T - 1) * D].rearrange("p (t d) -> p t d", d=D), full).then_inc(x_in, 16)
                sp.dma_start(m.x[0:LAST, (T - 1) * D:T * D], m.x_in[(T - 1) * P:N, :]).then_inc(x_in, 16)
                sp.wait_ge(blank_set, 1)
                sp.dma_start(m.recA.rearrange("(p c) f -> p c f", p=P), blank[:, :, :]).then_inc(blanked, 16)
                sp.dma_start(m.recB.rearrange("(p c) f -> p c f", p=P), blank[:, 0:NCB, :]).then_inc(blanked, 16)
                sp.dma_start(m.recC.rearrange("(p c) f -> p c f", p=P), blank[:, 0:NCB, :]).then_inc(blanked, 16)
                sp.wait_ge(x_in, 32)

            @block.gpsimd
            def _(pool):
                pool.memset(m.x[:, (T - 1) * D:T * D], 0.0).then_inc(made, 1)
                pool.iota(iota_b[:, :], [[1, NBA]], base=0, channel_multiplier=0,
                          allow_small_or_imprecise_dtypes=True).then_inc(made, 1)
                pool.iota(iota_c[:, :], [[1, NCA]], base=0, channel_multiplier=0,
                          allow_small_or_imprecise_dtypes=True).then_inc(made, 1)
                pool.iota(m.lanes[:, :], [[1, P]], base=0, channel_multiplier=0,
                          allow_small_or_imprecise_dtypes=True).then_inc(made, 1)
                pool.memset(m.ones[:, :], 1.0).then_inc(made, 1)
                pool.memset(m.ident[:, :], 0.0).then_inc(made, 1)
                pool.wait_ge(made, 6)
                pool.affine_select(out=m.ident[:, :], in_=m.ident[:, :], compare_op=ALU.not_equal, fill=1.0,
                                   base=0, pattern=[[-1, P]], channel_multiplier=1).then_inc(made, 1)
                pool.affine_select(out=tri[:, :], in_=m.ones[:, :], compare_op=ALU.is_gt, fill=0.0,
                                   base=0, pattern=[[1, P]], channel_multiplier=-1).then_inc(made, 1)
                pool.wait_ge(blanked, 48)

            @block.tensor
            def _(pe):
                pe.wait_ge(made, 8)
                bucket_ends(pe, 0, 1)

            @block.vector
            def _(v):
                ch = Chain(v, dve)
                link = ch.link
                link(v.memset(blank[:, :, :], 0.0))
                v.memset(blank[:, :, 0:1], -1.0).then_inc(blank_set, 1)
                for j in range(R8 + 3):
                    last = v.memset(m.consts[:, j:j + 1], m.const_values[j])
                link(last)
                link(v.memset(m.zeros[:, :], 0.0))
                link(v.memset(recs[0][:, :, :], 0.0))
                v.wait_ge(loaded, 16 * 5)
                v.wait_ge(made, 8)
                link(v.tensor_copy(recs[0][:, :, A_WEIGHT], w_in[:, :]))
                link(v.memset(recs[1][:, :, :], 0.0))
                src, dst, ty4, ty8 = (ints[:, f, :] for f in range(4))
                link(v.tensor_scalar(tmp_i[:, 0, :], dst, 7, None, ALU.arith_shift_right))
                link(v.scalar_tensor_tensor(out=key[:, 0, :], in0=tmp_i[:, 0, :], scalar=float(R4), in1=ty4,
                                            op0=ALU.mult, op1=ALU.add))
                link(v.tensor_copy(recs[1][:, :, B_DST_TILE], tmp_i[:, 0, :]))
                link(v.tensor_copy(key[:, 2, :], tmp_i[:, 0, :]))
                link(v.tensor_scalar(tmp_i[:, 1, :], src, 7, None, ALU.arith_shift_right))
                link(v.tensor_copy(key[:, 1, :], tmp_i[:, 1, :]))
                link(v.tensor_scalar(tmp_i[:, 0, :], dst, 127, None, ALU.bitwise_and))
                link(v.tensor_scalar(tmp_i[:, 1, :], src, 127, None, ALU.bitwise_and))
                link(v.tensor_copy(recs[0][:, :, A_LANE], tmp_i[:, 0, :]))
                link(v.tensor_copy(recs[1][:, :, B_LANE], tmp_i[:, 1, :]))
                link(v.tensor_copy(recs[0][:, :, A_SRC], src))
                link(v.tensor_copy(recs[1][:, :, B_DST], dst))
                link(v.tensor_copy(recs[1][:, :, B_DST_LANE], tmp_i[:, 0, :]))
                link(v.scalar_tensor_tensor(out=recs[0][:, :, A_SRC8], in0=ty8, scalar=float(NP), in1=src,
                                            op0=ALU.mult, op1=ALU.add))
                link(v.scalar_tensor_tensor(out=recs[0][:, :, A_SRC4], in0=ty4, scalar=float(NP), in1=src,
                                            op0=ALU.mult, op1=ALU.add))
                positions(v, 0, 1)

    return positions, bucket_ends


def normalise_setup(m, v, ch, stats, mv, rstd, nbias, root_asked, root_done):
    for t in range(T):
        last = v.bn_stats(stats[:, t * 6:t * 6 + 6], m.x[:, t * D:(t + 1) * D])
    ch.link(last)
    for t in range(T):
        last = v.bn_aggr(mv[:, 2 * t:2 * t + 2], stats[:, 6 * t:6 * t + 6])
    ch.link(last)
    both = mv[:, :].rearrange("p (t k) -> p t k", k=2)
    v.tensor_scalar(rstd[:, :], both[:, :, 1], EPS, None, ALU.add).then_inc(root_asked, 1)
    v.wait_ge(root_done, 1)
    ch.link(v.reciprocal(rstd[:, :], rstd[:, :]))
    ch.link(v.scalar_tensor_tensor(out=nbias[:, :], in0=both[:, :, 0], scalar=-1.0, in1=rstd[:, :],
                                   op0=ALU.mult, op1=ALU.mult))


def project(m, nc, name, h_table=None, tables=(), small=None, beside=None, then_vector=None, then_tensor=None,
            then_sync=None, keep=None):
    n_tab = len(tables)
    outs = [("table", w, d) for w, d in tables]
    if small:
        outs.append(("small", *small))
    Q = 2 * len(outs)
    BANKS = 6
    engine = ["v" if outs[q % len(outs)][0] != "table" or q % 2 else "a" for q in range(Q)] if outs else []
    rank = [engine[:q].count(engine[q]) for q in range(Q)]
    per_round = {e: engine.count(e) for e in "va"}
    QT = 2 * n_tab
    SLOTS = 4

    def before(q, count, lanes):
        if q >= lanes:
            return 0, q - lanes
        return 1, max((z for z in range(count) if z % lanes == q), default=q)

    ks = ExitStack()
    with ks:
        sb = lambda n, s, d=F32: ks.enter_context(nc.sbuf_tensor(f"{name}_{n}", s, d))
        sem = lambda n: semaphore(m, nc, f"{name}_{n}")
        stats = sb("stats", [P, T * 6])
        mv = sb("mv", [P, T * 2])
        rstd = sb("rstd", [P, T])
        nbias = sb("nbias", [P, T])
        root_asked, root_done, norm_set = sem("root_asked"), sem("root_done"), sem("norm_set")
        h_ready, turned, h_turned, multiplied = sem("h_ready"), sem("turned"), sem("h_turned"), sem("multiplied")
        left = {"v": sem("left_v"), "a": sem("left_a")}
        stored = [sem(f"stored{s}") for s in range(SLOTS)]
        h_stored = [sem(f"h_stored{s}") for s in range(2)]
        h_kept = sem("h_kept")
        dve = sem("dve")

        def tile(i, b):
            return i * 2 + b

        def leave(eng, who, i, b):
            for o, out in enumerate(outs):
                q = b * len(outs) + o
                if engine[q] != who:
                    continue
                eng.wait_ge(multiplied, i * Q + q + 1)
                bank = m.ps[:, 2 + q % BANKS, :]
                kind = out[0]
                if kind == "table":
                    qt = b * n_tab + o
                    wait_at_least(eng, stored[qt % SLOTS], (i * (QT // SLOTS) + qt // SLOTS) * 16)
                    if not isinstance(i, int):
                        alone(eng, m)
                    dst = m.stage[:, qt % SLOTS, :]
                    ins = eng.tensor_copy(dst, bank) if who == "v" else eng.activation(dst, bank, ACT.Copy)
                else:
                    if not isinstance(i, int):
                        alone(eng, m)
                    w = out[1].shape[2]
                    ins = eng.tensor_copy(out[2][:, bass.ds(tile(i, b) * w, w)], bank[:, 0:w])
                ins.then_inc(left[who], 1)

        with nc.Block() as block:

            @block.vector
            def _(v):
                ch = Chain(v, dve)
                normalise_setup(m, v, ch, stats, mv, rstd, nbias, root_asked, root_done)
                v.sem_inc(norm_set, 1)

                def copy_hT(t, b):
                    v.wait_ge(turned, t + 1)
                    wait_at_least(v, multiplied, (t - 1) * len(outs))
                    if keep is not None:
                        wait_at_least(v, h_kept, t - 1)
                    v.tensor_copy(m.hT[:, b, 0:KC, :].rearrange("p k n -> p (k n)"), m.ps[:, b, :])\
                     .then_inc(h_turned, 1)

                def pair(i):
                    for b in range(2):
                        t = tile(i, b)
                        if not (isinstance(t, int) and t == T - 1):
                            copy_hT(t + 1, 1 - b)
                        leave(v, "v", i, b)
                if outs:
                    copy_hT(0, 0)
                    peeled(v, T // 2, pair)
                if then_vector:
                    then_vector(v)

            @block.scalar
            def _(a):
                a.wait_ge(root_asked, 1)
                a.activation(rstd[:, :], rstd[:, :], ACT.Sqrt).then_inc(root_done, 1)
                a.wait_ge(norm_set, 1)

                def rows(t, i, b):
                    if outs:
                        wait_at_least(a, turned, t - 1)
                    if h_table is not None:
                        wait_at_least(a, h_stored[b], i * 16)
                    if not isinstance(i, int):
                        alone(a, m)
                    a.activation(m.h[:, b, :], m.x[:, bass.ds(t * D, D)], ACT.Relu,
                                 bias=nbias[:, bass.ds(t, 1)], scale=rstd[:, bass.ds(t, 1)]).then_inc(h_ready, 1)

                def pair(i):
                    for b in range(2):
                        t = tile(i, b)
                        if not (isinstance(t, int) and t == T - 1):
                            rows(t + 1, i + b, 1 - b)
                        leave(a, "a", i, b)
                        if keep is not None:
                            a.wait_ge(h_turned, t + 1)
                            alone(a, m)
                            a.activation(keep[:, bass.ds(t * D, D)], m.hT[:, b, 0:KC, :].rearrange("p k n -> p (k n)"),
                                         ACT.Copy).then_inc(h_kept, 1)
                rows(0, 0, 0)
                peeled(a, T // 2, pair)

            @block.tensor
            def _(pe):
                def turn(t, b):
                    pe.wait_ge(h_ready, t + 1)
                    wait_at_least(pe, h_turned, t - 1)
                    for k in range(KC):
                        last = pe.transpose(m.ps[:, b, k * P:(k + 1) * P], m.h[:, b, k * P:(k + 1) * P], m.ident[:, :])
                    last.then_inc(turned, 1)

                def pair(i):
                    for b in range(2):
                        t = tile(i, b)
                        if not (isinstance(t, int) and t == T - 1):
                            turn(t + 1, 1 - b)
                        pe.wait_ge(h_turned, t + 1)
                        for o, out in enumerate(outs):
                            q = b * len(outs) + o
                            back, z = before(q, Q, BANKS)
                            if not (isinstance(i, int) and i < back):
                                e = engine[z]
                                pe.wait_ge(left[e], (i - back) * per_round[e] + rank[z] + 1)
                            w = out[1]
                            for k in range(KC):
                                last = pe.matmul(m.ps[:, 2 + q % BANKS, 0:w.shape[2]], m.hT[:, b, k, :],
                                                 w[:, k, :], start=k == 0, stop=k == KC - 1)
                            last.then_inc(multiplied, 1)
                if outs:
                    turn(0, 0)
                    peeled(pe, T // 2, pair)
                if then_tensor:
                    then_tensor(pe)

            @block.sync
            def _(sp):
                def pair(i):
                    for b in range(2):
                        t = tile(i, b)
                        if h_table is not None:
                            sp.wait_ge(h_ready, t + 1)
                            sp.dma_start(h_table[bass.ds(t * P, P), :], m.h[:, b, :]).then_inc(h_stored[b], 16)
                        for o in range(n_tab):
                            q, qt = b * len(outs) + o, b * n_tab + o
                            e = engine[q]
                            sp.wait_ge(left[e], i * per_round[e] + rank[q] + 1)
                            sp.dma_start(outs[o][2][bass.ds(t * P, P), :], m.stage[:, qt % SLOTS, :])\
                              .then_inc(stored[qt % SLOTS], 16)
                if h_table is not None or n_tab:
                    peeled(sp, T // 2, pair)
                if h_table is not None:
                    for s in h_stored:
                        sp.wait_ge(s, 16 * (T // 2))
                if n_tab:
                    for s in stored:
                        sp.wait_ge(s, 16 * (T // 2) * (QT // SLOTS))
                if then_sync:
                    then_sync(sp)

            if beside:
                @block.gpsimd
                def _(pool):
                    beside(pool)


def target_values(m, nc, name, n_chunks, buckets, records, places, table, out, beside=None):
    W2 = 2 * H
    W3 = 3 * W2
    ks = ExitStack()
    with ks:
        sb = lambda n, s, d=F32: ks.enter_context(nc.sbuf_tensor(f"{name}_{n}", s, d))
        sem = lambda n: semaphore(m, nc, f"{name}_{n}")
        HS = 4
        onehot = m.stage[:, 0:2, :].rearrange("p s d -> p (s d)").bitcast(BF16).rearrange("p (u w) -> p u w", u=HS)
        flipped = m.stage[:, 2, :].bitcast(BF16).rearrange("p (u w) -> p u w", u=2)
        drawn = m.stage[:, 3, 0:2 * F * W3].rearrange("p (u w) -> p u w", u=2)
        partial = m.stage[:, 3, 2 * F * W3:2 * F * (W3 + W2)].rearrange("p (u w) -> p u w", u=2)
        parts = sb("parts", [P, buckets, 3, W2], BF16)
        ident = sb("ident", [P, P], BF16)
        rest = m.h[:, :, :].rearrange("p s d -> p (s d)")[:, 0:buckets * W2].rearrange("p (b f) -> p b f", f=W2)
        hot, turned, copied, valued, taken = (sem(n) for n in ("hot", "turned", "copied", "valued", "taken"))
        split, summed, whole = sem("split"), sem("summed"), sem("whole")
        dve = sem("dve")
        rounds = n_chunks // (HS * F)
        flat = parts[:, :, :, :].rearrange("p b s f -> p (b s f)")

        with nc.Block() as block:

            @block.vector
            def _(v):
                ch = Chain(v, dve)
                v.tensor_copy(ident[:, :], m.ident[:, :])
                ch.link(v.tensor_copy(parts[:, :, 0, :], table))
                ch.link(v.tensor_tensor(rest, table, parts[:, :, 0, :], op=ALU.subtract))
                ch.link(v.tensor_copy(parts[:, :, 1, :], rest))
                ch.link(v.tensor_tensor(rest, rest, parts[:, :, 1, :], op=ALU.subtract))
                v.tensor_copy(parts[:, :, 2, :], rest).then_inc(split, 1)

                def heat(q, u):
                    v.tensor_tensor(onehot[:, u, :].rearrange("p (f n) -> p f n", f=F),
                                    m.lanes[:, :].unsqueeze(1).broadcast_to([P, F, P]),
                                    records[:, bass.ds(q * F, F), A_LANE:A_LANE + 1].broadcast_to([P, F, P]),
                                    op=ALU.is_equal).then_inc(hot, 1)
                for u in range(HS):
                    heat(u, u)

                def body(i):
                    for w in range(HS):
                        q, u = HS * i + w, w % 2
                        v.wait_ge(taken, q + 1)
                        part = lambda n: drawn[:, u, :].rearrange("p (f s w) -> p f s w", f=F, s=3)[:, :, n, :]
                        pair = partial[:, u, :].rearrange("p (f w) -> p f w", f=F)
                        v.tensor_tensor(pair, part(0), part(1), op=ALU.add).then_inc(summed, 1)
                        if not (isinstance(q, int) and q + HS >= HS * rounds):
                            v.wait_ge(turned, q + 1)
                            heat(q + HS, w)
                        v.wait_ge(summed, q + 1)
                        alone(v, m)
                        v.tensor_tensor(out[:, bass.ds(q * (F * W2), F * W2)].rearrange("p (f w) -> p f w", f=F),
                                        pair, part(2), op=ALU.add).then_inc(whole, 1)
                peeled(v, rounds, body)

            if beside:
                @block.gpsimd
                def _(pool):
                    beside(pool)

            @block.scalar
            def _(a):
                def turn(q, u):
                    a.wait_ge(turned, q + 1)
                    wait_at_least(a, valued, q - 1)
                    a.activation(flipped[:, u, :], m.ps[:, u, :], ACT.Copy).then_inc(copied, 1)

                turn(0, 0)

                def body(i):
                    for w in range(HS):
                        q, u = HS * i + w, w % 2
                        if not (isinstance(q, int) and q + 1 >= HS * rounds):
                            turn(q + 1, 1 - u)
                        a.wait_ge(valued, q + 1)
                        wait_at_least(a, whole, q - 1)
                        a.activation(drawn[:, u, :], m.ps[:, 2 + u, 0:F * W3], ACT.Copy).then_inc(taken, 1)
                peeled(a, rounds, body)

            @block.tensor
            def _(pe):
                def turn(q, w):
                    u = w % 2
                    pe.wait_ge(hot, q + 1)
                    wait_at_least(pe, copied, q - 1)
                    for f in range(F):
                        last = pe.matmul(m.ps[:, u, f * P:(f + 1) * P], onehot[:, w, f * P:(f + 1) * P],
                                         ident[:, :], start=True, stop=True)
                    last.then_inc(turned, 1)

                pe.wait_ge(split, 1)
                turn(0, 0)

                def body(i):
                    for w in range(HS):
                        q, u = HS * i + w, w % 2
                        at = offsets(nc, mybir.EngineType.PE, places, q * F, F, (buckets - 1) * H)
                        if not (isinstance(q, int) and q + 1 >= HS * rounds):
                            turn(q + 1, (w + 1) % HS)
                        pe.wait_ge(copied, q + 1)
                        wait_at_least(pe, taken, q - 1)
                        for f in range(F):
                            last = pe.matmul(m.ps[:, 2 + u, f * W3:(f + 1) * W3], flipped[:, u, f * P:(f + 1) * P],
                                             flat[:, bass.ds(at[f] * 6, W3)], start=True, stop=True)
                        last.then_inc(valued, 1)
                peeled(pe, rounds, body)


class Gather:

    def __init__(self, m, nc, name, index, table, ring, width):
        self.m, self.index, self.table, self.ring, self.width = m, index, table, ring, width
        self.indexed = semaphore(m, nc, f"{name}_indexed")
        self.fetched = [semaphore(m, nc, f"{name}_fetched{g}") for g in range(G)]

    def feed(self, a, c, g):
        a.copy(self.m.ib[:, g:g + 1], self.index[:, bass.ds(c, 1)]).then_inc(self.indexed, 1)

    def fetch(self, pool, c, g):
        pool.wait_ge(self.indexed, c + 1)
        alone(pool, self.m)
        pool.indirect_dma_start(out=self.ring[:, g, 0:self.width], out_offset=None, in_=self.table,
                                in_offset=bass.IndirectOffsetOnAxis(ap=self.m.ib[:, g:g + 1], axis=0))\
            .then_inc(self.fetched[g], 16)


def look_up(m, nc, name, n_chunks, records, table, raw, tile_hot, out):
    W3 = 3 * T
    HS = 4
    ks = ExitStack()
    with ks:
        sb = lambda n, s, d=F32: ks.enter_context(nc.sbuf_tensor(f"{name}_{n}", s, d))
        sem = lambda n: semaphore(m, nc, f"{name}_{n}")
        onehot = m.stage[:, 0:2, :].rearrange("p s d -> p (s d)").bitcast(BF16).rearrange("p (u w) -> p u w", u=HS)
        flipped = m.stage[:, 2, :].bitcast(BF16).rearrange("p (u w) -> p u w", u=2)
        parts = sb("parts", [P, 3, T], BF16)
        ident = sb("ident", [P, P], BF16)
        rest = sb("rest", [P, T])
        hot, turned, copied, valued, drawn, split, dve = (
            sem(n) for n in ("hot", "turned", "copied", "valued", "drawn", "split", "dve"))
        rounds = n_chunks // (HS * F)

        with nc.Block() as block:

            @block.vector
            def _(v):
                ch = Chain(v, dve)
                v.tensor_copy(ident[:, :], m.ident[:, :])
                ch.link(v.tensor_copy(parts[:, 0, :], table))
                ch.link(v.tensor_tensor(rest[:, :], table, parts[:, 0, :], op=ALU.subtract))
                ch.link(v.tensor_copy(parts[:, 1, :], rest[:, :]))
                ch.link(v.tensor_tensor(rest[:, :], rest[:, :], parts[:, 1, :], op=ALU.subtract))
                v.tensor_copy(parts[:, 2, :], rest[:, :]).then_inc(split, 1)

                def heat(q, w):
                    v.tensor_tensor(onehot[:, w, :].rearrange("p (f n) -> p f n", f=F),
                                    m.lanes[:, :].unsqueeze(1).broadcast_to([P, F, P]),
                                    records[:, bass.ds(q * F, F), B_DST_LANE:B_DST_LANE + 1].broadcast_to([P, F, P]),
                                    op=ALU.is_equal).then_inc(hot, 1)

                for w in range(HS):
                    heat(w, w)

                def body(i):
                    for w in range(HS):
                        q = HS * i + w
                        if not (isinstance(q, int) and q + HS >= HS * rounds):
                            v.wait_ge(turned, q + 1)
                            heat(q + HS, w)
                peeled(v, rounds, body)
                tiles = tile_hot.rearrange("p (c t) -> p c t", t=T)
                v.tensor_tensor(tiles, m.lanes[:, 0:T].unsqueeze(1).broadcast_to([P, n_chunks, T]),
                                records[:, 0:n_chunks, B_DST_TILE:B_DST_TILE + 1].broadcast_to([P, n_chunks, T]),
                                op=ALU.is_equal)
                v.wait_ge(drawn, HS * rounds)
                part = lambda n: raw.rearrange("p (c s t) -> p c s t", s=3, t=T)[:, :, n, :]
                ch.link(v.tensor_tensor(part(0), part(0), part(1), op=ALU.add))
                ch.link(v.tensor_tensor(part(0), part(0), part(2), op=ALU.add))
                ch.link(v.tensor_tensor(part(0), part(0), tiles, op=ALU.mult))
                ch.link(v.tensor_reduce(out, part(0), AX.X, ALU.add))

            @block.scalar
            def _(a):
                def turn(q, u):
                    a.wait_ge(turned, q + 1)
                    wait_at_least(a, valued, q - 1)
                    a.activation(flipped[:, u, :], m.ps[:, u, :], ACT.Copy).then_inc(copied, 1)

                turn(0, 0)

                def body(i):
                    for w in range(HS):
                        q, u = HS * i + w, w % 2
                        if not (isinstance(q, int) and q + 1 >= HS * rounds):
                            turn(q + 1, 1 - u)
                        a.wait_ge(valued, q + 1)
                        alone(a, m)
                        a.activation(raw[:, bass.ds(q * (F * W3), F * W3)], m.ps[:, 2 + u, 0:F * W3], ACT.Copy)\
                         .then_inc(drawn, 1)
                peeled(a, rounds, body)

            @block.tensor
            def _(pe):
                def turn(q, w):
                    pe.wait_ge(hot, q + 1)
                    wait_at_least(pe, copied, q - 1)
                    for f in range(F):
                        last = pe.matmul(m.ps[:, w % 2, f * P:(f + 1) * P], onehot[:, w, f * P:(f + 1) * P],
                                         ident[:, :], start=True, stop=True)
                    last.then_inc(turned, 1)

                pe.wait_ge(split, 1)
                turn(0, 0)

                def body(i):
                    for w in range(HS):
                        q, u = HS * i + w, w % 2
                        if not (isinstance(q, int) and q + 1 >= HS * rounds):
                            turn(q + 1, (w + 1) % HS)
                        pe.wait_ge(copied, q + 1)
                        wait_at_least(pe, drawn, q - 1)
                        for f in range(F):
                            last = pe.matmul(m.ps[:, 2 + u, f * W3:(f + 1) * W3], flipped[:, u, f * P:(f + 1) * P],
                                             parts[:, :, :].rearrange("p s t -> p (s t)"), start=True, stop=True)
                        last.then_inc(valued, 1)
                peeled(pe, rounds, body)


def segment_max_one(m, nc, name, n_chunks, buckets, records, logits, places, best):
    HS = 4
    ks = ExitStack()
    with ks:
        sb = lambda n, s, d=F32: ks.enter_context(nc.sbuf_tensor(f"{name}_{n}", s, d))
        sem = lambda n: semaphore(m, nc, f"{name}_{n}")
        other = m.rows[:, 0:HS, :]
        marked = m.rows[:, HS:2 * HS, :]
        chunk_best = sb("chunk_best", [P, HS, F])
        parted, squared, filled, turned, reduced, taken, dve = (
            sem(n) for n in ("parted", "squared", "filled", "turned", "reduced", "taken", "dve"))
        rounds = n_chunks // (HS * F)

        with nc.Block() as block:

            @block.gpsimd
            def _(pool):
                def body(i):
                    for w in range(HS):
                        q = HS * i + w
                        wait_at_least(pool, filled, q + 1 - HS)
                        if not isinstance(i, int):
                            alone(pool, m)
                        pool.tensor_tensor(other[:, w, :].rearrange("p (f n) -> p f n", f=F),
                                           m.lanes[:, :].unsqueeze(1).broadcast_to([P, F, P]),
                                           records[:, bass.ds(q * F, F), B_LANE:B_LANE + 1].broadcast_to([P, F, P]),
                                           op=ALU.subtract).then_inc(parted, 1)
                peeled(pool, rounds, body)

            @block.scalar
            def _(a):
                def square(q, w):
                    a.wait_ge(parted, q + 1)
                    a.activation(other[:, w, :], other[:, w, :], ACT.Square).then_inc(squared, 1)

                square(0, 0)

                def body(i):
                    for w in range(HS):
                        q = HS * i + w
                        if not (isinstance(q, int) and q + 1 >= HS * rounds):
                            square(q + 1, (w + 1) % HS)
                        a.wait_ge(squared, q + 1)
                        wait_at_least(a, turned, q + 1 - HS)
                        alone(a, m)
                        for f in range(F):
                            last = a.activation(marked[:, w, f * P:(f + 1) * P], other[:, w, f * P:(f + 1) * P],
                                                ACT.Identity, scale=-BIG, bias=logits[:, bass.ds((q * F + f) * H, 1)])
                        last.then_inc(filled, 1)
                peeled(a, rounds, body)

            @block.vector
            def _(v):
                def body(i):
                    for w in range(HS):
                        q = HS * i + w
                        v.wait_ge(turned, q + 1)
                        v.tensor_reduce(chunk_best[:, w, :], m.ps[:, w, :].rearrange("p (f e) -> p f e", f=F),
                                        AX.X, ALU.max).then_inc(reduced, 1)
                        at = offsets(nc, mybir.EngineType.DVE, places, q * F, F, (buckets - 1) * H)
                        v.wait_ge(reduced, q + 1)
                        wait_at_least(v, taken, q)
                        for f in range(F):
                            b = best[:, f, bass.ds(at[f], 1)]
                            last = v.tensor_tensor(b, b, chunk_best[:, w, f:f + 1], op=ALU.max)
                        last.then_inc(taken, 1)
                peeled(v, rounds, body)
                v.wait_ge(taken, HS * rounds)
                ch = Chain(v, dve)
                for f in range(1, F):
                    ch.link(v.tensor_tensor(best[:, 0, :], best[:, 0, :], best[:, f, :], op=ALU.max))

            @block.tensor
            def _(pe):
                def body(i):
                    for w in range(HS):
                        q = HS * i + w
                        pe.wait_ge(filled, q + 1)
                        wait_at_least(pe, reduced, q + 1 - HS)
                        for f in range(F):
                            last = pe.transpose(m.ps[:, w, f * P:(f + 1) * P], marked[:, w, f * P:(f + 1) * P],
                                                m.ident[:, :])
                        last.then_inc(turned, 1)
                peeled(pe, rounds, body)


def segment_max(m, nc, name, n_chunks, buckets, lane, index, table, logits, places, best, h_turned, weights, products):
    ON_ACT, ON_POOL = 5, 2
    AHEAD, LAG = 4, 3
    UNIT = R4 * KC
    bank_of = [idx % 3 for idx in range(UNIT - 1)] + [1]
    back = [next(d for d in range(1, UNIT) if bank_of[idx - d] == bank_of[idx]) for idx in range(UNIT)]
    ks = ExitStack()
    with ks:
        sb = lambda n, s, d=F32: ks.enter_context(nc.sbuf_tensor(f"{name}_{n}", s, d))
        sem = lambda n: semaphore(m, nc, f"{name}_{n}")
        masks = sb("masks", [P, PSLOTS, P])
        marked = m.rows[:, :, :].rearrange("p g d -> p (g d)").rearrange("p (s w) -> p s w", s=PSLOTS)
        ring = sb("ring", [P, G, H])
        chunk_best = sb("chunk_best", [P, 2, H])
        masked, kept, turned, reduced, taken = (sem(n) for n in ("masked", "kept", "turned", "reduced", "taken"))
        filled_a, filled_p, filled_v = (sem(f"filled_{n}") for n in "apv")
        h_in, multiplied = sem("h_in"), sem("multiplied")
        left = {"a": sem("left_a"), "v": sem("left_v")}
        stored = [sem(f"stored{r}") for r in range(R4)]
        rows = Gather(m, nc, name, index, table, ring, H)
        units = n_chunks // UNIT
        assert units > T and UNIT % G == 0
        heads_of = lambda s, lo, hi: marked[:, s, lo * P:hi * P]
        banks = lambda idx: m.ps[:, 2 * bank_of[idx]:2 * bank_of[idx] + 2, :]
        hT = m.hT[:, 0, 0:KC, :]

        def all_units(eng, body):
            def unit(i):
                for idx in range(UNIT):
                    body(i, idx)
            unit(0)
            with eng.Fori(1, T) as i:
                unit(i)
            for i in range(T, units):
                unit(i)

        def leave(eng, who, i, r):
            eng.wait_ge(multiplied, i * R4 + r + 1)
            wait_at_least(eng, stored[r], i * 16)
            dst, src = m.stage[:, r, :], m.ps[:, 6 + r % 2, :]
            (eng.activation(dst, src, ACT.Copy) if who == "a" else eng.tensor_copy(dst, src)).then_inc(left[who], 1)

        with nc.Block() as block:

            @block.sync
            def _(sp):
                def tile(i):
                    for r in range(R4):
                        sp.wait_ge(left["av"[r % 2]], i * 2 + r // 2 + 1)
                        sp.dma_start(products[bass.ds(i * P + r * NP, P), :], m.stage[:, r, :]).then_inc(stored[r], 16)
                peeled(sp, T, tile)
                for q in stored:
                    sp.wait_ge(q, 16 * T)

            @block.gpsimd
            def _(pool):
                for c in range(AHEAD):
                    rows.fetch(pool, c, c % G)

                def body(i, idx):
                    c, g, s = i * UNIT + idx, idx % G, idx % PSLOTS
                    if not (isinstance(c, int) and c + AHEAD >= n_chunks):
                        rows.fetch(pool, c + AHEAD, (g + AHEAD) % G)
                    pool.wait_ge(rows.fetched[g], 16 * ((UNIT // G) * i + idx // G) + 16)
                    wait_at_least(pool, turned, c + 1 - PSLOTS)
                    pool.wait_ge(masked, c + 1)
                    pool.tensor_tensor(
                        heads_of(s, ON_ACT, ON_ACT + ON_POOL).rearrange("p (h n) -> p h n", h=ON_POOL),
                        masks[:, s, :].unsqueeze(1).broadcast_to([P, ON_POOL, P]),
                        ring[:, g, ON_ACT:ON_ACT + ON_POOL].unsqueeze(2).broadcast_to([P, ON_POOL, P]),
                        op=ALU.add).then_inc(filled_p, 1)
                all_units(pool, body)

            @block.scalar
            def _(a):
                def turn_in(i):
                    wait_at_least(a, multiplied, i * R4)
                    if not isinstance(i, int):
                        alone(a, m)
                    a.activation(hT.rearrange("p k n -> p (k n)"), h_turned[:, bass.ds(i * D, D)], ACT.Copy).then_inc(h_in, 1)

                for g in range(G):
                    rows.feed(a, g, g)
                turn_in(0)

                def body(i, idx):
                    c, g, s = i * UNIT + idx, idx % G, idx % PSLOTS
                    a.wait_ge(rows.fetched[g], 16 * ((UNIT // G) * i + idx // G) + 16)
                    wait_at_least(a, turned, c + 1 - PSLOTS)
                    a.wait_ge(masked, c + 1)
                    for h in range(ON_ACT):
                        last = a.activation(heads_of(s, h, h + 1), masks[:, s, :], ACT.Identity,
                                            bias=ring[:, g, h:h + 1])
                    last.then_inc(filled_a, 1)
                    if g % 2:
                        a.copy(logits[:, bass.ds((c - 1) * H, 2 * H)],
                               ring[:, g - 1:g + 1, :].rearrange("p g h -> p (g h)")).then_inc(kept, 1)
                    if not (isinstance(c, int) and (c < LAG or c - LAG + G >= n_chunks)):
                        a.wait_ge(turned, c - LAG + 1)
                        a.wait_ge(kept, i * (UNIT // 2) + (idx - LAG) // 2 + 1)
                        alone(a, m)
                        rows.feed(a, c - LAG + G, (g - LAG) % G)
                    if not (isinstance(i, int) and i >= T):
                        if idx == 3 and not (isinstance(i, int) and i == 0):
                            turn_in(i)
                        if idx in (6, 14):
                            leave(a, "a", i, idx // 6 // 2 * 2)
                all_units(a, body)

            @block.vector
            def _(v):
                def mask(c, s):
                    v.tensor_scalar(masks[:, s, :], m.lanes[:, :], lane(c), -BIG, ALU.not_equal, ALU.mult)\
                     .then_inc(masked, 1)

                def fill_rest(i, idx):
                    c, g = i * UNIT + idx, idx % G
                    v.wait_ge(rows.fetched[g], 16 * ((UNIT // G) * i + idx // G) + 16)
                    v.wait_ge(masked, c + 1)
                    n = H - ON_ACT - ON_POOL
                    v.tensor_tensor(
                        heads_of(g % PSLOTS, H - n, H).rearrange("p (h n) -> p h n", h=n),
                        masks[:, g % PSLOTS, :].unsqueeze(1).broadcast_to([P, n, P]),
                        ring[:, g, H - n:H].unsqueeze(2).broadcast_to([P, n, P]), op=ALU.add).then_inc(filled_v, 1)

                for s in range(PSLOTS):
                    mask(s, s)
                for g in range(2):
                    fill_rest(0, g)
                at = []

                def body(i, idx):
                    c, g, s = i * UNIT + idx, idx % G, idx % PSLOTS
                    v.wait_ge(turned, c + 1)
                    v.tensor_reduce(chunk_best[:, g % 2, :], banks(idx).rearrange("p a b -> p (a b)")
                                    .rearrange("p (h e) -> p h e", e=P), AX.X, ALU.max).then_inc(reduced, 1)
                    if g % F == 0:
                        at[:] = offsets(nc, mybir.EngineType.DVE, places, c, F, (buckets - 1) * H)
                    if not (isinstance(c, int) and c + PSLOTS >= n_chunks):
                        mask(c + PSLOTS, s)
                    if not (isinstance(c, int) and c + 2 >= n_chunks):
                        wait_at_least(v, turned, c + 3 - PSLOTS)
                        fill_rest(i, idx + 2)
                    v.wait_ge(reduced, c + 1)
                    wait_at_least(v, taken, c)
                    b = best[:, bass.ds(at[g % F], H)]
                    v.tensor_tensor(b, b, chunk_best[:, g % 2, :], op=ALU.max).then_inc(taken, 1)
                    if idx == 8 and not (isinstance(i, int) and i >= T):
                        leave(v, "v", i, 1)
                    if idx == 0 and not (isinstance(i, int) and (i == 0 or i > T)):
                        leave(v, "v", i - 1, 3)
                all_units(v, body)

            @block.tensor
            def _(pe):
                def body(i, idx):
                    c, s = i * UNIT + idx, idx % PSLOTS
                    pe.wait_ge(filled_a, c + 1)
                    pe.wait_ge(filled_p, c + 1)
                    pe.wait_ge(filled_v, c + 1)
                    wait_at_least(pe, reduced, c + 1 - back[idx])
                    for h in range(H):
                        last = pe.transpose(m.ps[:, 2 * bank_of[idx] + h // 4, (h % 4) * P:(h % 4 + 1) * P],
                                            heads_of(s, h, h + 1), m.ident[:, :])
                    last.then_inc(turned, 1)
                    if isinstance(i, int) and i >= T:
                        return
                    r, k = idx // KC, idx % KC
                    if idx == 0:
                        pe.wait_ge(h_in, i + 1)
                    if k == 0:
                        wait_at_least(pe, left["av"[r % 2]], i * 2 + r // 2)
                    p = pe.matmul(m.ps[:, 6 + r % 2, :], hT[:, k, :], weights[r][:, k, :], start=k == 0, stop=k == KC - 1)
                    if k == KC - 1:
                        p.then_inc(multiplied, 1)
                all_units(pe, body)


def aggregate(m, nc, name, n_chunks, buckets, index, lane, table, places, weight=None, head_weight=None, sums=None,
              prefetch=()):
    per_head = head_weight is not None
    width = AW if sums else D
    ks = ExitStack()
    with ks:
        sb = lambda n, s, d=F32: ks.enter_context(nc.sbuf_tensor(f"{name}_{n}", s, d))
        sem = lambda n: semaphore(m, nc, f"{name}_{n}")
        onehot = sb("onehot", [P, PSLOTS, P])
        msg = m.stage
        indexed, hot, weighed, summed, added = (sem(n) for n in ("indexed", "hot", "weighed", "summed", "added"))
        fetched = [sem(f"fetched{g}") for g in range(G)]
        rounds = n_chunks // G
        weighed_a = sem("weighed_a")
        ON_ACT = 4
        prefetched = sem("prefetched")

        with nc.Block() as block:

            @block.sync
            def _(sp):
                for dst, src in prefetch:
                    sp.dma_start(dst, src).then_inc(prefetched, 16)
                if prefetch:
                    sp.wait_ge(prefetched, 16 * len(prefetch))

            @block.scalar
            def _(a):
                for g in range(G):
                    a.copy(m.ib[:, g:g + 1], index[:, g:g + 1]).then_inc(indexed, 1)
                if per_head:
                    def body(i):
                        for g in range(G):
                            c, s = i * G + g, g % PSLOTS
                            a.wait_ge(fetched[g], i * 16 + 16)
                            wait_at_least(a, summed, c + 1 - PSLOTS)
                            alone(a, m)
                            for h in range(ON_ACT):
                                last = a.activation(msg[:, s, h * C:(h + 1) * C], m.rows[:, g, h * C:(h + 1) * C], ACT.Copy,
                                                    scale=head_weight(c, h))
                            last.then_inc(weighed_a, 1)
                            if isinstance(i, int) and c + G - 1 >= n_chunks or isinstance(c, int) and c < 1:
                                continue
                            a.wait_ge(weighed, c)
                            a.wait_ge(weighed_a, c)
                            alone(a, m)
                            a.copy(m.ib[:, (g - 1) % G:(g - 1) % G + 1], index[:, bass.ds(c - 1 + G, 1)]).then_inc(indexed, 1)
                    peeled(a, rounds, body)
                else:
                    with a.Fori(0, rounds - 1) as i:
                        for g in range(G):
                            a.wait_ge(summed, i * G + g + 1)
                            alone(a, m)
                            a.copy(m.ib[:, g:g + 1], index[:, bass.ds((i + 1) * G + g, 1)]).then_inc(indexed, 1)

            @block.gpsimd
            def _(pool):
                with pool.Fori(0, rounds) as i:
                    for g in range(G):
                        pool.wait_ge(indexed, i * G + g + 1)
                        alone(pool, m)
                        pool.indirect_dma_start(
                            out=m.rows[:, g, :], out_offset=None, in_=table,
                            in_offset=bass.IndirectOffsetOnAxis(ap=m.ib[:, g:g + 1], axis=0))\
                            .then_inc(fetched[g], 16)

            @block.vector
            def _(v):
                def heat(i, g):
                    c, s = i * G + g, g % PSLOTS
                    if weight is None:
                        v.tensor_scalar(onehot[:, s, :], m.lanes[:, :], lane(c), None, ALU.is_equal).then_inc(hot, 1)
                    else:
                        v.tensor_scalar(onehot[:, s, :], m.lanes[:, :], lane(c), weight(c), ALU.is_equal, ALU.mult)\
                         .then_inc(hot, 1)
                    if per_head:
                        v.wait_ge(fetched[g], i * 16 + 16)
                        on_dve = lambda rows: rows[:, ON_ACT * C:D].rearrange("p (h c) -> p h c", c=C)
                        v.tensor_tensor(on_dve(msg[:, s, :]), on_dve(m.rows[:, g, :]),
                                        head_weight(c, ON_ACT, H - ON_ACT).unsqueeze(2).broadcast_to([P, H - ON_ACT, C]),
                                        op=ALU.mult)\
                         .then_inc(weighed, 1)

                for s in range(PSLOTS):
                    heat(0, s)

                def body(i):
                    for g in range(G):
                        c, s = i * G + g, g % PSLOTS
                        if g % F == 0:
                            at = offsets(nc, mybir.EngineType.DVE, places, c, F, (buckets - 1) * AW)
                        v.wait_ge(summed, c + 1)
                        wait_at_least(v, added, c)
                        acc = m.region[:, bass.ds(at[g % F], width)]
                        sums_of = m.ps[:, 2 * s:2 * s + 2, :].rearrange("p a b -> p (a b)")[:, 0:width]
                        v.tensor_tensor(acc, acc, sums_of, op=ALU.add).then_inc(added, 1)
                        if not (isinstance(c, int) and c + PSLOTS >= n_chunks):
                            ahead = g + PSLOTS
                            heat(i + ahead // G, ahead % G)
                peeled(v, rounds, body)

            @block.tensor
            def _(pe):
                def body(i):
                    for g in range(G):
                        c, s = i * G + g, g % PSLOTS
                        pe.wait_ge(hot, c + 1)
                        if per_head:
                            pe.wait_ge(weighed, c + 1)
                            pe.wait_ge(weighed_a, c + 1)
                        else:
                            pe.wait_ge(fetched[g], i * 16 + 16)
                        wait_at_least(pe, added, c + 1 - PSLOTS)
                        rows = msg[:, s, :] if per_head else m.rows[:, g, :]
                        if sums:
                            pe.matmul(m.ps[:, 2 * s + 1, 0:H], onehot[:, s, :], sums(c), start=True, stop=True)
                        pe.matmul(m.ps[:, 2 * s, :], onehot[:, s, :], rows, start=True, stop=True).then_inc(summed, 1)
                peeled(pe, rounds, body)


def fold_attention(m, nc, name, loads, folds):
    ks = ExitStack()
    with ks:
        sem = lambda n: semaphore(m, nc, f"{name}_{n}")
        loaded, dve = sem("loaded"), sem("dve")
        with nc.Block() as block:

            @block.sync
            def _(sp):
                for dst, src in loads:
                    sp.dma_start(dst, src).then_inc(loaded, 16)

            @block.vector
            def _(v):
                ch = Chain(v, dve)
                if loads:
                    v.wait_ge(loaded, 16 * len(loads))
                for w, row, groups, out in folds:
                    prod = m.scratch.rearrange("p (k d) -> p k d", k=KC)
                    ch.link(v.tensor_tensor(prod, w, row.unsqueeze(1).broadcast_to([P, KC, D]), op=ALU.mult))
                    for k in range(KC):
                        ch.link(v.tensor_reduce(out[:, k, :], prod[:, k, :].rearrange("p (g c) -> p g c", g=groups),
                                                AX.X, ALU.add))


def attention_table(m, nc, name, buckets, target, best, out_sb, own=None):
    ks = ExitStack()
    with ks:
        sem = lambda n: semaphore(m, nc, f"{name}_{n}")
        dve, set_ = sem("dve"), sem("set")
        asked, done = sem("asked"), sem("done")
        logit, top = out_sb[:, :, 0:H], out_sb[:, :, H:2 * H]
        with nc.Block() as block:

            @block.vector
            def _(v):
                ch = Chain(v, dve)
                link = ch.link
                link(v.tensor_copy(logit, target))
                link(v.tensor_tensor(top, best, logit, op=ALU.add))
                link(v.tensor_scalar(m.scratch[:, 0:buckets * H].rearrange("p (b h) -> p b h", h=H), top, 0.2, None, ALU.mult))
                v.tensor_tensor(top, top, m.scratch[:, 0:buckets * H].rearrange("p (b h) -> p b h", h=H),
                                op=ALU.max).then_inc(set_, 1)
                v.wait_ge(set_, 1)
                if own:
                    src, w = own
                    link(v.tensor_tensor(w, src, logit, op=ALU.add))
                    s3 = m.scratch[:, 0:buckets * H].rearrange("p (b h) -> p b h", h=H)
                    link(v.tensor_scalar(s3, w, 0.2, None, ALU.mult))
                    link(v.tensor_tensor(w, w, s3, op=ALU.max))
                    v.tensor_tensor(w, w, top, op=ALU.subtract).then_inc(asked, 1)

            @block.scalar
            def _(a):
                if own:
                    a.wait_ge(asked, 1)
                    a.activation(own[1], own[1], ACT.Exp).then_inc(done, 1)


def edge_weights(m, nc, name, n_chunks, logits, targets, out):
    ks = ExitStack()
    with ks:
        sem = lambda n: semaphore(m, nc, f"{name}_{n}")
        dve, asked, done = sem("dve"), sem("asked"), sem("done")
        w = n_chunks * H
        cube = lambda a: a.rearrange("p (c h) -> p c h", h=H)
        tg = targets[:, 0:n_chunks * 2 * H].rearrange("p (c f) -> p c f", f=2 * H)
        scr = m.scratch[:, 0:w]
        with nc.Block() as block:

            @block.vector
            def _(v):
                ch = Chain(v, dve)
                link = ch.link
                link(v.tensor_tensor(cube(out[:, 0:w]), cube(logits[:, 0:w]), tg[:, :, 0:H], op=ALU.add))
                link(v.tensor_scalar(scr, out[:, 0:w], 0.2, None, ALU.mult))
                link(v.tensor_tensor(out[:, 0:w], out[:, 0:w], scr, op=ALU.max))
                link(v.tensor_tensor(cube(out[:, 0:w]), cube(out[:, 0:w]), tg[:, :, H:2 * H], op=ALU.subtract))
                v.tensor_scalar(out[:, 0:w], out[:, 0:w], 0.0, None, ALU.min).then_inc(asked, 1)

            @block.scalar
            def _(a):
                a.wait_ge(asked, 1)
                a.activation(out[:, 0:w], out[:, 0:w], ACT.Exp).then_inc(done, 1)


def fill(m, nc, name, jobs):
    ks = ExitStack()
    with ks:
        sem = lambda n: semaphore(m, nc, f"{name}_{n}")
        dve, stored, set_ = sem("dve"), sem("stored"), sem("set")
        with nc.Block() as block:

            @block.vector
            def _(v):
                ch = Chain(v, dve)
                for kind, dst, what in jobs:
                    if kind == "set":
                        ch.link(v.memset(dst, what))
                    elif kind == "copy":
                        ch.link(v.tensor_copy(dst, what))
                    elif kind == "add":
                        ch.link(v.tensor_tensor(dst, dst, what, op=ALU.add))
                v.sem_inc(set_, 1)

            @block.sync
            def _(sp):
                stores = [(d, w) for k, d, w in jobs if k == "store"]
                if stores:
                    sp.wait_ge(set_, 1)
                    for d, w in stores:
                        sp.dma_start(d, w).then_inc(stored, 16)
                    sp.wait_ge(stored, 16 * len(stores))


def acc_rows(m, n=T):
    return m.region[:, 0:n * AW].rearrange("p (b w) -> p b w", w=AW)


def spline_network(m, nc):
    CA, CB = (1 / 6) ** (1 / 3), (4 / 6) ** (1 / 3)
    ks = ExitStack()
    with ks:
        sb = lambda n, s, d=F32: ks.enter_context(nc.sbuf_tensor(f"kan_{n}", s, d))
        sem = lambda n: semaphore(m, nc, f"kan_{n}")
        weights = m.region[:, T * AW:T * AW + (R8 + 1) * KC * D].rearrange("p (j k d) -> p j k d", k=KC, d=D)
        dist, wide, near, wide2, near2 = (
            m.own[:, 2 * n * D:2 * (n + 1) * D].rearrange("p (b d) -> p b d", b=2) for n in range(5))
        basis = m.rows[:, 0:4, :]
        aT, silu = m.rows[:, 4:6, :], m.rows[:, 6:8, :]
        grown = m.stage[:, 0, :]
        rden = sb("rden", [P, T])
        den_set, agg_ready, turned = (sem(n) for n in ("den_set", "agg_ready", "turned"))
        aT_set, grown_set, silu_set, powers = (sem(n) for n in ("aT_set", "grown_set", "silu_set", "powers"))
        basis_set, eaten, added = (sem(n) for n in ("basis_set", "eaten", "added"))
        dve, act = sem("dve"), sem("act")
        acc = acc_rows(m)
        scatter = Scatter(m, nc, "scatterC", m.recC)

        with nc.Block() as block:

            @block.sync
            def _(sp):
                scatter.load(sp, m.rc)

            @block.gpsimd
            def _(pool):
                scatter.run(pool, m.posC, m.rec_inA)

            @block.scalar
            def _(a):
                ch = Chain(a, act)
                a.wait_ge(den_set, 1)

                def agg(t, b):
                    wait_at_least(a, turned, t - 1)
                    if not isinstance(t, int):
                        alone(a, m)
                    a.activation(m.h[:, b, :], m.region[:, bass.ds(t * AW, D)], ACT.Copy,
                                 scale=rden[:, bass.ds(t, 1)]).then_inc(agg_ready, 1)

                def pair(i):
                    for b in range(2):
                        t = 2 * i + b
                        if not (isinstance(t, int) and t == T - 1):
                            agg(t + 1, 1 - b)
                        a.wait_ge(aT_set, t + 1)
                        wait_at_least(a, silu_set, t)
                        a.activation(grown, aT[:, b, :], ACT.Exp, scale=-1.0).then_inc(grown_set, 1)
                        for q in range(R8):
                            z = q % 2
                            wait_at_least(a, basis_set, t * R8 + q - 1)
                            ch.link(a.activation(dist[:, z, :], aT[:, b, :], ACT.Abs, scale=2.5,
                                                 bias=m.consts[:, q:q + 1]))
                            a.activation(wide[:, z, :], dist[:, z, :], ACT.Relu, scale=-CA, bias=m.consts[:, R8:R8 + 1])
                            ch.link(a.activation(near[:, z, :], dist[:, z, :], ACT.Relu, scale=-CB,
                                                 bias=m.consts[:, R8 + 1:R8 + 2]))
                            a.activation(wide2[:, z, :], wide[:, z, :], ACT.Square)
                            a.activation(near2[:, z, :], near[:, z, :], ACT.Square).then_inc(powers, 1)
                agg(0, 0)
                ch.rounds(T // 2, 4 * R8, pair)

            @block.vector
            def _(v):
                ch = Chain(v, dve)
                link = ch.link
                link(v.tensor_scalar(rden[:, :], acc[:, :, D], 1e-30, None, ALU.max))
                v.reciprocal(rden[:, :], rden[:, :]).then_inc(den_set, 1)

                def copy_aT(t, b):
                    v.wait_ge(turned, t + 1)
                    wait_at_least(v, powers, (t - 1) * R8)
                    v.tensor_copy(aT[:, b, :], m.ps[:, b, :]).then_inc(aT_set, 1)

                def one_basis(t, q):
                    z = q % 2
                    v.wait_ge(powers, t * R8 + q + 1)
                    v.tensor_tensor(wide2[:, z, :], wide2[:, z, :], wide[:, z, :], op=ALU.mult)
                    link(v.tensor_tensor(near2[:, z, :], near2[:, z, :], near[:, z, :], op=ALU.mult))
                    wait_at_least(v, eaten, t * R8 + q - 3)
                    v.tensor_tensor(basis[:, q % 4, :], wide2[:, z, :], near2[:, z, :], op=ALU.subtract)\
                     .then_inc(basis_set, 1)

                def add_x(t, b):
                    v.wait_ge(eaten, (t + 1) * R8)
                    xt = m.x[:, bass.ds(t * D, D)]
                    v.tensor_tensor(xt, xt, m.ps[:, 2 + b, :], op=ALU.add).then_inc(added, 1)

                def pair(i):
                    for b in range(2):
                        t = 2 * i + b
                        v.wait_ge(grown_set, t + 1)
                        v.wait_ge(aT_set, t + 1)
                        link(v.tensor_scalar(grown, grown, 1.0, None, ALU.add))
                        link(v.reciprocal(grown, grown))
                        wait_at_least(v, eaten, (t - 1) * R8)
                        v.tensor_tensor(silu[:, b, :], aT[:, b, :], grown, op=ALU.mult).then_inc(silu_set, 1)
                        for q in range(R8):
                            if q == 2 and not (isinstance(t, int) and t == 0):
                                add_x(t - 1, 1 - b)
                            if q == 4 and not (isinstance(t, int) and t == T - 1):
                                copy_aT(t + 1, 1 - b)
                            one_basis(t, q)
                copy_aT(0, 0)
                ch.rounds(T // 2, 2 * (2 + R8), pair)
                add_x(T - 1, 1)

            @block.tensor
            def _(pe):
                def turn(t, b):
                    pe.wait_ge(agg_ready, t + 1)
                    wait_at_least(pe, aT_set, t - 1)
                    for k in range(KC):
                        last = pe.transpose(m.ps[:, b, k * P:(k + 1) * P], m.h[:, b, k * P:(k + 1) * P], m.ident[:, :])
                    last.then_inc(turned, 1)

                def pair(i):
                    for b in range(2):
                        t = 2 * i + b
                        if not (isinstance(t, int) and t == T - 1):
                            turn(t + 1, 1 - b)
                        pe.wait_ge(silu_set, t + 1)
                        wait_at_least(pe, added, t - 1)
                        for k in range(KC):
                            pe.matmul(m.ps[:, 2 + b, :], silu[:, b, k * P:(k + 1) * P], weights[:, 0, k, :],
                                      start=k == 0, stop=False)
                        for q in range(R8):
                            pe.wait_ge(basis_set, t * R8 + q + 1)
                            for k in range(KC):
                                last = pe.matmul(m.ps[:, 2 + b, :], basis[:, q % 4, k * P:(k + 1) * P],
                                                 weights[:, 1 + q, k, :], start=False, stop=q == R8 - 1 and k == KC - 1)
                            last.then_inc(eaten, 1)
                turn(0, 0)
                peeled(pe, T // 2, pair)


def mean_layer(m, nc, weights):
    ks = ExitStack()
    with ks:
        sb = lambda n, s, d=F32: ks.enter_context(nc.sbuf_tensor(f"mean_{n}", s, d))
        sem = lambda n: semaphore(m, nc, f"mean_{n}")
        bias = sb("bias", [P, D])
        rdeg = sb("rdeg", [P, T])
        loaded, deg_set, neigh_ready, turned, copied, whole, added = (
            sem(n) for n in ("loaded", "deg_set", "neigh_ready", "turned", "copied", "whole", "added"))
        h_in = [sem(f"h_in{b}") for b in range(2)]
        dve = sem("dve")
        acc = acc_rows(m)

        with nc.Block() as block:

            @block.sync
            def _(sp):
                sp.dma_start(bias[:, :], m.b1.rearrange("(a d) -> a d", a=1).broadcast_to([P, D])).then_inc(loaded, 16)

                def pair(i):
                    for b in range(2):
                        t = 2 * i + b
                        wait_at_least(sp, turned, t - 1)
                        sp.dma_start(m.rows[:, b, :], m.h_table[bass.ds(t * P, P), :]).then_inc(h_in[b], 16)
                peeled(sp, T // 2, pair)

            @block.scalar
            def _(a):
                a.wait_ge(deg_set, 1)

                def pair(i):
                    for b in range(2):
                        t = 2 * i + b
                        wait_at_least(a, turned, t - 1)
                        if not isinstance(i, int):
                            alone(a, m)
                        a.activation(m.h[:, b, :], m.region[:, bass.ds(t * AW, D)], ACT.Copy,
                                     scale=rdeg[:, bass.ds(t, 1)]).then_inc(neigh_ready, 1)
                peeled(a, T // 2, pair)

            @block.tensor
            def _(pe):
                def turn(t, i, b):
                    pe.wait_ge(h_in[b], i * 16 + 16)
                    pe.wait_ge(neigh_ready, t + 1)
                    wait_at_least(pe, copied, t - 1)
                    for o, rows in enumerate((m.rows[:, b, :], m.h[:, b, :])):
                        for k in range(KC):
                            last = pe.transpose(m.ps[:, 2 * b + o, k * P:(k + 1) * P], rows[:, k * P:(k + 1) * P],
                                                m.ident[:, :])
                    last.then_inc(turned, 1)

                turn(0, 0, 0)

                def pair(i):
                    for b in range(2):
                        t = 2 * i + b
                        if not (isinstance(t, int) and t == T - 1):
                            turn(t + 1, i + b, 1 - b)
                        pe.wait_ge(copied, t + 1)
                        wait_at_least(pe, added, t - 1)
                        for k in range(2 * KC):
                            last = pe.matmul(m.ps[:, 4 + b, :], m.hT[:, b, k, :], weights[:, k, :],
                                             start=k == 0, stop=k == 2 * KC - 1)
                        last.then_inc(whole, 1)
                peeled(pe, T // 2, pair)

            @block.vector
            def _(v):
                ch = Chain(v, dve)
                ch.link(v.tensor_scalar(rdeg[:, :], acc[:, :, D], 1.0, None, ALU.max))
                v.reciprocal(rdeg[:, :], rdeg[:, :]).then_inc(deg_set, 1)
                v.wait_ge(loaded, 16)

                def copy_hT(t, b):
                    v.wait_ge(turned, t + 1)
                    wait_at_least(v, whole, t - 1)
                    v.tensor_copy(m.hT[:, b, :, :].rearrange("p k n -> p (k n)"),
                                  m.ps[:, 2 * b:2 * b + 2, :].rearrange("p a n -> p (a n)")).then_inc(copied, 1)

                copy_hT(0, 0)

                def pair(i):
                    for b in range(2):
                        t = 2 * i + b
                        if not (isinstance(t, int) and t == T - 1):
                            copy_hT(t + 1, 1 - b)
                        v.wait_ge(whole, t + 1)
                        ch.link(v.tensor_tensor(m.stage[:, b, :], m.ps[:, 4 + b, :], bias[:, :], op=ALU.add))
                        xt = m.x[:, bass.ds(t * D, D)]
                        v.scalar_tensor_tensor(out=xt, in0=m.stage[:, b, :], scalar=0.0, in1=xt,
                                               op0=ALU.max, op1=ALU.add).then_inc(added, 1)
                ch.rounds(T // 2, 2, pair)


def relational(m, nc, name, source, comp, bias, beside=None):
    ks = ExitStack()
    with ks:
        sb = lambda n, s, d=F32: ks.enter_context(nc.sbuf_tensor(f"{name}_{n}", s, d))
        sem = lambda n: semaphore(m, nc, f"{name}_{n}")
        stats = sb("stats", [P, T * 6])
        mv = sb("mv", [P, T * 2])
        rstd = sb("rstd", [P, T])
        nbias = sb("nbias", [P, T])
        slab = lambda o, n: m.region[:, T * AW + o * KC * D:T * AW + (o + n) * KC * D]
        weights = slab(0, BASES).rearrange("p (b k d) -> p b k d", b=BASES, k=KC)
        loop = slab(BASES, 1).rearrange("p (k d) -> p k d", k=KC)
        hb = slab(BASES + 1, 2).rearrange("p (s b d) -> p s b d", s=2, b=BASES)
        mix = (slab(BASES + 3, 2).rearrange("p (r d) -> p r d", r=R8), m.rows)
        root_asked, root_done, norm_set = sem("root_asked"), sem("root_done"), sem("norm_set")
        few_in, h_ready, turned, h_turned = sem("few_in"), sem("h_ready"), sem("turned"), sem("h_turned")
        multiplied, own_ready = sem("multiplied"), sem("own_ready")
        hb_set, own_set, begun, mixed = sem("hb_set"), sem("own_set"), sem("begun"), sem("mixed")
        HALF = R8 // 2
        stored = [[sem(f"stored{b}{o}") for o in range(2)] for b in range(2)]
        dve = sem("dve")
        MIX = (BASES - 1) * R8

        with nc.Block() as block:

            @block.sync
            def _(sp):
                sp.dma_start(m.comp[:, :], comp.rearrange("(a r) b -> a (r b)", a=1).broadcast_to([P, R8 * BASES]))\
                  .then_inc(few_in, 16)
                sp.dma_start(m.own_bias[:, :], bias.rearrange("(a d) -> a d", a=1).broadcast_to([P, D])).then_inc(few_in, 16)

                view = m.rel_table.rearrange("(r n) d -> n r d", r=R8)

                def pair(i):
                    for b in range(2):
                        t = 2 * i + b
                        for o in range(2):
                            sp.wait_ge(mixed, t * MIX + MIX - (1 - o) * HALF)
                            sp.dma_start(view[bass.ds(t * P, P), o * HALF:(o + 1) * HALF, :],
                                         mix[b][:, o * HALF:(o + 1) * HALF, :]).then_inc(stored[b][o], 16)
                peeled(sp, T // 2, pair)
                for s in stored[0] + stored[1]:
                    sp.wait_ge(s, 16 * (T // 2))

            @block.vector
            def _(v):
                ch = Chain(v, dve)
                if source == "norm":
                    normalise_setup(m, v, ch, stats, mv, rstd, nbias, root_asked, root_done)
                v.sem_inc(norm_set, 1)
                v.wait_ge(few_in, 32)

                def mid_rows(t, b):
                    wait_at_least(v, turned, t - 1)
                    if not isinstance(t, int):
                        alone(v, m)
                    v.tensor_scalar(m.h[:, b, :], m.region[:, bass.ds(t * AW, D)], 0.0, None, ALU.max).then_inc(h_ready, 1)

                def copy_hT(t, b):
                    v.wait_ge(turned, t + 1)
                    wait_at_least(v, own_ready, t - 1)
                    v.tensor_copy(m.hT[:, b, 0:KC, :].rearrange("p k n -> p (k n)"), m.ps[:, b, :])\
                     .then_inc(h_turned, 1)

                def pair(i):
                    for b in range(2):
                        t = 2 * i + b
                        more = not (isinstance(t, int) and t == T - 1)
                        for j in range(1, BASES):
                            if j == 2 and more:
                                copy_hT(t + 1, 1 - b)
                                if source == "mid" and not (isinstance(t, int) and t + 2 >= T):
                                    mid_rows(t + 2, b)
                            for r in range(R8):
                                if j == 1:
                                    v.wait_ge(begun, t * R8 + r + 1)
                                else:
                                    v.wait_ge(mixed, t * MIX + (j - 2) * R8 + r + 1)
                                if r == 0:
                                    v.wait_ge(hb_set, t * BASES + j + 1)
                                v.scalar_tensor_tensor(
                                    out=mix[b][:, r, :], in0=hb[:, b, j, :],
                                    scalar=m.comp[:, r * BASES + j:r * BASES + j + 1], in1=mix[b][:, r, :], op0=ALU.mult, op1=ALU.add).then_inc(mixed, 1)
                            if j == BASES - 1:
                                v.wait_ge(own_ready, t + 1)
                                v.tensor_tensor(m.region[:, bass.ds(t * AW, D)], m.ps[:, 6 + b, :], m.own_bias[:, :],
                                                op=ALU.add).then_inc(own_set, 1)
                if source == "mid":
                    mid_rows(0, 0)
                    mid_rows(1, 1)
                copy_hT(0, 0)
                peeled(v, T // 2, pair)

            @block.scalar
            def _(a):
                if source == "norm":
                    a.wait_ge(root_asked, 1)
                    a.activation(rstd[:, :], rstd[:, :], ACT.Sqrt).then_inc(root_done, 1)
                a.wait_ge(norm_set, 1)
                a.wait_ge(few_in, 32)

                def rows(t, b):
                    wait_at_least(a, turned, t - 1)
                    if not isinstance(t, int):
                        alone(a, m)
                    a.activation(m.h[:, b, :], m.x[:, bass.ds(t * D, D)], ACT.Relu,
                                 bias=nbias[:, bass.ds(t, 1)], scale=rstd[:, bass.ds(t, 1)]).then_inc(h_ready, 1)

                def pair(i):
                    for b in range(2):
                        t = 2 * i + b
                        if source == "norm" and not (isinstance(t, int) and t == T - 1):
                            rows(t + 1, 1 - b)
                        wait_at_least(a, mixed, (t - 1) * MIX)
                        for j in range(BASES):
                            a.wait_ge(multiplied, t * BASES + j + 1)
                            a.activation(hb[:, b, j, :], m.ps[:, 2 + j, :], ACT.Copy).then_inc(hb_set, 1)
                            if j == 0:
                                a.wait_ge(hb_set, t * BASES + 1)
                                for r in range(R8):
                                    if r % HALF == 0:
                                        wait_at_least(a, stored[b][r // HALF], i * 16)
                                    a.activation(mix[b][:, r, :], hb[:, b, 0, :], ACT.Copy,
                                                 scale=m.comp[:, r * BASES:r * BASES + 1]).then_inc(begun, 1)
                if source == "norm":
                    rows(0, 0)
                peeled(a, T // 2, pair)

            @block.tensor
            def _(pe):
                def turn(t, b):
                    pe.wait_ge(h_ready, t + 1)
                    wait_at_least(pe, h_turned, t - 1)
                    for k in range(KC):
                        last = pe.transpose(m.ps[:, b, k * P:(k + 1) * P], m.h[:, b, k * P:(k + 1) * P], m.ident[:, :])
                    last.then_inc(turned, 1)

                def pair(i):
                    for b in range(2):
                        t = 2 * i + b
                        if not (isinstance(t, int) and t == T - 1):
                            turn(t + 1, 1 - b)
                        pe.wait_ge(h_turned, t + 1)
                        for j in range(BASES):
                            wait_at_least(pe, hb_set, (t - 1) * BASES + j + 1)
                            for k in range(KC):
                                last = pe.matmul(m.ps[:, 2 + j, :], m.hT[:, b, k, :], weights[:, j, k, :],
                                                 start=k == 0, stop=k == KC - 1)
                            last.then_inc(multiplied, 1)
                        wait_at_least(pe, own_set, t - 1)
                        for k in range(KC):
                            last = pe.matmul(m.ps[:, 6 + b, :], m.hT[:, b, k, :], loop[:, k, :],
                                             start=k == 0, stop=k == KC - 1)
                        last.then_inc(own_ready, 1)
                turn(0, 0)
                peeled(pe, T // 2, pair)

            if beside:
                @block.gpsimd
                def _(pool):
                    beside(pool)


class Fold:

    def __init__(self, m, nc, name, weights, vectors, out):
        sem = lambda n: semaphore(m, nc, f"{name}_{n}")
        self.m, self.weights, self.vectors, self.out = m, weights, vectors, out
        self.w_in = [sem(f"w_in{u}") for u in range(2)]
        self.vectors_in, self.step = sem("vectors_in"), sem("step")

    def run(self, pool):
        m = self.m
        ch = Chain(pool, self.step)
        link = ch.link
        quarter = self.weights.rearrange("r (k p) d -> p r k d", p=P)
        rows = [m.hT[:, o, KC:2 * KC, :].rearrange("p k n -> p (k n)") for o in range(2)]
        prod = m.stage[:, 2, :].rearrange("p (h c) -> p h c", h=H)

        def relation(r):
            def load(k):
                pool.dma_start(m.stage[:, k % 2, :], quarter[:, bass.ds(r, 1), k, :].rearrange("p r d -> p (r d)"))\
                    .then_inc(self.w_in[k % 2], 16)

            for o in range(2):
                pool.dma_start(rows[o], self.vectors[o].rearrange("r h c -> r (h c)")[bass.ds(r, 1), :].broadcast_to([P, D]))\
                    .then_inc(self.vectors_in, 16)
            load(0)
            pool.wait_ge(self.vectors_in, r * 32 + 32)
            for k in range(KC):
                if k + 1 < KC:
                    load(k + 1)
                pool.wait_ge(self.w_in[k % 2], r * 32 + (k // 2) * 16 + 16)
                for o in range(2):
                    link(pool.tensor_tensor(m.stage[:, 2, :], m.stage[:, k % 2, :], rows[o], op=ALU.mult))
                    n = C // 2
                    while n > 1:
                        link(pool.tensor_tensor(prod[:, :, 0:n], prod[:, :, 0:n], prod[:, :, n:2 * n], op=ALU.add))
                        n //= 2
                    alone(pool, m)
                    link(pool.tensor_tensor(self.out[:, k, bass.ds((r * 2 + o) * H, H)], prod[:, :, 0], prod[:, :, 1],
                                            op=ALU.add))

        def rounds(eng, n, body):
            with eng.Fori(0, n) as i:
                body(i)
        ch.rounds(R4, KC * 2 * 7, relation, loop=rounds)


def fuse_relations(m, nc):
    ks = ExitStack()
    with ks:
        sb = lambda n, s, d=F32: ks.enter_context(nc.sbuf_tensor(f"fuse_{n}", s, d))
        sem = lambda n: semaphore(m, nc, f"fuse_{n}")
        behind = m.region[:, NBA * AW:]
        w1 = behind[:, 0:KC * SEM_D].rearrange("p (k d) -> p k d", k=KC)
        b1, w2, junk = (behind[:, (KC + n) * SEM_D:(KC + n + 1) * SEM_D] for n in range(3))
        bias = m.stage
        xt = m.rows[:, :, :].rearrange("p (b r) d -> p b r d", b=2)
        z = m.own[:, 0:2 * R4 * D].rearrange("p (b r d) -> p b r d", b=2, r=R4)
        zT = m.own[:, 2 * R4 * D:2 * R4 * D + 2 * D].rearrange("p (b d) -> p b d", b=2)
        th = m.hT[:, :, :, :].rearrange("p b k n -> p (b k n)").rearrange("p (b r d) -> p b r d", b=2, r=R4)
        den = sb("den", [P, 2, R4, H])
        own = sb("own", [P, 2, R4, H])
        w = sb("w", [P, R4])
        top = sb("top", [P, 4])
        beta = sb("beta", [P, R4])
        loaded, z_ready, turned, zT_set, pre_ready = (
            sem(n) for n in ("loaded", "z_ready", "turned", "zT_set", "pre_ready"))
        th_set, asked, answered, out_set, stored = (sem(n) for n in ("th_set", "asked", "answered", "out_set", "stored"))
        xt_in = [sem(f"xt_in{b}") for b in range(2)]
        dve, dve_w, own_set = sem("dve"), sem("dve_w"), sem("own_set")
        divided, scaled, biased = sem("divided"), sem("scaled"), sem("biased")

        with nc.Block() as block:

            @block.sync
            def _(sp):
                sp.dma_start(w1, m.sem_w1.rearrange("(k p) d -> p k d", p=P)).then_inc(loaded, 16)
                sp.dma_start(b1, m.sem_b1.rearrange("(a d) -> a d", a=1).broadcast_to([P, SEM_D])).then_inc(loaded, 16)
                sp.dma_start(w2, m.sem_w2.rearrange("d a -> a d").broadcast_to([P, SEM_D])).then_inc(loaded, 16)
                sp.dma_start(bias[:, :, :].rearrange("p r d -> p (r d)"),
                             m.bias3.rearrange("(a r) d -> a (r d)", a=1).broadcast_to([P, R4 * D])).then_inc(loaded, 16)
                view = m.xt_table.rearrange("(r n) d -> n r d", r=R4)

                def pair(i):
                    for b in range(2):
                        t = 2 * i + b
                        wait_at_least(sp, z_ready, R4 * (t - 1))
                        sp.dma_start(xt[:, b, :, :], view[bass.ds(t * P, P), :, :]).then_inc(xt_in[b], 16)
                        if not (isinstance(t, int) and t < 3):
                            store(t - 3)

                def store(t, rows=P):
                    sp.wait_ge(out_set, t + 1)
                    sp.dma_start(m.out[bass.ds(t * P, rows), :], m.x[0:rows, bass.ds(t * D, D)]).then_inc(stored, 16)
                pair(0)
                pair(1)
                with sp.Fori(2, T // 2) as i:
                    pair(i)
                store(T - 3)
                store(T - 2)
                store(T - 1, LAST)
                sp.wait_ge(stored, 16 * T)

            @block.vector
            def _(v):
                cw, cs = Chain(v, dve_w), Chain(v, dve)
                by_head = lambda a: a.rearrange("p (h c) -> p h c", h=H)
                wide = lambda a: a.unsqueeze(2).broadcast_to([P, H, C])
                LS = R4 + 1 + 3 + R4

                def denominators(t, b):
                    cw.base, cw.k = t * 2, 0
                    sums = m.region[:, bass.ds(t * R4 * AW, R4 * AW)].rearrange("p (r w) -> p r w", w=AW)[:, :, D:AW]
                    selfs = m.self_w[:, bass.ds(t * R4 * H, R4 * H)].rearrange("p (r h) -> p r h", h=H)
                    cw.link(v.tensor_tensor(den[:, b, :, :], sums, selfs, op=ALU.add))
                    cw.link(v.reciprocal(den[:, b, :, :], den[:, b, :, :]))
                    v.tensor_tensor(own[:, b, :, :], selfs, den[:, b, :, :], op=ALU.mult).then_inc(own_set, 1)

                def outputs(t, b):
                    mine = m.region[:, bass.ds(t * R4 * AW, R4 * AW)].rearrange("p (r w) -> p r w", w=AW)
                    for r in range(R4):
                        v.tensor_tensor(by_head(z[:, b, r, :]), by_head(mine[:, r, 0:D]), wide(den[:, b, r, :]),
                                        op=ALU.mult).then_inc(divided, 1)
                    for r in range(R4):
                        v.wait_ge(divided, t * R4 + r + 1)
                        v.wait_ge(biased, t * R4 + r + 1)
                        v.tensor_tensor(z[:, b, r, :], z[:, b, r, :], xt[:, b, r, :], op=ALU.add).then_inc(z_ready, 1)

                def scores(t, b):
                    cs.base, cs.k = t * LS, 0
                    link = cs.link
                    for r in range(R4):
                        v.wait_ge(th_set, t * R4 + r + 1)
                        link(v.tensor_tensor_reduce(out=junk, in0=th[:, b, r, :], in1=w2, scale=1.0, scalar=0.0,
                                                    op0=ALU.mult, op1=ALU.add, accum_out=w[:, r:r + 1]))
                    link(v.tensor_reduce(top[:, 0:1], w[:, :], AX.X, ALU.max))
                    v.tensor_scalar(beta[:, :], w[:, :], top[:, 0:1], None, ALU.subtract).then_inc(asked, 1)
                    v.wait_ge(answered, t + 1)
                    link(v.tensor_reduce(top[:, 1:2], beta[:, :], AX.X, ALU.add))
                    link(v.reciprocal(top[:, 2:3], top[:, 1:2]))
                    link(v.tensor_scalar(beta[:, :], beta[:, :], top[:, 2:3], None, ALU.mult))
                    xs = m.x[:, bass.ds(t * D, D)]
                    for r in range(R4):
                        link(v.scalar_tensor_tensor(out=xs, in0=z[:, b, r, :], scalar=beta[:, r:r + 1], in1=xs,
                                                    op0=ALU.mult, op1=ALU.add))
                    v.sem_inc(out_set, 1)
                    assert cs.k == LS

                v.wait_ge(loaded, 64)
                denominators(0, 0)
                denominators(1, 1)
                outputs(0, 0)

                def pair(i):
                    for b in range(2):
                        t = 2 * i + b
                        if not (isinstance(t, int) and t + 2 >= T):
                            denominators(t + 2, b)
                        if not (isinstance(t, int) and t == T - 1):
                            wait_at_least(v, turned, R4 * t)
                            outputs(t + 1, 1 - b)
                        scores(t, b)
                peeled(v, T // 2, pair)

            @block.scalar
            def _(a):
                def pair(i):
                    for b in range(2):
                        t = 2 * i + b
                        for r in range(R4):
                            a.wait_ge(turned, t * R4 + r + 1)
                            wait_at_least(a, pre_ready, t * R4 + r - 1)
                            a.activation(zT[:, r % 2, :], m.ps[:, r % 2, :], ACT.Copy).then_inc(zT_set, 1)
                            if r:
                                squash(t, r - 1, b)
                            elif not (isinstance(t, int) and t == 0):
                                answer(t - 1)
                        squash(t, R4 - 1, b)

                def squash(t, r, b):
                    a.wait_ge(pre_ready, t * R4 + r + 1)
                    a.activation(th[:, b, r, :], m.ps[:, 2 + r % 2, 0:SEM_D], ACT.Tanh).then_inc(th_set, 1)

                def answer(t):
                    a.wait_ge(asked, t + 1)
                    a.activation(beta[:, :], beta[:, :], ACT.Exp).then_inc(answered, 1)
                peeled(a, T // 2, pair)
                answer(T - 1)

            @block.tensor
            def _(pe):
                pe.wait_ge(loaded, 64)

                def pair(i):
                    for b in range(2):
                        t = 2 * i + b
                        for r in range(R4):
                            pe.wait_ge(z_ready, t * R4 + r + 1)
                            wait_at_least(pe, zT_set, t * R4 + r - 1)
                            for k in range(KC):
                                last = pe.transpose(m.ps[:, r % 2, k * P:(k + 1) * P], z[:, b, r, k * P:(k + 1) * P],
                                                    m.ident[:, :])
                            last.then_inc(turned, 1)
                            wait_at_least(pe, th_set, t * R4 + r - 1)
                            pre = m.ps[:, 2 + r % 2, 0:SEM_D]
                            pe.matmul(pre, m.ones[0:1, :], b1[0:1, :], start=True, stop=False)
                            pe.wait_ge(zT_set, t * R4 + r + 1)
                            for k in range(KC):
                                last = pe.matmul(pre, zT[:, r % 2, k * P:(k + 1) * P], w1[:, k, :],
                                                 start=False, stop=k == KC - 1)
                            last.then_inc(pre_ready, 1)
                peeled(pe, T // 2, pair)

            @block.gpsimd
            def _(pool):
                def pair(i):
                    for b in range(2):
                        t = 2 * i + b
                        pool.wait_ge(xt_in[b], i * 16 + 16)
                        pool.wait_ge(own_set, t + 1)
                        for r in range(R4):
                            xr = xt[:, b, r, :].rearrange("p (h c) -> p h c", h=H)
                            pool.tensor_tensor(xr, xr, own[:, b, r, :].unsqueeze(2).broadcast_to([P, H, C]), op=ALU.mult)\
                                .then_inc(scaled, 1)
                        for r in range(R4):
                            pool.wait_ge(scaled, t * R4 + r + 1)
                            pool.tensor_tensor(xt[:, b, r, :], xt[:, b, r, :], bias[:, r, :], op=ALU.add)\
                                .then_inc(biased, 1)
                pool.wait_ge(loaded, 64)
                peeled(pool, T // 2, pair)


def gnn_kernel(nc, a):
    m = Core()
    m.x_in, m.src, m.dst, m.type4 = a["x_in"], a["src"], a["dst"], a["type4"]
    m.type8, m.weight, m.w0, m.a0 = a["type8"], a["weight"], a["w0"], a["a0"]
    m.w1, m.b1, m.w3, m.att_src = a["w1"], a["b1"], a["w3"], a["att_src"]
    m.att_dst, m.bias3, m.sem_w1, m.sem_b1 = a["att_dst"], a["bias3"], a["sem_w1"], a["sem_b1"]
    m.sem_w2, m.base_wT, m.spline_wT, m.basis = a["sem_w2"], a["base_wT"], a["spline_wT"], a["basis"]
    m.comps, m.biases, m.loops, m.out = a["comps"], a["biases"], a["loops"], a["out"]
    ks = ExitStack()
    with ks:
        sb = lambda n, s, d=F32: ks.enter_context(nc.sbuf_tensor(n, s, d))
        dram = lambda n, s: nc.dram_tensor(n, s, F32, kind="Internal").ap()
        m.gate = nc.alloc_semaphore("gate")
        m.sems = []
        m.recA, m.recB, m.recC = (dram(n, (P * c, REC)) for n, c in (("recA", NCA), ("recB", NCB), ("recC", NCB)))
        m.h_table = dram("h_table", (NP, D))
        m.rel_table = dram("rel_table", (R8 * NP, D))
        m.xt_table = dram("xt_table", (R4 * NP, D))
        m.source_table = dram("source_table", (R4 * NP, H))

        m.ps = ks.enter_context(nc.psum_tensor("ps", [P, 8, 512], F32))
        m.x = sb("x", [P, T * D])
        m.region = sb("region", [P, T * AW + (R8 + 1) * KC * D])
        m.own = sb("own", [P, T * D])
        m.rows = sb("rows", [P, G, D])
        m.ib = sb("ib", [P, G], U32)
        m.h = sb("h", [P, 2, D])
        m.stage = sb("stage", [P, 4, D])
        m.scratch = m.stage[:, :, :].rearrange("p s d -> p (s d)")
        m.hT = sb("hT", [P, 2, 2 * KC, P])
        m.ident = sb("ident", [P, P])
        m.ones = sb("ones", [P, P])
        m.lanes = sb("lanes", [P, P])
        m.zeros = sb("zeros", [P, 8])
        m.consts = sb("consts", [P, R8 + 3])
        m.const_values = [3.5 - j for j in range(R8)] + [2 * (1 / 6) ** (1 / 3), (4 / 6) ** (1 / 3), 0.0]
        m.ra = sb("ra", [P, NCA, REC])
        m.rb = sb("rb", [P, NCB, REC])
        m.ix_src, m.ix_src8, m.ix_src4 = (sb(f"ix_{n}", [P, c], U32) for n, c in (("src", NCB), ("src8", NCB), ("src4", NCA)))
        m.ix_bdst = sb("ix_bdst", [P, NCB], U32)
        m.accA, m.maxA = (sb(n, [1, NCA], I32) for n in ("accA", "maxA"))
        m.accB, m.maxB, m.accC = (sb(n, [1, NCB], I32) for n in ("accB", "maxB", "accC"))
        edge = m.own
        m.posA, m.rec_inA = sb("posA", [EP, EC], U32), sb("rec_inA", [EP, EC, REC])
        m.pos_blk, m.rec_blk = sb("pos_blk", [EP, 2, SC], U32), sb("rec_blk", [EP, 2, SC, REC])
        m.posB, m.posC = sb("posB", [EP, EC], U32), sb("posC", [EP, EC], U32)
        m.rec_inB = m.rows[0:EP, 0:3, :].rearrange("p g d -> p (g d)")[:, 0:EC * REC].rearrange("p (c f) -> p c f", f=REC)
        positions, bucket_ends = prepare(m, nc)

        laneA = lambda c: m.ra[:, bass.ds(c, 1), A_LANE]
        laneB = lambda c: m.rb[:, bass.ds(c, 1), B_LANE]
        m.rc = m.rb
        laneC = lambda c: m.rc[:, bass.ds(c, 1), A_LANE]
        sums_of_ones = lambda c: m.ones[:, 0:H]
        weights_at = lambda o, n=KC * D: m.region[:, T * AW + o * KC * D:T * AW + o * KC * D + n]
        cube = lambda ap: ap.rearrange("p (k d) -> p k d", d=D)
        by_k = lambda w: w.rearrange("(k p) d -> p k d", p=P)
        zero = ("set", m.region[:, 0:T * AW], 0.0)

        with ExitStack() as layer:
            sl = lambda n, s, d=F32: layer.enter_context(nc.sbuf_tensor(n, s, d))
            fold = sl("fold0", [P, KC, 2])
            st = sl("st", [P, T * 2])
            att = weights_at(1, 2 * D)
            fold_attention(m, nc, "fold0",
                           [(cube(weights_at(0)), m.w0.rearrange("(k p) d -> p k d", p=P)),
                            (att, m.a0.rearrange("d a -> a d").broadcast_to([P, 2 * D]))],
                           [(cube(weights_at(0)), att[:, j * D:(j + 1) * D], 1, fold[:, :, j:j + 1]) for j in range(2)])
            scatter = Scatter(m, nc, "scatterB", m.recB)

            def rest_of_positions(v):
                positions(v, 1, 2)
                positions(v, 2, 0)

            def rest_of_ends(pe):
                bucket_ends(pe, 1, 2)
                bucket_ends(pe, 2, 0)

            project(m, nc, "p0", h_table=m.h_table, small=(fold[:, :, :], st[:, :]),
                    beside=lambda pool: scatter.run(pool, m.posB, m.rec_inB),
                    then_vector=rest_of_positions, then_tensor=rest_of_ends,
                    then_sync=lambda sp: scatter.load(sp, m.rb))
            st3 = st[:, :].rearrange("p (t k) -> p t k", k=2)
            tgt = sl("tgt0", [P, T, H])
            best = sl("best0", [P, F, T * H])
            tt = sl("tt0", [P, T, 2 * H])
            logits, targets = edge[:, 0:NCB * H], edge[:, NCB * H:NCB * 3 * H]
            fill(m, nc, "f0", [("set", logits, 0.0), ("set", tgt[:, :, :], 0.0), ("copy", tgt[:, :, 0], st3[:, :, 0]),
                               ("set", best[:, :, :], -BIG), zero,
                               ("copy", m.ix_bdst[:, :], m.rb[:, :, B_DST])])
            weights = sl("ew0", [P, NCB * H])
            look_up(m, nc, "l0", NCB, m.rb, st3[:, :, 1], weights_at(0, NCB * 3 * T), weights_at(3, NCB * T),
                    logits.rearrange("p (c h) -> p c h", h=H)[:, :, 0])
            segment_max_one(m, nc, "m0", NCB, NBB, m.rb, logits, m.maxB, best)
            attention_table(m, nc, "t0", T, tgt[:, :, :], best[:, 0, :].rearrange("p (b h) -> p b h", h=H), tt)
            target_values(m, nc, "v0", NCB, NBB, m.rb, m.maxB, tt[:, :, :], targets)
            edge_weights(m, nc, "e0", NCB, logits, targets, weights)
            aggregate(m, nc, "a0", NCB, NBB, m.ix_bdst, laneB, m.h_table, m.accB,
                      weight=lambda c: weights[:, bass.ds(c * H, 1)], sums=sums_of_ones,
                      prefetch=[(cube(weights_at(0)), by_k(m.base_wT))] +
                      [(cube(weights_at(1 + j)), by_k(m.spline_wT[j])) for j in range(R8)])
        spline_network(m, nc)

        recycle_semaphores(m, nc)

        mean_w = m.region[:, T * AW + (R8 - 1) * KC * D:T * AW + (R8 + 1) * KC * D].rearrange("p (k d) -> p k d", d=D)

        def relation_weights(n):
            return [(cube(weights_at(b)), by_k(m.basis[n][b])) for b in range(BASES)] + \
                [(cube(weights_at(BASES)), by_k(m.loops[n]))]

        cleared = semaphore(m, nc, "cleared")

        def clear(pool):
            pool.memset(m.region[:, 0:T * AW], 0.0).then_inc(cleared, 1)

        project(m, nc, "p1", h_table=m.h_table, beside=clear)
        fill(m, nc, "f1", [("copy", m.ix_src[:, :], m.rc[:, :, A_SRC]), ("copy", m.ix_src8[:, :], m.rc[:, :, A_SRC8])])
        aggregate(m, nc, "a1", NCB, T, m.ix_src, laneC, m.h_table, m.accC, sums=sums_of_ones,
                  prefetch=[(mean_w, by_k(m.w1))] + relation_weights(0))
        mean_layer(m, nc, mean_w)

        recycle_semaphores(m, nc)
        fold = sb("fold3", [P, KC, R4 * 2 * H])
        with ExitStack() as layer:
            sl = lambda n, s, d=F32: layer.enter_context(nc.sbuf_tensor(n, s, d))
            m.comp = sl("comp", [P, R8 * BASES])
            m.own_bias = sl("own_bias", [P, D])
            folding = Fold(m, nc, "fold3", m.w3, (m.att_src, m.att_dst), fold)
            scatter_a = Scatter(m, nc, "scatterA", m.recA)

            def sort_a(pool):
                scatter_a.run(pool, m.posA, m.rec_inA)
                scatter_a.load(pool, m.ra)

            for n in range(2):
                relational(m, nc, f"r2{n}", ("norm", "mid")[n], m.comps[n], m.biases[n],
                           beside=folding.run if n else sort_a)
                aggregate(m, nc, f"a2{n}", NCB, T, m.ix_src8, laneC, m.rel_table, m.accC,
                          weight=lambda c: m.rc[:, bass.ds(c, 1), A_WEIGHT],
                          prefetch=relation_weights(1) if n == 0 else
                          [(cube(weights_at(r)), by_k(m.w3[r])) for r in range(R4)])
            fill(m, nc, "f22", [("add", m.x[:, :].rearrange("p (t d) -> p t d", d=D), acc_rows(m)[:, :, 0:D])])

        recycle_semaphores(m, nc)

        al = sb("al", [P, T * R4 * 2 * H])
        best = sb("best3", [P, NBA * H])
        m.self_w = sb("self_w", [P, NBA * H])
        tt = m.region[:, NBA * AW:NBA * (AW + 2 * H)].rearrange("p (b f) -> p b f", f=2 * H)
        al3 = al[:, :].rearrange("p (b f) -> p b f", f=2 * H)
        with ExitStack() as layer:
            sl = lambda n, s, d=F32: layer.enter_context(nc.sbuf_tensor(n, s, d))
            h_turned = weights_at(R4, T * D)
            project(m, nc, "p3", small=(fold[:, :, :], al[:, :]), keep=h_turned)
            al4 = al[:, :].rearrange("p (t r f) -> p t r f", r=R4, f=2 * H)
            fill(m, nc, "f3", [("copy", m.ix_src4[:, :], m.ra[:, :, A_SRC4]), ("copy", best[:, :].rearrange("p (b h) -> p b h", h=H), al3[:, :, 0:H])] +
                 [("store", m.source_table[r * NP:(r + 1) * NP, :].rearrange("(t p) h -> p t h", p=P), al4[:, :, r, 0:H])
                  for r in range(R4)])
            logits, targets = edge[:, 0:NCA * H], edge[:, NCA * H:NCA * 3 * H]
            segment_max(m, nc, "m3", NCA, NBA, laneA, m.ix_src4, m.source_table, logits, m.maxA, best,
                        h_turned, [cube(weights_at(r)) for r in range(R4)], m.xt_table)
            attention_table(m, nc, "t3", NBA, al3[:, :, H:2 * H], best[:, :].rearrange("p (b h) -> p b h", h=H), tt,
                            own=(al3[:, :, 0:H], m.self_w[:, :].rearrange("p (b h) -> p b h", h=H)))
            cleared = semaphore(m, nc, "cleared3")
            target_values(m, nc, "v3", NCA, NBA, m.ra, m.maxA, tt, targets,
                          beside=lambda pool: pool.memset(m.region[:, 0:NBA * AW], 0.0).then_inc(cleared, 1))
            weights = m.region[:, NBA * (AW + 2 * H):NBA * (AW + 2 * H) + NCA * H]
            edge_weights(m, nc, "e3", NCA, logits, targets, weights)
            col = lambda c, h=0, n=H: weights[:, bass.ds(c * H + h, n)]
            head = lambda c, h, n=1: col(c, h, n)
            aggregate(m, nc, "a3", NCA, NBA, m.ix_src4, laneA, m.xt_table, m.accA, head_weight=head, sums=col)
        fuse_relations(m, nc)
    return m


_NAMES = dict(x="x_in", src="src", dst="dst", edge_type_4="type4", edge_type_8="type8", edge_weight="weight",
              L0_gnn_W="w0", L0_gnn_a="a0", L1_gnn_W="w1", L1_gnn_b="b1", L3_gnn_W="w3",
              L3_gnn_att_src="att_src", L3_gnn_att_dst="att_dst", L3_gnn_bias="bias3", L3_gnn_sem_W1="sem_w1",
              L3_gnn_sem_b1="sem_b1", L3_gnn_sem_W2="sem_w2",
              L2_gnn_basis0="basis0", L2_gnn_comp0="comp0", L2_gnn_bias0="bias0", L2_gnn_loop0="loop0",
              L2_gnn_basis1="basis1", L2_gnn_comp1="comp1", L2_gnn_bias1="bias1", L2_gnn_loop1="loop1")


def lay_out(inputs):
    import numpy as np
    arrays = {mine: np.ascontiguousarray(inputs[name]) for name, mine in _NAMES.items()}
    arrays["base_wT"] = np.ascontiguousarray(np.transpose(np.asarray(inputs["L0_gnn_base_w"])))
    arrays["spline_wT"] = np.ascontiguousarray(np.transpose(np.asarray(inputs["L0_gnn_spline_w"]), (2, 1, 0)))
    return arrays


def program(nc, arrays):
    a = {n: nc.dram_tensor(f"in_{n}", v.shape, mybir.dt.from_np(v.dtype), kind="ExternalInput").ap()
         for n, v in arrays.items()}
    a["out"] = nc.dram_tensor("out_dram", (N, D), F32, kind="ExternalOutput").ap()
    for one, both in (("basis", "basis"), ("comp", "comps"), ("bias", "biases"), ("loop", "loops")):
        a[both] = (a[one + "0"], a[one + "1"])
    return gnn_kernel(nc, a)


def kernel(**inputs):
    import concourse.bacc as _bacc
    from concourse.bass_utils import run_bass_kernel_spmd as _run

    arrays = lay_out(inputs)
    nc = _bacc.Bacc("TRN2", target_bir_lowering=False, num_devices=1)
    program(nc, arrays)
    r = _run(nc, [{f"in_{n}": v for n, v in arrays.items()}], core_ids=[0])
    return r.results[0]["out_dram"]
```
